# Optimizing a Trainium2 kernel written in Bass

```python
import numpy as np
import jax
import jax.numpy as jnp

def _softmax(x, axis=-1):
    return jax.nn.softmax(x, axis=axis)

def _gelu(x):
    return jax.nn.gelu(x, approximate=True)

def _silu(x):
    return jax.nn.silu(x)

def _sigmoid(x):
    return jax.nn.sigmoid(x)

def _layernorm(x, axis=-1, eps=1e-05):
    m = jnp.mean(x, axis=axis, keepdims=True)
    v = jnp.var(x, axis=axis, keepdims=True)
    return (x - m) / jnp.sqrt(v + eps)

def _scatter_add(tgt, idx, src, axis=0):
    return tgt.at[idx].add(src)

def _segment_sum(src, seg, n):
    return jax.ops.segment_sum(src, seg, n)
kernel_name = 'mk_adaln_attn_ffn_d1_seqx_r4_091a1c'

def setup_inputs(seed: int=0):
    np.random.seed(seed)
    _w = jnp.asarray

    def _rec_inputs():
        import jax
        import jax.numpy as jnp
        _rk = jax.random.key(seed)
        x = -0.0003929 + 0.9999 * jax.random.normal(jax.random.fold_in(_rk, 1), (32, 64, 1024), jnp.float32)
        _lenS = 64 - jax.random.randint(jax.random.fold_in(_rk, 7), (32,), 0, max(1, 64 // 4) + 1, jnp.int32)
        _lenS2 = 64 - jax.random.randint(jax.random.fold_in(_rk, 8), (32,), 0, max(1, 64 // 4) + 1, jnp.int32)
        itok_B_8_3872 = jax.random.randint(jax.random.fold_in(_rk, 11), (32,), 8, 3873, jnp.int32)
        itok_B_0_15 = jax.random.randint(jax.random.fold_in(_rk, 12), (32,), 0, 16, jnp.int32)
        return (x, itok_B_8_3872, itok_B_0_15)
    x, itok_B_8_3872, itok_B_0_15 = _rec_inputs()

    def _L0_cond_setup():
        import math
        import jax, jax.numpy as jnp
        import numpy as np
        H, N, B, L = (64, 64, 16, 1024)
        DT_MIN, DT_MAX = (0.001, 0.1)

        def _get_kernel(log_dt, C, log_A_real, A_imag, length):
            Cc = C[..., 0] + 1j * C[..., 1]
            dt = jnp.exp(log_dt)
            A = -jnp.exp(log_A_real) + 1j * A_imag
            dtA = A * dt[:, None]
            P = dtA[:, :, None] * jnp.arange(length, dtype=jnp.float32)
            Cs = Cc * (jnp.exp(dtA) - 1.0) / A
            K = 2.0 * jnp.einsum('hn,hnl->hl', Cs, jnp.exp(P)).real
            return K
        key = jax.random.key(seed)
        ks = jax.random.split(key, 6)
        u = jax.random.normal(ks[0], (B, H, L), dtype=jnp.float32)
        length = jax.random.randint(ks[1], (B,), 0, L)
        log_dt = jax.random.uniform(ks[2], (H,), dtype=jnp.float32) * (math.log(DT_MAX) - math.log(DT_MIN)) + math.log(DT_MIN)
        C = jax.random.normal(ks[3], (H, N, 2), dtype=jnp.float32)
        log_A_real = jnp.log(0.5 * jnp.ones((H, N), dtype=jnp.float32))
        A_imag = math.pi * jnp.broadcast_to(jnp.arange(N, dtype=jnp.float32), (H, N))
        D = jax.random.normal(ks[4], (H,), dtype=jnp.float32)
        return {'u': u, 'length': length, 'log_dt': log_dt, 'C': C, 'log_A_real': log_A_real, 'A_imag': A_imag, 'D': D}
    _L0_cond_all = _L0_cond_setup()
    _L0_cond_in = {k: v for k, v in _L0_cond_all.items() if k in ('log_dt', 'C', 'log_A_real', 'A_imag', 'D')}
    del _L0_cond_all

    def _L0_attn_setup():
        import jax, jax.numpy as jnp
        import numpy as np
        H = 32
        HKV = 8
        D = 1024
        HD = D // H
        S = 256
        MASK_OUT = 0.9
        MIN_REMAIN = 128
        THETA = 10000.0

        def rope_tables(seq_len, hd):
            inv_freq = 1.0 / THETA ** (jnp.arange(0, hd, 2, dtype=jnp.float32) / hd)
            t = jnp.arange(seq_len, dtype=jnp.float32)
            freqs = jnp.outer(t, inv_freq)
            emb = jnp.concatenate([freqs, freqs], axis=-1)
            return (jnp.cos(emb), jnp.sin(emb))

        def rotate_half(x):
            x1, x2 = jnp.split(x, 2, axis=-1)
            return jnp.concatenate([-x2, x1], axis=-1)

        def apply_rope(x, cos, sin):
            return x * cos + rotate_half(x) * sin
        key = jax.random.key(seed)
        k0, k1, k2, k3, k4 = jax.random.split(key, 5)
        hidden_states = jax.random.normal(k0, (1, S, D), jnp.float32)
        Wq = jax.random.normal(k1, (D, D), jnp.float32) * 0.02
        Wk = jax.random.normal(k2, (HKV * HD, D), jnp.float32) * 0.02
        Wv = jax.random.normal(k3, (HKV * HD, D), jnp.float32) * 0.02
        Wo = jax.random.normal(k4, (D, D), jnp.float32) * 0.02
        return {'hidden_states': hidden_states, 'Wq': Wq, 'Wk': Wk, 'Wv': Wv, 'Wo': Wo}
    _L0_attn_all = _L0_attn_setup()
    _L0_attn_in = {k: v for k, v in _L0_attn_all.items() if k in ('Wq', 'Wk', 'Wv', 'Wo')}
    del _L0_attn_all

    def _L0_cond2_setup():
        import jax, jax.numpy as jnp
        import numpy as np
        NUM_CONDITIONS = 16
        IN_CH = 64
        OUT_CH = 64
        B = 64
        T = 1024
        key = jax.random.key(seed)
        k_x, k_w, k_c = jax.random.split(key, 3)
        x = jax.random.normal(k_x, (B, IN_CH, T), dtype=jnp.float32)
        bound = float(np.sqrt(6.0 / IN_CH))
        weights = jax.random.uniform(k_w, (NUM_CONDITIONS, IN_CH, OUT_CH), dtype=jnp.float32, minval=-bound, maxval=bound)
        condition = jax.random.randint(k_c, (B,), 0, NUM_CONDITIONS, dtype=jnp.int64)
        return {'x': x, 'weights': weights, 'condition': condition}
    _L0_cond2_all = _L0_cond2_setup()
    _L0_cond2_in = {k: v for k, v in _L0_cond2_all.items() if k in ('weights',)}
    del _L0_cond2_all

    def _L0_ffn_setup():
        import jax, jax.numpy as jnp
        import numpy as np
        E = 8
        R = 8
        DIN = 1024
        DOUT = 1024
        TOP_K = 2
        SCALING = 2.0

        def _moe_lora(xf, gate_W, A, B):
            gate_probs = jax.nn.softmax(xf @ gate_W.T, axis=-1)
            weights, sel = jax.lax.top_k(gate_probs, TOP_K)
            weights = weights / jnp.sum(weights, axis=-1, keepdims=True)
            T = xf.shape[0]
            w_dense = jnp.zeros((T, E), xf.dtype).at[jnp.arange(T)[:, None], sel].add(weights)
            h = jnp.einsum('td,erd->ter', xf, A)
            h = h * (w_dense[:, :, None] * SCALING)
            return jnp.einsum('ter,eor->to', h, B)
        key = jax.random.key(seed)
        k0, k1, k2, k3, k4 = jax.random.split(key, 5)
        x = jax.random.normal(k0, (4, 512, DIN), jnp.float32)
        W_base = jax.random.normal(k1, (DOUT, DIN), jnp.float32) * 0.02
        gate_W = jax.random.normal(k2, (E, DIN), jnp.float32) * 0.02
        A = jax.random.normal(k3, (E, R, DIN), jnp.float32) * 0.02
        B = jax.random.normal(k4, (E, DOUT, R), jnp.float32) * 0.02
        return {'x': x, 'W_base': W_base, 'gate_W': gate_W, 'A': A, 'B': B}
    _L0_ffn_all = _L0_ffn_setup()
    _L0_ffn_in = {k: v for k, v in _L0_ffn_all.items() if k in ('W_base', 'gate_W', 'A', 'B')}
    del _L0_ffn_all
    return {'x': x, 'itok_B_8_3872': itok_B_8_3872, 'itok_B_0_15': itok_B_0_15, 'L0_cond_log_dt': _L0_cond_in['log_dt'], 'L0_cond_C': _L0_cond_in['C'], 'L0_cond_log_A_real': _L0_cond_in['log_A_real'], 'L0_cond_A_imag': _L0_cond_in['A_imag'], 'L0_cond_D': _L0_cond_in['D'], 'L0_attn_Wq': _L0_attn_in['Wq'], 'L0_attn_Wk': _L0_attn_in['Wk'], 'L0_attn_Wv': _L0_attn_in['Wv'], 'L0_attn_Wo': _L0_attn_in['Wo'], 'L0_cond2_weights': _L0_cond2_in['weights'], 'L0_ffn_W_base': _L0_ffn_in['W_base'], 'L0_ffn_gate_W': _L0_ffn_in['gate_W'], 'L0_ffn_A': _L0_ffn_in['A'], 'L0_ffn_B': _L0_ffn_in['B']}

def reference(x, itok_B_8_3872, itok_B_0_15, L0_cond_log_dt, L0_cond_C, L0_cond_log_A_real, L0_cond_A_imag, L0_cond_D, L0_attn_Wq, L0_attn_Wk, L0_attn_Wv, L0_attn_Wo, L0_cond2_weights, L0_ffn_W_base, L0_ffn_gate_W, L0_ffn_A, L0_ffn_B):
    import jax
    import jax.numpy as jnp

    def _L0_cond_ref(u, length, log_dt, C, log_A_real, A_imag, D):
        import math
        import jax, jax.numpy as jnp
        import numpy as np
        H, N, B, L = (64, 64, 16, 1024)
        DT_MIN, DT_MAX = (0.001, 0.1)

        def _get_kernel(log_dt, C, log_A_real, A_imag, length):
            Cc = C[..., 0] + 1j * C[..., 1]
            dt = jnp.exp(log_dt)
            A = -jnp.exp(log_A_real) + 1j * A_imag
            dtA = A * dt[:, None]
            P = dtA[:, :, None] * jnp.arange(length, dtype=jnp.float32)
            Cs = Cc * (jnp.exp(dtA) - 1.0) / A
            K = 2.0 * jnp.einsum('hn,hnl->hl', Cs, jnp.exp(P)).real
            return K
        Bq, Hq, Lq = u.shape
        mask = (jnp.arange(Lq) < length[:, None]).astype(u.dtype)
        u_m = u * mask[:, None, :]
        kernel = _get_kernel(log_dt, C, log_A_real, A_imag, Lq)
        n = 2 * Lq
        k_f = jnp.fft.rfft(kernel, n=n)
        u_f = jnp.fft.rfft(u_m, n=n)
        y = jnp.fft.irfft(u_f * k_f, n=n)[..., :Lq]
        y = y + u_m * D[:, None]
        return y * mask[:, None, :]

    def _L0_attn_ref(hidden_states, Wq, Wk, Wv, Wo):
        import jax, jax.numpy as jnp
        import numpy as np
        H = 32
        HKV = 8
        D = 1024
        HD = D // H
        S = 256
        MASK_OUT = 0.9
        MIN_REMAIN = 128
        THETA = 10000.0

        def rope_tables(seq_len, hd):
            inv_freq = 1.0 / THETA ** (jnp.arange(0, hd, 2, dtype=jnp.float32) / hd)
            t = jnp.arange(seq_len, dtype=jnp.float32)
            freqs = jnp.outer(t, inv_freq)
            emb = jnp.concatenate([freqs, freqs], axis=-1)
            return (jnp.cos(emb), jnp.sin(emb))

        def rotate_half(x):
            x1, x2 = jnp.split(x, 2, axis=-1)
            return jnp.concatenate([-x2, x1], axis=-1)

        def apply_rope(x, cos, sin):
            return x * cos + rotate_half(x) * sin
        B, Sq, Dm = hidden_states.shape
        dtype = hidden_states.dtype
        neg = jnp.finfo(dtype).min
        q = (hidden_states @ Wq.T).reshape(B, Sq, H, HD).transpose(0, 2, 1, 3)
        k = (hidden_states @ Wk.T).reshape(B, Sq, HKV, HD).transpose(0, 2, 1, 3)
        v = (hidden_states @ Wv.T).reshape(B, Sq, HKV, HD).transpose(0, 2, 1, 3)
        rep = H // HKV
        k = jnp.repeat(k, rep, axis=1)
        v = jnp.repeat(v, rep, axis=1)
        cos, sin = rope_tables(Sq, HD)
        qr = apply_rope(q, cos, sin)
        kr = apply_rope(k, cos, sin)
        draft = jnp.einsum('bhqd,bhkd->bhqk', qr, kr)
        qi = jnp.arange(Sq)
        ki = jnp.arange(Sq)
        causal_future = qi[:, None] < ki[None, :]
        draft = draft + jnp.where(causal_future, neg, jnp.asarray(0.0, dtype))
        num_remain = max(min(Sq, MIN_REMAIN), Sq - int(Sq * MASK_OUT))
        _, draft_indices = jax.lax.top_k(draft, num_remain)
        mask = jnp.full((B, H, Sq, Sq), neg, dtype)
        b_idx = jnp.arange(B)[:, None, None, None]
        h_idx = jnp.arange(H)[None, :, None, None]
        s_idx = jnp.arange(Sq)[None, None, :, None]
        mask = mask.at[b_idx, h_idx, s_idx, draft_indices].set(0.0)
        mask = jnp.where(causal_future[None, None, :, :], neg, mask)
        scores = jnp.einsum('bhqd,bhkd->bhqk', qr, kr) / np.sqrt(HD).astype(np.float32) + mask
        attn = jax.nn.softmax(scores, axis=-1)
        out = jnp.einsum('bhqk,bhkd->bhqd', attn, v)
        out = out.transpose(0, 2, 1, 3).reshape(B, Sq, Dm)
        return out @ Wo.T

    def _L0_cond2_ref(x, weights, condition):
        import jax, jax.numpy as jnp
        import numpy as np
        NUM_CONDITIONS = 16
        IN_CH = 64
        OUT_CH = 64
        B = 64
        T = 1024
        W = weights[condition]
        return jnp.einsum('bct,bcd->bdt', x, W)

    def _L0_ffn_ref(x, W_base, gate_W, A, B):
        import jax, jax.numpy as jnp
        import numpy as np
        E = 8
        R = 8
        DIN = 1024
        DOUT = 1024
        TOP_K = 2
        SCALING = 2.0

        def _moe_lora(xf, gate_W, A, B):
            gate_probs = jax.nn.softmax(xf @ gate_W.T, axis=-1)
            weights, sel = jax.lax.top_k(gate_probs, TOP_K)
            weights = weights / jnp.sum(weights, axis=-1, keepdims=True)
            T = xf.shape[0]
            w_dense = jnp.zeros((T, E), xf.dtype).at[jnp.arange(T)[:, None], sel].add(weights)
            h = jnp.einsum('td,erd->ter', xf, A)
            h = h * (w_dense[:, :, None] * SCALING)
            return jnp.einsum('ter,eor->to', h, B)
        xf = x.reshape(-1, x.shape[-1])
        out = xf @ W_base.T + _moe_lora(xf, gate_W, A, B)
        return out.reshape(*x.shape[:-1], DOUT)
    x = x + _L0_attn_ref(_L0_cond_ref(x, itok_B_8_3872, L0_cond_log_dt, L0_cond_C, L0_cond_log_A_real, L0_cond_A_imag, L0_cond_D), L0_attn_Wq, L0_attn_Wk, L0_attn_Wv, L0_attn_Wo)
    x = x + _L0_ffn_ref(_L0_cond2_ref(x, L0_cond2_weights, itok_B_0_15), L0_ffn_W_base, L0_ffn_gate_W, L0_ffn_A, L0_ffn_B)
    return x

_drawn_inputs = setup_inputs


def setup_inputs(seed=0):
    import zlib

    import numpy as np

    out = dict(_drawn_inputs(seed))
    spreads = {'L0_cond_log_A_real': (-0.6931471824645996, 0.2)}
    factors = {}
    for name, (base, spread) in spreads.items():
        noise = np.random.default_rng([zlib.crc32(name.encode()), seed]).standard_normal(out[name].shape)
        drawn = base * np.exp(spread * noise) if base else spread * noise
        out[name] = jnp.asarray(drawn.astype(out[name].dtype))
    for name, factor in factors.items():
        out[name] = (out[name] * factor).astype(out[name].dtype)
    return out
```

```python
from contextlib import ExitStack

import concourse.bass as bass
import numpy as np
from concourse import mybir

F32 = mybir.dt.float32
F32R = mybir.dt.float32r
I32 = mybir.dt.int32
U32 = mybir.dt.uint32
ALU = mybir.AluOpType
ACT = mybir.ActivationFunctionType
AX_X = mybir.AxisListType.X

P = 128
NB, S, L = 32, 64, 1024
TOK = NB * S
NJ = L // P
NMODE = 64
HD, NKV, REP = 32, 8, 4
NG = NKV // 4
NQT = NG * REP
NPAIR = NB // 2
NE, RANK = 8, 8
NPROJ = NE + NE * RANK
NCOND = 16
SCALING = 2.0
HB = 32
HGRP = 8
NHG = S // HGRP
GP = HGRP // 2
KROW = P - 1 + L
ROUND = 12582912.0
SIN_SCALE = 6.283184
TWO_PI = 2.0 * np.pi


def _short(v, bits):
    m, e = np.frexp(v)
    return float(np.ldexp(np.round(m * 2.0 ** bits), int(e) - bits))


PI_A = 6.28125
PI_B = _short(TWO_PI - PI_A, 11)
PI_C = float(TWO_PI - PI_A - PI_B)

CONSTS = {}


def _layout(*fields):
    at = 0
    for name, n in fields:
        CONSTS[name] = (at, n)
        at += n
    return at


NCONST = _layout(("ident", P), ("cos", S), ("sin", S), ("causal", S), ("pos", NJ), ("step", HB),
                 ("off", 3), ("off_rad", 3), ("half_pi", 1), ("chan", 1), ("iota8", NE))


def constants():
    t = np.zeros((P, NCONST), np.float32)

    def put(name, v):
        at, n = CONSTS[name]
        t[:, at:at + n] = v

    p = np.arange(P)
    put("ident", np.eye(P))
    inv_freq = (1.0 / np.float32(10000.0) ** (np.arange(0, HD, 2, dtype=np.float32) / HD)).astype(np.float32)
    freqs = np.outer(np.arange(S, dtype=np.float32), inv_freq).astype(np.float32)
    emb = np.concatenate([freqs, freqs], axis=-1)
    put("cos", np.cos(emb.astype(np.float64)).T[p % HD])
    sign = np.where(p % HD < HD // 2, -1.0, 1.0)[:, None]
    put("sin", sign * np.sin(emb.astype(np.float64)).T[p % HD])
    k, q = np.arange(S)[None, :], (p % S)[:, None]
    put("causal", np.where(q < k, np.finfo(np.float32).min, np.float32(0)))
    put("pos", p[:, None] + P * np.arange(NJ)[None, :])
    put("step", np.arange(HB)[None, :])
    im = (p >= NMODE)[:, None]
    off = np.concatenate([np.where(im, 0.5, 0.25), np.where(im, 0.25, 0.0), np.where(im, 0.0, 0.25)], axis=1)
    put("off", off)
    put("off_rad", off * SIN_SCALE)
    put("half_pi", np.pi / 2)
    put("chan", (p % S)[:, None])
    put("iota8", np.arange(NE)[None, :])
    return t


class Step:

    def __init__(self, ctx, nc, name):
        self.sem = ctx.enter_context(nc.semaphore(name))

    def done(self, ins):
        ins.then_inc(self.sem, 1)

    def wait(self, eng, n):
        if n > 0:
            eng.wait_ge(self.sem, n)


class Loads:

    def __init__(self, ctx, nc, name, ring, parts=1):
        self.sems = [ctx.enter_context(nc.semaphore(f"{name}{i}")) for i in range(ring)]
        self.ring, self.parts = ring, parts

    def start(self, eng, use, dst, src):
        if dst.dtype == F32R:
            dst = dst.bitcast(F32)
        if src.dtype == F32R:
            src = src.bitcast(F32)
        eng.dma_start(dst, src).then_inc(self.sems[use % self.ring], 16)

    def wait(self, eng, use):
        eng.wait_ge(self.sems[use % self.ring], 16 * self.parts * (use // self.ring + 1))


def across(ap, n):
    return ap.unsqueeze(1).to_broadcast([ap.shape[0], n, ap.shape[1]])


def along(ap, n):
    return ap.unsqueeze(2).to_broadcast([ap.shape[0], ap.shape[1], n])


def build(nc, x_conv, x_nat, lens, cond, log_dt, c_re, c_im, log_a, a_im, d_skip,
          w_qk, w_v, w_o, w_cond, w_base, w_proj, w_b, consts, out):
    ctx = ExitStack()
    with ctx:
        def sb(name, shape, dt=F32, stack=ctx):
            return stack.enter_context(nc.sbuf_tensor(name, shape, dt))

        def step(name):
            return Step(ctx, nc, name)

        def loads(name, ring=1, parts=1):
            return Loads(ctx, nc, name, ring, parts)

        kpad = nc.dram_tensor("kpad", [S, KROW + 1], F32, kind="Internal")
        qk_dram = [nc.dram_tensor(f"qk_{n}", [NG + NQT, P, TOK], F32, kind="Internal").ap() for n in ("hi", "lo")]
        v_dram = [nc.dram_tensor(f"v_{n}", [TOK, NKV * HD], F32, kind="Internal").ap() for n in ("hi", "lo")]
        x1_dram = nc.dram_tensor("x1_scratch", [TOK, L], F32, kind="Internal").ap()

        ps = ctx.enter_context(nc.psum_tensor("ps", [P, 8, 512], F32))

        cst = sb("cst", [P, NCONST])

        def C(name):
            at, n = CONSTS[name]
            return cst[:, at:at + n]

        s12 = ExitStack()
        y = [sb(f"y_{n}", [P, NJ, NB, S], F32R, s12) for n in ("hi", "lo")]
        WR = 3
        wraw = sb("wraw", [P, WR, NJ * P], F32, s12)
        wsp = [sb(f"w12_{n}", [P, WR, NJ * P], F32R, s12) for n in ("hi", "lo")]

        s1 = ExitStack()
        TR = 3
        toep = sb("toep", [P, TR, L], F32, s1)
        XH, XR = 2, 2
        xc = sb("xc", [P, XR, XH, NJ * NB], F32, s1)
        ym = sb("ym", [P, 2, 2, NJ * NB], F32, s1)
        valid = sb("valid", [P, NJ, NB], F32, s1)
        len_i = sb("len_i", [P, NB], I32, s1)
        len_f = sb("len_f", [P, NB], F32, s1)
        prm = sb("prm", [P, 5, S], F32, s1)
        t64 = sb("t64", [P, 25, S], F32, s1)
        d_row = sb("d_row", [1, S], F32, s1)
        zeros = sb("zeros", [S, P - 1], F32, s1)
        GC = HGRP * HB
        ph = sb("ph", [P, 2, GC], F32, s1)
        mg = sb("mg", [P, 2, GC], F32, s1)
        rn = sb("rn", [P, 3, GC], F32, s1)
        ltab = sb("ltab", [P, GC], F32, s1)
        rtab = sb("rtab", [P, GC], F32, s1)
        ksb = sb("ksb", [HB, 2, GC], F32, s1)
        s1.close()

        s2 = ExitStack()
        RR = 2
        rot = sb("rot", [P, RR, 512], F32, s2)
        rc = sb("rc", [P, RR, 512], F32, s2)
        rf = sb("rf", [P, RR, 512], F32, s2)
        SR = 3
        stg = [sb(f"stg_{n}", [P, SR, 512], F32R, s2) for n in ("hi", "lo")]
        s2.close()
        s12.close()

        mix = [sb(f"mix_{n}", [P, NPAIR, P], F32R) for n in ("hi", "lo")]
        cidx_i = sb("cidx_i", [P, NB], I32)
        cidx = sb("cidx", [P, NPAIR], U32)
        craw = sb("craw", [P, NPAIR, S])

        s3 = ExitStack()
        wo = [sb(f"wo_{n}", [P, NQT, L], F32R, s3) for n in ("hi", "lo")]
        WS = 2
        wstage3 = sb("wstage3", [P, WS, L], F32, s3)
        q_sb = [sb(f"q_{n}", [P, 2, 2, NQT, S], F32R, s3) for n in ("hi", "lo")]
        k_bd = [sb(f"kbd_{n}", [P, 2, 2, NG, 4 * S], F32R, s3) for n in ("hi", "lo")]
        v_bd = [sb(f"vbd_{n}", [P, 2, 2, NG, 2, P], F32R, s3) for n in ("hi", "lo")]
        sc = sb("sc", [P, 2, 1024], F32, s3)
        stat = sb("stat", [P, 2, 3, 16], F32, s3)
        pt = [sb(f"pt_{n}", [P, 1024], F32R, s3) for n in ("hi", "lo")]
        ot = [sb(f"ot_{n}", [P, 2, NQT, 2, S], F32R, s3) for n in ("hi", "lo")]
        xr = sb("xr", [P, 3, L], F32, s3)
        s3.close()

        s4 = ExitStack()
        wb = [sb(f"wb_{n}", [P, NJ, L], F32R, s4) for n in ("hi", "lo")]
        wpj = [sb(f"wpj_{n}", [P, NJ, NPROJ], F32R, s4) for n in ("hi", "lo")]
        wpj_raw = sb("wpj_raw", [P, NJ, NPROJ], F32, s4)
        bexp = [sb(f"bexp_{n}", [NE * RANK, L], F32R, s4) for n in ("hi", "lo")]
        bexp_raw = sb("bexp_raw", [NE * RANK, L], F32, s4)
        wstage4 = sb("wstage4", [P, WS, L], F32, s4)
        x1 = sb("x1", [P, 4, L], F32, s4)
        x1s = [sb(f"x1s_{n}", [P, 2, L], F32R, s4) for n in ("hi", "lo")]
        xf = [sb(f"xf_{n}", [P, 2, NJ, P], F32R, s4) for n in ("hi", "lo")]
        gt = sb("gt", [P, 8, NE], F32, s4)
        gi = sb("gi", [P, NE], U32, s4)
        gs = sb("gs", [P, 8], F32, s4)
        hw = sb("hw", [P, NE * RANK], F32, s4)
        ht = [sb(f"ht_{n}", [NE * RANK, P], F32R, s4) for n in ("hi", "lo")]
        s4.close()

        ld_cst, ld_prm, ld_len, ld_d = loads("ld_cst"), loads("ld_prm", 1, 10), loads("ld_len"), loads("ld_d")
        ld_cond, ld_cmix = loads("ld_cond"), loads("ld_cmix", 1, NPAIR)
        st_zero, st_k = loads("st_zero"), loads("st_k", 2)
        ld_toep, ld_xc = loads("ld_toep", TR), loads("ld_xc", XR)
        ld_w = [ctx.enter_context(nc.semaphore(f"ld_w{i}")) for i in range(WR)]
        st_stg = loads("st_stg", SR, 2)
        ld_w3, ld_q, ld_k, ld_v, ld_x = (loads("ld_w3", WS), loads("ld_q", 2, 4), loads("ld_k", 2, 16),
                                         loads("ld_v", 2, 16), loads("ld_x", 3))
        st_x1 = loads("st_x1", 3)
        ld_w4, ld_p4, ld_x1, st_out = loads("ld_w4", WS), loads("ld_p4", 1, 2), loads("ld_x1", 4), loads("st_out", 4)
        a_set, v_set, v_rho, v_ang, v_cs = map(step, ("a_set", "v_set", "v_rho", "v_ang", "v_cs"))
        g_zero, v_cidx, v_len, v_valid = map(step, ("g_zero", "v_cidx", "v_len", "v_valid"))
        g_mag, a_mag, v_ph, v_round, a_sin, v_tab = map(step, ("g_mag", "a_mag", "v_ph", "v_round", "a_sin", "v_tab"))
        pe_k, v_ke, v_k = map(step, ("pe_k", "v_ke", "v_k"))
        pe_conv, v_mask, a_yhi, g_ylo = map(step, ("pe_conv", "v_mask", "a_yhi", "g_ylo"))
        a_mix, g_mix = map(step, ("a_mix", "g_mix"))
        a_whi, g_wlo, pe_unit = map(step, ("a_whi", "g_wlo", "pe_unit"))
        pe_v, a_vhi, v_vlo = map(step, ("pe_v", "a_vhi", "v_vlo"))
        pe_m, v_rot, v_rcos, g_rsin, g_rsum, a_rhi, g_rlo = map(
            step, ("pe_m", "v_rot", "v_rcos", "g_rsin", "g_rsum", "a_rhi", "g_rlo"))
        v_zero3, g_zero3, a_w3, g_w3 = map(step, ("v_zero3", "g_zero3", "a_w3", "g_w3"))
        pe_s, v_sc, v_max, g_sub, a_exp, v_sum, v_rec, g_prob = map(
            step, ("pe_s", "v_sc", "v_max", "g_sub", "a_exp", "v_sum", "v_rec", "g_prob"))
        pe_t, a_pthi, v_ptlo, pe_o, a_othi, v_otlo, pe_y, v_x1 = map(
            step, ("pe_t", "a_pthi", "v_ptlo", "pe_o", "a_othi", "v_otlo", "pe_y", "v_x1"))
        a_p4, g_p4, a_w4, g_w4 = map(step, ("a_p4", "g_p4", "a_w4", "g_w4"))
        a_x1hi, g_x1lo, pe_mix, a_xfhi, v_xflo = map(step, ("a_x1hi", "g_x1lo", "pe_mix", "a_xfhi", "v_xflo"))
        pe_f, v_gate, a_gate, v_h, pe_ht, a_hthi, v_htlo, pe_out, v_out = map(
            step, ("pe_f", "v_gate", "a_gate", "v_h", "pe_ht", "a_hthi", "v_htlo", "pe_out", "v_out"))

        queues = {"sync": [], "gpsimd": [], "scalar": [], "vector": [], "tensor": []}

        def on(engine):
            return queues[engine].append

        def bank(n):
            return ps[:, n, :]

        PASSES = ((0, 0), (0, 1), (1, 0))

        names64 = ("dt", "ea", "ar", "rho", "rho32", "th", "k", "r", "vr", "v32", "e1", "tanh", "sh", "ch", "em1",
                   "cm1", "nr", "ni", "den", "t0", "t1", "gr", "gi", "cr", "ci")

        def M(name):
            return t64[:, names64.index(name), :]

        LOGDT, LOGA, AIM, CRE, CIM = (prm[:, i, :] for i in range(5))

        @on("sync")
        def _(sp):
            for half in (slice(0, NMODE), slice(NMODE, P)):
                for i, src in enumerate((log_dt.partition_broadcast(NMODE), log_a, a_im, c_re, c_im)):
                    ld_prm.start(sp, 0, prm[half, i, :], src)
            ld_cst.start(sp, 0, cst[:], consts)
            ld_d.start(sp, 0, d_row[:], d_skip.rearrange("(a h) -> a h", a=1))
            ld_len.start(sp, 0, len_i[:], lens.partition_broadcast(P))
            g_zero.wait(sp, 1)
            st_zero.start(sp, 0, kpad.ap()[:, 0:P - 1], zeros[:])

        @on("scalar")
        def _(act):
            ld_prm.wait(act, 0)
            a_set.done(act.activation(M("dt"), LOGDT, ACT.Exp))
            a_set.done(act.activation(M("ea"), LOGA, ACT.Exp))
            v_rho.wait(act, 1)
            a_set.done(act.activation(M("e1"), M("rho"), ACT.Exp))
            a_set.done(act.activation(M("tanh"), M("rho"), ACT.Tanh, scale=0.5))

        def magnitudes(act, g):
            for i in range(2):
                g_mag.wait(act, 2 * g + i + 1)
                a_mag.done(act.activation(mg[:, i, :], mg[:, i, :], ACT.Exp))

        def sines(act, g):
            v_round.wait(act, 3 * (g + 1))
            for i in range(3):
                a_sin.done(act.activation(rn[:, i, :], rn[:, i, :], ACT.Sin, scale=-SIN_SCALE,
                                          bias=C("off_rad")[:, i:i + 1]))

        @on("scalar")
        def _(act):
            magnitudes(act, 0)
            v_ang.wait(act, 1)
            ld_cst.wait(act, 0)
            a_set.done(act.activation(M("sh"), M("r"), ACT.Sin, scale=0.5))
            a_set.done(act.activation(M("ch"), M("r"), ACT.Sin, scale=0.4999998, bias=C("half_pi")))
            sines(act, 0)

        def exponents(gp, g):
            v_tab.wait(gp, 2 * g)
            hs = slice(g * HGRP, (g + 1) * HGRP)
            for i, r in enumerate(("rho32", "rho")):
                g_mag.done(gp.tensor_tensor(mg[:, i, :].rearrange("p (h s) -> p h s", s=HB), along(M(r)[:, hs], HB),
                                            across(C("step"), HGRP), ALU.mult))

        @on("gpsimd")
        def _(gp):
            g_zero.done(gp.memset(zeros[:], 0.0))
            ld_cst.wait(gp, 0)
            v_rho.wait(gp, 1)
            exponents(gp, 0)

        def chain(v, ins):
            v_set.done(ins)
            chain.n += 1
            v_set.wait(v, chain.n)

        chain.n = 0

        @on("vector")
        def _(v):
            a_set.wait(v, 2)
            chain(v, v.tensor_scalar(M("ar"), M("ea"), -1.0, None, ALU.mult))
            chain(v, v.tensor_tensor(M("rho"), M("ar"), M("dt"), ALU.mult))
            v_rho.done(v.tensor_scalar(M("rho32"), M("rho"), float(HB), None, ALU.mult))
            chain(v, v.tensor_tensor(M("th"), AIM, M("dt"), ALU.mult))
            chain(v, v.tensor_scalar(M("k"), M("th"), 1.0 / TWO_PI, ROUND, ALU.mult, ALU.add))
            chain(v, v.tensor_scalar(M("k"), M("k"), ROUND, None, ALU.subtract))
            chain(v, v.scalar_tensor_tensor(M("t0"), M("k"), -PI_A, M("th"), ALU.mult, ALU.add))
            chain(v, v.scalar_tensor_tensor(M("t1"), M("k"), -PI_B, M("t0"), ALU.mult, ALU.add))
            chain(v, v.scalar_tensor_tensor(M("r"), M("k"), -PI_C, M("t1"), ALU.mult, ALU.add))
            chain(v, v.tensor_scalar(M("vr"), M("r"), 1.0 / TWO_PI, None, ALU.mult))
            chain(v, v.tensor_scalar(M("t0"), M("vr"), float(HB), ROUND, ALU.mult, ALU.add))
            chain(v, v.tensor_scalar(M("t1"), M("t0"), ROUND, None, ALU.subtract))
            v_ang.done(v.scalar_tensor_tensor(M("v32"), M("vr"), float(HB), M("t1"), ALU.mult, ALU.subtract))
            v_ang.wait(v, 1)

        def phases(v, g):
            hs = slice(g * HGRP, (g + 1) * HGRP)
            for i, r in enumerate(("v32", "vr")):
                v_ph.done(v.tensor_tensor(ph[:, i, :].rearrange("p (h s) -> p h s", s=HB), along(M(r)[:, hs], HB),
                                          across(C("step"), HGRP), ALU.mult))
            v_ph.wait(v, 5 * g + 2)
            for i, part in enumerate((0, 0, 1)):
                v_ph.done(v.tensor_scalar(rn[:, i, :], ph[:, part, :], C("off")[:, i:i + 1], ROUND, ALU.add, ALU.add))
            v_ph.wait(v, 5 * g + 5)
            for i, part in enumerate((0, 0, 1)):
                v_round.done(v.scalar_tensor_tensor(rn[:, i, :], rn[:, i, :], ROUND, ph[:, part, :],
                                                    ALU.subtract, ALU.subtract))

        @on("vector")
        def _(v):
            ld_cst.wait(v, 0)
            phases(v, 0)
            a_set.wait(v, 6)
            chain(v, v.scalar_tensor_tensor(M("em1"), M("e1"), 1.0, M("tanh"), ALU.add, ALU.mult))
            chain(v, v.scalar_tensor_tensor(M("cm1"), M("sh"), -2.0, M("sh"), ALU.mult, ALU.mult))
            chain(v, v.scalar_tensor_tensor(M("t0"), M("cm1"), 1.0, M("em1"), ALU.add, ALU.mult))
            chain(v, v.tensor_tensor(M("nr"), M("t0"), M("cm1"), ALU.add))
            chain(v, v.scalar_tensor_tensor(M("t1"), M("sh"), 2.0, M("ch"), ALU.mult, ALU.mult))
            chain(v, v.tensor_tensor(M("ni"), M("t1"), M("e1"), ALU.mult))
            chain(v, v.tensor_tensor(M("t0"), M("ar"), M("ar"), ALU.mult))
            chain(v, v.tensor_tensor(M("t1"), AIM, AIM, ALU.mult))
            chain(v, v.tensor_tensor(M("k"), M("t0"), M("t1"), ALU.add))
            chain(v, v.reciprocal(M("den"), M("k")))
            chain(v, v.tensor_tensor(M("t0"), M("nr"), M("ar"), ALU.mult))
            chain(v, v.tensor_tensor(M("t1"), M("ni"), AIM, ALU.mult))
            chain(v, v.tensor_tensor(M("t0"), M("t0"), M("t1"), ALU.add))
            chain(v, v.tensor_tensor(M("gr"), M("t0"), M("den"), ALU.mult))
            chain(v, v.tensor_tensor(M("t0"), M("ni"), M("ar"), ALU.mult))
            chain(v, v.tensor_tensor(M("t1"), M("nr"), AIM, ALU.mult))
            chain(v, v.tensor_tensor(M("t0"), M("t0"), M("t1"), ALU.subtract))
            chain(v, v.tensor_tensor(M("gi"), M("t0"), M("den"), ALU.mult))
            chain(v, v.scalar_tensor_tensor(M("t0"), M("gr"), 2.0, CRE, ALU.mult, ALU.mult))
            chain(v, v.scalar_tensor_tensor(M("t1"), M("gi"), 2.0, CIM, ALU.mult, ALU.mult))
            chain(v, v.tensor_tensor(M("cr"), M("t0"), M("t1"), ALU.subtract))
            chain(v, v.scalar_tensor_tensor(M("t0"), M("gi"), 2.0, CRE, ALU.mult, ALU.mult))
            chain(v, v.scalar_tensor_tensor(M("t1"), M("gr"), 2.0, CIM, ALU.mult, ALU.mult))
            chain(v, v.tensor_tensor(M("ci"), M("t0"), M("t1"), ALU.add))

        def tables(v, g):
            hs = slice(g * HGRP, (g + 1) * HGRP)
            a_sin.wait(v, 3 * (g + 1))
            for i, c in enumerate(("cr", "ci")):
                w = rn[:, i, :].rearrange("p (h s) -> p h s", s=HB)
                chain(v, v.tensor_tensor(w, w, along(M(c)[:, hs], HB), ALU.mult))
            chain(v, v.tensor_tensor(rn[:, 0, :], rn[:, 0, :], rn[:, 1, :], ALU.subtract))
            a_mag.wait(v, 2 * (g + 1))
            pe_k.wait(v, g)
            v_tab.done(v.tensor_tensor(ltab[:], rn[:, 0, :], mg[:, 0, :], ALU.mult))
            v_tab.done(v.tensor_tensor(rtab[:], rn[:, 2, :], mg[:, 1, :], ALU.mult))

        def kernels_pe(pe, g):
            v_tab.wait(pe, 2 * (g + 1))
            v_ke.wait(pe, g - 1)
            for h in range(HGRP):
                cols = slice(h * HB, (h + 1) * HB)
                mm = pe.matmul(ps[0:HB, 4 + g % 2, cols], ltab[:, cols], rtab[:, cols], start=True, stop=True)
            pe_k.done(mm)

        def kernels_out(v, g):
            pe_k.wait(v, g + 1)
            if g >= 2:
                st_k.wait(v, g - 2)
            v_ke.done(v.tensor_copy(ksb[:, g % 2, :], ps[0:HB, 4 + g % 2, 0:GC]))
            v_ke.wait(v, g + 1)
            k0 = ksb[0:1, g % 2, :].rearrange("p (h s) -> p h s", s=HB)[:, :, 0]
            v_k.done(v.tensor_tensor(k0, k0, d_row[:, g * HGRP:(g + 1) * HGRP], ALU.add))

        def store_kernels(sp, g):
            v_k.wait(sp, g + 1)
            st_k.start(sp, g, kpad.ap()[g * HGRP:(g + 1) * HGRP, P - 1:P - 1 + L].rearrange("h (a b) -> a h b", b=HB),
                       ksb[:, g % 2, :].rearrange("a (h b) -> a h b", b=HB))

        def load_x_conv(sp, t):
            if t >= XR:
                pe_conv.wait(sp, (t - XR + 1) * XH)
            ld_xc.start(sp, t, xc[:, t % XR, :, :], x_conv[:, t * XH:(t + 1) * XH, :])

        @on("sync")
        def _(sp):
            load_x_conv(sp, 0)
            load_x_conv(sp, 1)
            sp.dma_start(wraw[:, 0:2, :].rearrange("p a n -> p (a n)"), w_v).then_inc(ld_w[0], 16)
            sp.dma_start(wraw[:, 2, :], w_qk[0]).then_inc(ld_w[2], 16)
            store_kernels(sp, 0)
            st_zero.wait(sp, 0)
            for h in range(S):
                g = h // HGRP
                if h % HGRP == 0:
                    st_k.wait(sp, g)
                if h % HGRP == 6 and g + 1 < NHG:
                    store_kernels(sp, g + 1)
                if h % XH == 0 and 0 < h // XH and h // XH + XR - 1 < S // XH:
                    load_x_conv(sp, h // XH + XR - 1)
                if h >= TR:
                    pe_conv.wait(sp, h - TR + 1)
                ld_toep.start(sp, h, toep[:, h % TR, :], bass.AP(kpad, h * (KROW + 1), [[1, P], [1, L]]))

        def convolve(pe, h):
            n, i = h // 2, h % 2
            if h % XH == 0:
                ld_xc.wait(pe, h // XH)
            if i == 0:
                v_mask.wait(pe, n - 3)
            ld_toep.wait(pe, h)
            for d in range(NJ):
                mm = pe.matmul(ps[:, n % 4, i * 256 + d * NB:(i + 1) * 256], toep[:, h % TR, d * P:(d + 1) * P],
                               xc[:, (h // XH) % XR, h % XH, 0:(NJ - d) * NB], start=(d == 0), stop=(d == NJ - 1))
            pe_conv.done(mm)

        @on("tensor")
        def _(pe):
            kernels_pe(pe, 0)
            for h in range(S):
                convolve(pe, h)
                if h % HGRP == 3 and h // HGRP + 1 < NHG:
                    kernels_pe(pe, h // HGRP + 1)

        @on("vector")
        def _(v):
            ld_len.wait(v, 0)
            v_len.done(v.tensor_copy(len_f[:], len_i[:]))
            v_len.wait(v, 1)
            v_valid.done(v.tensor_tensor(valid[:], across(len_f[:], NJ), along(C("pos"), NB), ALU.is_gt))
            tables(v, 0)
            ld_d.wait(v, 0)
            kernels_out(v, 0)
            v_valid.wait(v, 1)
            phases(v, 1)
            for n in range(S // 2):
                g, k = n // GP, n % GP
                if k == 0 and g + 1 < NHG:
                    tables(v, g + 1)
                pe_conv.wait(v, 2 * n + 2)
                a_yhi.wait(v, n - 1)
                g_ylo.wait(v, n - 1)
                v_mask.done(v.tensor_tensor(ym[:, n % 2, :, :], bank(n % 4).rearrange("p (i c) -> p i c", i=2),
                                            across(valid[:].rearrange("p j b -> p (j b)"), 2), ALU.mult))
                if k == 1 and g + 1 < NHG:
                    kernels_out(v, g + 1)
                if k == 2 and g + 2 < NHG:
                    phases(v, g + 2)

        def y_pair(part, n, i):
            return y[part][:, :, :, 2 * n + i]

        def ym_pair(n, i):
            return ym[:, n % 2, i, :].rearrange("p (j b) -> p j b", b=NB)

        @on("scalar")
        def _(act):
            weight_hi(act, -1)
            weight_hi(act, 0)
            magnitudes(act, 1)
            sines(act, 1)
            for n in range(S // 2):
                g = n // GP
                if n % GP == 3 and g + 2 < NHG:
                    magnitudes(act, g + 2)
                    sines(act, g + 2)
                v_mask.wait(act, n + 1)
                act.activation(y_pair(0, n, 0), ym_pair(n, 0), ACT.Copy)
                a_yhi.done(act.activation(y_pair(0, n, 1), ym_pair(n, 1), ACT.Copy))

        @on("gpsimd")
        def _(gp):
            weight_lo(gp, -1)
            weight_lo(gp, 0)
            exponents(gp, 1)
            for n in range(S // 2):
                g = n // GP
                if n % GP == 2 and g + 2 < NHG:
                    exponents(gp, g + 2)
                a_yhi.wait(gp, n + 1)
                gp.tensor_tensor(y_pair(1, n, 0), ym_pair(n, 0), y_pair(0, n, 0).bitcast(F32), ALU.subtract)
                g_ylo.done(gp.tensor_tensor(y_pair(1, n, 1), ym_pair(n, 1), y_pair(0, n, 1).bitcast(F32), ALU.subtract))

        NU = NG + NQT

        def w_slot(m):
            return slice(0, 2) if m < 0 else slice((m + 2) % WR, (m + 2) % WR + 1)

        def w_loaded(eng, m):
            s = w_slot(m).start
            eng.wait_ge(ld_w[s], 16 * (1 if m < 0 else (m - 1) // WR + 2 if s == 0 else m // WR + 1))

        def w_users(m):
            return 0 if m <= 0 else 1 if m < WR else m - WR + 2

        def load_weights(sp, m):
            a_whi.wait(sp, w_users(m))
            g_wlo.wait(sp, w_users(m))
            s = w_slot(m).start
            sp.dma_start(wraw[:, s, :], w_qk[m]).then_inc(ld_w[s], 16)

        def weight_hi(act, m):
            w_loaded(act, m)
            pe_unit.wait(act, w_users(m))
            a_whi.done(act.activation(wsp[0][:, w_slot(m), :], wraw[:, w_slot(m), :], ACT.Copy))

        def weight_lo(gp, m):
            a_whi.wait(gp, m + 2)
            g_wlo.done(gp.tensor_tensor(wsp[1][:, w_slot(m), :], wraw[:, w_slot(m), :],
                                        wsp[0][:, w_slot(m), :].bitcast(F32), ALU.subtract))

        NVB = TOK // P // 2

        @on("sync")
        def _(sp):
            load_weights(sp, 1)
            load_weights(sp, 2)
            for n in range(NVB):
                a_vhi.wait(sp, n + 1)
                v_vlo.wait(sp, n + 1)
                for part in range(2):
                    dst = v_dram[part][2 * n * P:(2 * n + 2) * P, :].rearrange("(t p) d -> p t d", p=P)
                    st_stg.start(sp, n, dst, stg[part][:, n % SR, :].rearrange("p (t d) -> p t d", t=2))
            for m in range(NU):
                if m + WR < NU:
                    load_weights(sp, m + WR)
                for g in range(4):
                    n = NVB + 4 * m + g
                    a_rhi.wait(sp, 4 * m + g + 1)
                    g_rlo.wait(sp, 4 * m + g + 1)
                    for part in range(2):
                        st_stg.start(sp, n, qk_dram[part][m, :, g * 512:(g + 1) * 512], stg[part][:, n % SR, :])
            for n in range(NVB + 4 * NU - SR, NVB + 4 * NU):
                st_stg.wait(sp, n)

        @on("tensor")
        def _(pe):
            yt = [p.rearrange("p j b s -> p j (b s)") for p in (y[0][:], y[1][:])]
            wv = [w[:, 0:2, :].rearrange("p a n -> p (a n)").rearrange("p (j d) -> p j d", j=NJ) for w in wsp]
            v_mask.wait(pe, S // 2)
            v_ke.wait(pe, NHG)
            a_yhi.wait(pe, S // 2)
            g_ylo.wait(pe, S // 2)
            a_whi.wait(pe, 1)
            g_wlo.wait(pe, 1)
            for n in range(NVB):
                for t in range(2):
                    tok = slice((2 * n + t) * P, (2 * n + t + 1) * P)
                    for j in range(NJ):
                        for a, b in PASSES:
                            mm = pe.matmul(ps[:, n, t * 256:(t + 1) * 256], yt[a][:, j, tok], wv[b][:, j, :],
                                           start=(j == 0 and a + b == 0), stop=(j == NJ - 1 and a == 1))
                pe_v.done(mm) if n < NVB - 1 else pe_unit.done(mm)
            for m in range(NU):
                a_whi.wait(pe, m + 2)
                g_wlo.wait(pe, m + 2)
                for j in range(NJ):
                    for a, b in PASSES:
                        w = wsp[a][:, w_slot(m).start, :].rearrange("p (j d) -> p j d", j=NJ)[:, j, :]
                        for g in range(4):
                            if j == 0 and a + b == 0:
                                if m < 2:
                                    v_vlo.wait(pe, 4 * m + g + 1)
                                else:
                                    v_rcos.wait(pe, 4 * (m - 2) + g + 1)
                            mm = pe.matmul(ps[:, 4 * (m % 2) + g, :], w, yt[b][:, j, g * 512:(g + 1) * 512],
                                           start=(j == 0 and a + b == 0), stop=(j == NJ - 1 and a == 1))
                            if j == NJ - 1 and a == 1:
                                if g < 3:
                                    pe_m.done(mm)
                                else:
                                    pe_unit.done(mm)

        def v_ready(eng, n):
            if n < NVB - 1:
                pe_v.wait(eng, n + 1)
            else:
                pe_unit.wait(eng, 1)

        def m_ready(eng, m, g):
            if g < 3:
                pe_m.wait(eng, 3 * m + g + 1)
            else:
                pe_unit.wait(eng, m + 2)

        def staging_free(eng, n):
            if n >= SR:
                st_stg.wait(eng, n - SR)

        @on("scalar")
        def _(act):
            g_ylo.wait(act, S // 2)
            for n in range(NVB):
                v_ready(act, n)
                staging_free(act, n)
                a_vhi.done(act.activation(stg[0][:, n % SR, :], bank(n), ACT.Copy))
            for m in range(NU):
                if m < NU - 1:
                    weight_hi(act, m + 1)
                for g in range(4):
                    n = 4 * m + g
                    g_rsum.wait(act, n + 1)
                    staging_free(act, NVB + n)
                    a_rhi.done(act.activation(stg[0][:, (NVB + n) % SR, :], rf[:, n % RR, :], ACT.Copy))

        @on("vector")
        def _(v):
            for n in range(NVB):
                a_vhi.wait(v, n + 1)
                v_vlo.done(v.tensor_tensor(stg[1][:, n % SR, :], bank(n), stg[0][:, n % SR, :].bitcast(F32),
                                           ALU.subtract))
            swap = [(i + HD // 2) % HD for i in range(HD)]
            for n in range(4 * NU):
                m, g = n // 4, n % 4
                m_ready(v, m, g)
                g_rsum.wait(v, n + 1 - RR)
                acc = bank(4 * (m % 2) + g)
                v_rot.done(v.stream_shuffle(rot[:, n % RR, :], acc, swap))
                v_rcos.done(v.tensor_tensor(rc[:, n % RR, :].rearrange("p (b s) -> p b s", s=S),
                                            acc.rearrange("p (b s) -> p b s", s=S), across(C("cos"), 8), ALU.mult))

        @on("gpsimd")
        def _(gp):
            for m in range(NU):
                if m < NU - 1:
                    weight_lo(gp, m + 1)
                for g in range(4):
                    n = 4 * m + g
                    s = (NVB + n) % SR
                    v_rot.wait(gp, n + 1)
                    r = rot[:, n % RR, :].rearrange("p (b s) -> p b s", s=S)
                    g_rsin.done(gp.tensor_tensor(r, r, across(C("sin"), 8), ALU.mult))
                    g_rsin.wait(gp, n + 1)
                    v_rcos.wait(gp, n + 1)
                    a_rhi.wait(gp, n + 1 - RR)
                    g_rsum.done(gp.tensor_tensor(rf[:, n % RR, :], rot[:, n % RR, :], rc[:, n % RR, :], ALU.add))
                    a_rhi.wait(gp, n + 1)
                    g_rlo.done(gp.tensor_tensor(stg[1][:, s, :], rf[:, n % RR, :], stg[0][:, s, :].bitcast(F32),
                                                ALU.subtract))

        NUNIT = 2 * NPAIR
        HALF_SLOTS = range(-2, NUNIT + 2)
        INV_SQRT = 1.0 / float(np.sqrt(HD))

        def load_pair(sp, i):
            if i >= 2:
                pe_s.wait(sp, 2 * (i - 2) + 2)
            for part in range(2):
                for b in range(2):
                    tok = slice((2 * i + b) * S, (2 * i + b + 1) * S)
                    ld_q.start(sp, i, q_sb[part][:, i % 2, b, :, :], qk_dram[part][NG:NU, :, tok].rearrange("t p k -> p t k"))
                for g in range(4):
                    rows = slice(g * HD, (g + 1) * HD)
                    for b in range(2):
                        ld_k.start(sp, i, k_bd[part][rows, i % 2, b, :, g * S:(g + 1) * S],
                                   qk_dram[part][0:NG, rows, (2 * i + b) * S:(2 * i + b + 1) * S].rearrange("t p k -> p t k"))
            if i >= 2:
                pe_o.wait(sp, 2 * (i - 2) + 2)
            for part in range(2):
                for pair in range(2):
                    for x in range(2):
                        at = pair * 64 + x * HD
                        for b in range(2):
                            src = v_dram[part][(2 * i + b) * S:(2 * i + b + 1) * S, :].rearrange("k (t c) -> k t c", c=P)
                            ld_v.start(sp, i, v_bd[part][x * S:(x + 1) * S, i % 2, b, :, pair, at:at + HD],
                                       src[:, :, at:at + HD])

        def load_residual(sp, i):
            if i >= 3:
                st_x1.wait(sp, i - 3)
            ld_x.start(sp, i, xr[:, i % 3, :], x_nat[i * P:(i + 1) * P, :])

        @on("sync")
        def _(sp):
            v_zero3.wait(sp, 2)
            g_zero3.wait(sp, 2)
            load_pair(sp, 0)
            load_pair(sp, 1)
            load_residual(sp, 0)
            for t in range(NQT):
                if t >= WS:
                    a_w3.wait(sp, t - WS + 1)
                    g_w3.wait(sp, t - WS + 1)
                ld_w3.start(sp, t, wstage3[:, t % WS, :], w_o[:, t, :])
            load_residual(sp, 1)
            ld_cond.start(sp, 0, cidx_i[:], cond.partition_broadcast(P))
            for i in range(NPAIR):
                if i + 2 < NPAIR:
                    load_pair(sp, i + 2)
                    load_residual(sp, i + 2)
                v_x1.wait(sp, 2 * i + 2)
                st_x1.start(sp, i, x1_dram[i * P:(i + 1) * P, :], xr[:, i % 3, :])
            for i in range(NPAIR - 3, NPAIR):
                st_x1.wait(sp, i)

        def scores(pe, u):
            i, b = u // 2, u % 2
            ld_q.wait(pe, i)
            ld_k.wait(pe, i)
            v_sc.wait(pe, u)
            for G in range(NG):
                for rp in range(2):
                    for a, c in PASSES:
                        mm = pe.matmul(ps[:, G, rp * 256:(rp + 1) * 256],
                                       q_sb[a][:, i % 2, b, G * REP + 2 * rp:G * REP + 2 * rp + 2, :],
                                       k_bd[c][:, i % 2, b, G, :], start=(a + c == 0), stop=(a == 1))
            pe_s.done(mm)

        def turn_probs(pe, u):
            g_prob.wait(pe, u + 1)
            v_ptlo.wait(pe, u)
            for G in range(NG):
                for rp in range(2):
                    for pair in range(2):
                        at = G * 512 + rp * 256 + pair * P
                        mm = pe.transpose(ps[:, 2 + G, pair * 256 + rp * P:pair * 256 + (rp + 1) * P],
                                          sc[:, u % 2, at:at + P], C("ident"))
            pe_t.done(mm)

        def values(pe, u):
            i, b = u // 2, u % 2
            ld_v.wait(pe, i)
            a_pthi.wait(pe, u + 1)
            v_ptlo.wait(pe, u + 1)
            v_otlo.wait(pe, u - 1)
            for G in range(NG):
                for pair in range(2):
                    for a, c in PASSES:
                        at = G * 512 + pair * 256
                        mm = pe.matmul(ps[:, 4 + u % 2, G * 256:(G + 1) * 256], v_bd[c][:, i % 2, b, G, pair, :],
                                       pt[a][:, at:at + 256], start=(pair == 0 and a + c == 0),
                                       stop=(pair == 1 and a == 1))
            pe_o.done(mm)

        def project(pe, i, quarter):
            n, tiles = quarter // 2, range(quarter % 2 * 4, quarter % 2 * 4 + 4)
            if quarter == 0:
                a_othi.wait(pe, 2 * i + 2)
                v_otlo.wait(pe, 2 * i + 2)
            if quarter % 2 == 0:
                v_x1.wait(pe, 2 * (i - 1) + n + 1)
            for t in tiles:
                a_w3.wait(pe, t + 1)
                g_w3.wait(pe, t + 1)
                for a, c in PASSES:
                    mm = pe.matmul(ps[:, 6 + n, :], ot[a][:, i % 2, t, :, :], wo[c][:, t, n * 512:(n + 1) * 512],
                                   start=(t == 0 and a + c == 0), stop=(t == NQT - 1 and a == 1))
            pe_y.done(mm)

        @on("tensor")
        def _(pe):
            v_rcos.wait(pe, 4 * NU)
            for w in HALF_SLOTS:
                i, k = w // 2 - 1, w % 2
                if 0 <= w < NUNIT:
                    turn_probs(pe, w)
                if i >= 0:
                    project(pe, i, 2 * k)
                if 0 <= w < NUNIT:
                    values(pe, w)
                if w + 2 < NUNIT:
                    scores(pe, w + 2)
                if i >= 0:
                    project(pe, i, 2 * k + 1)

        def sc_groups(u):
            return sc[:, u % 2, :].rearrange("p (g k) -> p g k", k=S)

        @on("vector")
        def _(v):
            pe_unit.wait(v, NU + 1)
            for part in range(2):
                v_zero3.done(v.memset(k_bd[part][:].bitcast(F32), 0.0))
            for w in HALF_SLOTS:
                if w == 0:
                    ld_cond.wait(v, 0)
                    for b in range(2):
                        r = slice(b * S, (b + 1) * S)
                        v_cidx.done(v.tensor_scalar(cidx[r, :], cidx_i[r, b::2], float(S), C("chan")[r, :],
                                                    ALU.mult, ALU.add))
                if 0 <= w < NUNIT:
                    a_pthi.wait(v, w + 1)
                    v_ptlo.done(v.tensor_tensor(pt[1][:], ps[:, 2:4, :].rearrange("p a c -> p (a c)"),
                                                pt[0][:].bitcast(F32), ALU.subtract))
                if w >= 3:
                    i, n = (w - 1) // 2 - 1, (w - 1) % 2
                    pe_y.wait(v, 4 * i + 2 * n + 2)
                    ld_x.wait(v, i)
                    x = xr[:, i % 3, n * 512:(n + 1) * 512]
                    v_x1.done(v.tensor_tensor(x, bank(6 + n), x, ALU.add))
                if 0 <= w + 1 < NUNIT:
                    u = w + 1
                    a_exp.wait(v, u + 1)
                    v_sum.done(v.tensor_reduce(stat[:, u % 2, 1, :], sc_groups(u), AX_X, ALU.add))
                    v_sum.wait(v, u + 1)
                    v_rec.done(v.reciprocal(stat[:, u % 2, 2, :], stat[:, u % 2, 1, :]))
                if 0 <= w < NUNIT:
                    a_othi.wait(v, w + 1)
                    v_otlo.done(v.tensor_tensor(ot[1][:, (w // 2) % 2, :, w % 2, :],
                                                bank(4 + w % 2).rearrange("p (t q) -> p t q", q=S),
                                                ot[0][:, (w // 2) % 2, :, w % 2, :].bitcast(F32), ALU.subtract))
                if w + 2 < NUNIT:
                    u = w + 2
                    pe_s.wait(v, u + 1)
                    pe_t.wait(v, u - 1)
                    v_sc.done(v.scalar_tensor_tensor(sc_groups(u), ps[:, 0:2, :].rearrange("p a (g k) -> p (a g) k", k=S),
                                                     INV_SQRT, across(C("causal"), 16), ALU.mult, ALU.add))
                    v_sc.wait(v, u + 1)
                    v_max.done(v.tensor_reduce(stat[:, u % 2, 0, :], sc_groups(u), AX_X, ALU.max))
            i = NPAIR - 1
            pe_y.wait(v, 4 * i + 4)
            x = xr[:, i % 3, 512:]
            v_x1.done(v.tensor_tensor(x, bank(7), x, ALU.add))

        @on("gpsimd")
        def _(gp):
            pe_unit.wait(gp, NU + 1)
            for part in range(2):
                g_zero3.done(gp.memset(v_bd[part][:].bitcast(F32), 0.0))
            for w in range(-1, NUNIT - 1):
                u = w + 1
                v_max.wait(gp, u + 1)
                g_sub.done(gp.tensor_tensor(sc_groups(u), sc_groups(u), along(stat[:, u % 2, 0, :], S), ALU.subtract))
                if u < 1:
                    for t in range(NQT):
                        a_w3.wait(gp, t + 1)
                        g_w3.done(gp.tensor_tensor(wo[1][:, t, :], wstage3[:, t % WS, :], wo[0][:, t, :].bitcast(F32),
                                                   ALU.subtract))
                if u == 2:
                    for part in range(2):
                        g_zero3.done(gp.memset(mix[part][:].bitcast(F32), 0.0))
                    v_cidx.wait(gp, 2)
                    rows = w_cond.rearrange("n c d -> (n c) d")
                    for i in range(NPAIR):
                        gp.indirect_dma_start(craw[:, i, :], None, rows,
                                              bass.IndirectOffsetOnAxis(ap=cidx[:, i:i + 1], axis=0))\
                          .then_inc(ld_cmix.sems[0], 16)
                if u == 8:
                    a_mix.wait(gp, 2)
                    g_sub.wait(gp, u + 1)
                    for b in range(2):
                        r = slice(b * S, (b + 1) * S)
                        g_mix.done(gp.tensor_tensor(mix[1][r, :, b * S:(b + 1) * S], craw[r, :, :],
                                                    mix[0][r, :, b * S:(b + 1) * S].bitcast(F32), ALU.subtract))
                        g_mix.wait(gp, b + 1)
                v_rec.wait(gp, u + 1)
                g_prob.done(gp.tensor_tensor(sc_groups(u), sc_groups(u), along(stat[:, u % 2, 2, :], S), ALU.mult))

        @on("scalar")
        def _(act):
            for w in HALF_SLOTS:
                if 0 <= w < NUNIT:
                    pe_t.wait(act, w + 1)
                    pe_o.wait(act, w)
                    a_pthi.done(act.activation(pt[0][:], ps[:, 2:4, :].rearrange("p a c -> p (a c)"), ACT.Copy))
                if 0 <= w + 1 < NUNIT:
                    u = w + 1
                    g_sub.wait(act, u + 1)
                    a_exp.done(act.activation(sc[:, u % 2, :], sc[:, u % 2, :], ACT.Exp))
                if w == -1:
                    for t in range(NQT):
                        ld_w3.wait(act, t)
                        a_w3.done(act.activation(wo[0][:, t, :], wstage3[:, t % WS, :], ACT.Copy))
                if w == 4:
                    ld_cmix.wait(act, 0)
                    g_zero3.wait(act, 4)
                    for b in range(2):
                        r = slice(b * S, (b + 1) * S)
                        a_mix.done(act.activation(mix[0][r, :, b * S:(b + 1) * S], craw[r, :, :], ACT.Copy))
                if 0 <= w < NUNIT:
                    i = w // 2
                    pe_o.wait(act, w + 1)
                    pe_y.wait(act, 4 * (i - 1))
                    a_othi.done(act.activation(ot[0][:, i % 2, :, w % 2, :],
                                               bank(4 + w % 2).rearrange("p (t q) -> p t q", q=S), ACT.Copy))

        def load_x1(sp, i):
            if i >= 4:
                st_out.wait(sp, i - 4)
            ld_x1.start(sp, i, x1[:, i % 4, :], x1_dram[i * P:(i + 1) * P, :])

        @on("sync")
        def _(sp):
            v_x1.wait(sp, 2 * NPAIR)
            load_x1(sp, 0)
            ld_p4.start(sp, 0, wpj_raw[:], w_proj)
            ld_p4.start(sp, 0, bexp_raw[:], w_b)
            for t in range(NJ):
                if t >= WS:
                    a_w4.wait(sp, t - WS + 1)
                    g_w4.wait(sp, t - WS + 1)
                ld_w4.start(sp, t, wstage4[:, t % WS, :], w_base[:, t, :])
                if t == WS - 1:
                    load_x1(sp, 1)
            for i in range(NPAIR + 1):
                if i >= 1:
                    v_out.wait(sp, 2 * i)
                    st_out.start(sp, i - 1, out[(i - 1) * P:i * P, :], x1[:, (i - 1) % 4, :])
                if i + 2 < NPAIR:
                    load_x1(sp, i + 2)
            for i in range(NPAIR - 4, NPAIR):
                st_out.wait(sp, i)

        def mix_channels(pe, i):
            a_x1hi.wait(pe, i + 1)
            g_x1lo.wait(pe, i + 1)
            a_mix.wait(pe, 2)
            g_mix.wait(pe, 2)
            for half in range(2):
                v_xflo.wait(pe, 2 * (i - 1) + half + 1)
                for t in range(4):
                    for a, c in PASSES:
                        at = (half * 4 + t) * P
                        mm = pe.matmul(ps[:, half, t * P:(t + 1) * P], x1s[a][:, i % 2, at:at + P], mix[c][:, i, :],
                                       start=(a + c == 0), stop=(a == 1))
                pe_mix.done(mm)

        def base(pe, i, half):
            a_xfhi.wait(pe, 2 * i + half + 1)
            v_xflo.wait(pe, 2 * i + half + 1)
            if half == 0:
                v_out.wait(pe, 2 * (i - 1))
                v_h.wait(pe, i)
            for t in range(half * 4, half * 4 + 4):
                a_w4.wait(pe, t + 1)
                g_w4.wait(pe, t + 1)
                for a, c in PASSES:
                    first, last = t == 0 and a + c == 0, t == NJ - 1 and a == 1
                    for n in range(2):
                        pe.matmul(ps[:, 2 + 2 * (i % 2) + n, :], xf[a][:, i % 2, t, :], wb[c][:, t, n * 512:(n + 1) * 512],
                                  start=first, stop=False)
                    mm = pe.matmul(ps[:, 6, 0:NPROJ], xf[a][:, i % 2, t, :], wpj[c][:, t, :], start=first, stop=last)
            if half == 1:
                pe_f.done(mm)

        def turn_h(pe, i):
            v_h.wait(pe, i + 1)
            v_htlo.wait(pe, i)
            pe_ht.done(pe.transpose(ps[0:NE * RANK, 7, 0:P], hw[:], C("ident")))

        def experts(pe, i):
            a_hthi.wait(pe, i + 1)
            v_htlo.wait(pe, i + 1)
            for n in range(2):
                for a, c in PASSES:
                    mm = pe.matmul(ps[:, 2 + 2 * (i % 2) + n, :], ht[a][:], bexp[c][:, n * 512:(n + 1) * 512],
                                   start=False, stop=(a == 1))
                pe_out.done(mm)

        @on("tensor")
        def _(pe):
            v_x1.wait(pe, 2 * NPAIR)
            mix_channels(pe, 0)
            a_p4.wait(pe, 2)
            g_p4.wait(pe, 2)
            for i in range(NPAIR + 1):
                if i < NPAIR:
                    base(pe, i, 0)
                if i >= 1:
                    turn_h(pe, i - 1)
                if i + 1 < NPAIR:
                    mix_channels(pe, i + 1)
                if i >= 1:
                    experts(pe, i - 1)
                if i < NPAIR:
                    base(pe, i, 1)

        def x1_hi(act, i):
            ld_x1.wait(act, i)
            pe_mix.wait(act, 2 * (i - 1))
            a_x1hi.done(act.activation(x1s[0][:, i % 2, :], x1[:, i % 4, :], ACT.Copy))

        def xf_hi(act, i):
            pe_f.wait(act, i - 1)
            for half in range(2):
                pe_mix.wait(act, 2 * i + half + 1)
                a_xfhi.done(act.activation(xf[0][:, i % 2, half * 4:half * 4 + 4, :],
                                           bank(half).rearrange("p (t q) -> p t q", q=P), ACT.Copy))

        @on("scalar")
        def _(act):
            x1_hi(act, 0)
            ld_p4.wait(act, 0)
            a_p4.done(act.activation(wpj[0][:], wpj_raw[:], ACT.Copy))
            a_p4.done(act.activation(bexp[0][:], bexp_raw[:], ACT.Copy))
            xf_hi(act, 0)
            for t in range(NJ):
                ld_w4.wait(act, t)
                a_w4.done(act.activation(wb[0][:, t, :], wstage4[:, t % WS, :], ACT.Copy))
            x1_hi(act, 1)
            for i in range(NPAIR + 1):
                if i >= 1:
                    v_gate.wait(act, GATE_STEPS * (i - 1) + 2)
                    a_gate.done(act.activation(gt[:, 0, :], ps[:, 6, 0:NE], ACT.Exp, bias=gs[:, 1:2],
                                               accum_out=gs[:, 2:3]))
                    pe_ht.wait(act, i)
                    pe_out.wait(act, 2 * (i - 1))
                    a_hthi.done(act.activation(ht[0][:], ps[0:NE * RANK, 7, 0:P], ACT.Copy))
                if i + 1 < NPAIR:
                    xf_hi(act, i + 1)
                if i + 2 < NPAIR:
                    x1_hi(act, i + 2)

        @on("gpsimd")
        def _(gp):
            def x1_lo(i):
                a_x1hi.wait(gp, i + 1)
                g_x1lo.done(gp.tensor_tensor(x1s[1][:, i % 2, :], x1[:, i % 4, :], x1s[0][:, i % 2, :].bitcast(F32),
                                             ALU.subtract))

            x1_lo(0)
            for n, (lo, raw, hi) in enumerate(((wpj[1], wpj_raw, wpj[0]), (bexp[1], bexp_raw, bexp[0]))):
                a_p4.wait(gp, n + 1)
                g_p4.done(gp.tensor_tensor(lo[:], raw[:], hi[:].bitcast(F32), ALU.subtract))
            for t in range(NJ):
                a_w4.wait(gp, t + 1)
                g_w4.done(gp.tensor_tensor(wb[1][:, t, :], wstage4[:, t % WS, :], wb[0][:, t, :].bitcast(F32),
                                           ALU.subtract))
            for i in range(1, NPAIR):
                x1_lo(i)

        GATE_STEPS = 11

        def gate(v, i):
            n0 = GATE_STEPS * i

            def link(k, ins):
                v_gate.done(ins)
                v_gate.wait(v, n0 + k)

            logits = ps[:, 6, 0:NE]
            pe_f.wait(v, i + 1)
            link(1, v.tensor_reduce(gs[:, 0:1], logits, AX_X, ALU.max))
            link(2, v.tensor_scalar(gs[:, 1:2], gs[:, 0:1], -1.0, None, ALU.mult))
            a_gate.wait(v, i + 1)
            link(3, v.reciprocal(gs[:, 3:4], gs[:, 2:3]))
            link(4, v.tensor_scalar(gt[:, 1, :], gt[:, 0, :], gs[:, 3:4], None, ALU.mult))
            link(5, v.max(gt[:, 2, :], gt[:, 1, :]))
            link(6, v.max_index(gi[:], gt[:, 2, :], gt[:, 1, :]))
            link(7, v.tensor_copy(gt[:, 3, :], gi[:]))
            link(8, v.tensor_tensor(gs[:, 4:5], gt[:, 2, 0:1], gt[:, 2, 1:2], ALU.add))
            v.reciprocal(gs[:, 5:6], gs[:, 4:5]).then_inc(v_gate.sem, 1)
            for k in range(2):
                ins = v.tensor_scalar(gt[:, 4 + k, :], C("iota8"), gt[:, 3, k:k + 1], gt[:, 2, k:k + 1],
                                      ALU.is_equal, ALU.mult)
            v_gate.done(ins)
            v_gate.wait(v, n0 + 10)
            link(11, v.tensor_tensor(gt[:, 6, :], gt[:, 4, :], gt[:, 5, :], ALU.add))
            v_wts.done(v.tensor_scalar(gt[:, 7, :], gt[:, 6, :], gs[:, 5:6], SCALING, ALU.mult, ALU.mult))
            v_wts.wait(v, i + 1)
            pe_ht.wait(v, i)
            v_h.done(v.tensor_tensor(hw[:].rearrange("p (e r) -> p e r", r=RANK),
                                     ps[:, 6, NE:NPROJ].rearrange("p (e r) -> p e r", r=RANK),
                                     along(gt[:, 7, :], RANK), ALU.mult))

        v_wts = step("v_wts")

        def xf_lo(v, i):
            for half in range(2):
                a_xfhi.wait(v, 2 * i + half + 1)
                dst, hi = (xf[part][:, i % 2, half * 4:half * 4 + 4, :] for part in (1, 0))
                v_xflo.done(v.tensor_tensor(dst, bank(half).rearrange("p (t q) -> p t q", q=P), hi.bitcast(F32),
                                            ALU.subtract))

        @on("vector")
        def _(v):
            xf_lo(v, 0)
            for i in range(NPAIR + 1):
                if i >= 1:
                    gate(v, i - 1)
                    a_hthi.wait(v, i)
                    v_htlo.done(v.tensor_tensor(ht[1][:], ps[0:NE * RANK, 7, 0:P], ht[0][:].bitcast(F32), ALU.subtract))
                if i + 1 < NPAIR:
                    xf_lo(v, i + 1)
                if i >= 1:
                    for n in range(2):
                        pe_out.wait(v, 2 * (i - 1) + n + 1)
                        x = x1[:, (i - 1) % 4, n * 512:(n + 1) * 512]
                        v_out.done(v.tensor_tensor(x, bank(2 + 2 * ((i - 1) % 2) + n), x, ALU.add))

        block = ctx.enter_context(nc.Block())
        for name, register in (("sync", block.sync), ("gpsimd", block.gpsimd), ("scalar", block.scalar),
                               ("vector", block.vector), ("tensor", block.tensor)):
            @register
            def _(eng, queue=queues[name]):
                for part in queue:
                    part(eng)


def _layouts(i):
    def head_rows(w, heads):
        return w.reshape(-1, HD, L)[heads].reshape(-1, L)

    def feature_major(w):
        return w.reshape(-1, NJ, P).transpose(2, 1, 0)

    x = i["x"]
    q_heads = np.array([(4 * G + g) * REP + r for G in range(NG) for r in range(REP) for g in range(4)])
    wqk = np.concatenate([i["L0_attn_Wk"], head_rows(i["L0_attn_Wq"], q_heads)])
    wo = i["L0_attn_Wo"].reshape(L, -1, HD)[:, q_heads].reshape(L, NQT, P)
    proj = np.concatenate([i["L0_ffn_gate_W"], i["L0_ffn_A"].reshape(NE * RANK, L)])
    return [
        x.reshape(NB, S, NJ, P)[..., ::-1].transpose(3, 1, 2, 0).reshape(P, S, NJ * NB),
        x.reshape(TOK, L),
        i["itok_B_8_3872"], i["itok_B_0_15"],
        i["L0_cond_log_dt"],
        i["L0_cond_C"][..., 0].T, i["L0_cond_C"][..., 1].T,
        i["L0_cond_log_A_real"].T, i["L0_cond_A_imag"].T,
        i["L0_cond_D"],
        wqk.reshape(NG + NQT, P, NJ, P).transpose(0, 3, 2, 1).reshape(NG + NQT, P, NJ * P),
        feature_major(i["L0_attn_Wv"]).reshape(P, -1),
        wo.transpose(2, 1, 0),
        i["L0_cond2_weights"],
        feature_major(i["L0_ffn_W_base"]),
        feature_major(proj),
        i["L0_ffn_B"].transpose(0, 2, 1).reshape(NE * RANK, L),
        constants(),
    ]


def kernel(**inputs):
    import concourse.bacc as bacc
    from concourse.bass_utils import run_bass_kernel_spmd

    nc = bacc.Bacc("TRN2", target_bir_lowering=False, num_devices=1)
    arrays, args = {}, []
    for n, a in enumerate(_layouts({k: np.asarray(v) for k, v in inputs.items()})):
        a = np.ascontiguousarray(a)
        arrays[f"in_{n}_dram"] = a
        args.append(nc.dram_tensor(f"in_{n}_dram", a.shape, mybir.dt.from_np(a.dtype), kind="ExternalInput").ap())
    out = nc.dram_tensor("out_dram", (TOK, L), F32, kind="ExternalOutput").ap()
    build(nc, *args, out)
    r = run_bass_kernel_spmd(nc, [arrays], core_ids=[0])
    return r.results[0]["out_dram"].reshape(NB, S, L)
```

```python
from contextlib import ExitStack

import concourse.bass as bass
import numpy as np
from concourse import mybir

F32 = mybir.dt.float32
F32R = mybir.dt.float32r
I32 = mybir.dt.int32
U32 = mybir.dt.uint32
ALU = mybir.AluOpType
ACT = mybir.ActivationFunctionType
AX_X = mybir.AxisListType.X

P = 128
NB, S, L = 32, 64, 1024
TOK = NB * S
NJ = L // P
NMODE = 64
HD, NKV, REP = 32, 8, 4
NG = NKV // 4
NQT = NG * REP
NPAIR = NB // 2
NE, RANK = 8, 8
NPROJ = NE + NE * RANK
NBASE = NPROJ + L
JOINT = [(0, 366), (366, 732), (732, NBASE)]
NCOND = 16
SCALING = 2.0
HB = 32
HGRP = 8
NHG = S // HGRP
GP = HGRP // 2
KROW = P - 1 + L
ROUND = 12582912.0
SIN_SCALE = 6.283184
TWO_PI = 2.0 * np.pi


def _short(v, bits):
    m, e = np.frexp(v)
    return float(np.ldexp(np.round(m * 2.0 ** bits), int(e) - bits))


PI_A = 6.28125
PI_B = _short(TWO_PI - PI_A, 11)
PI_C = float(TWO_PI - PI_A - PI_B)

CONSTS = {}


def _layout(*fields):
    at = 0
    for name, n in fields:
        CONSTS[name] = (at, n)
        at += n
    return at


NCONST = _layout(("ident", P), ("cos", S), ("sin", S), ("causal", S), ("pos", NJ), ("step", HB),
                 ("off", 3), ("off_rad", 3), ("half_pi", 1), ("chan", 1), ("iota8", NE))


def constants():
    t = np.zeros((P, NCONST), np.float32)

    def put(name, v):
        at, n = CONSTS[name]
        t[:, at:at + n] = v

    p = np.arange(P)
    put("ident", np.eye(P))
    inv_freq = (1.0 / np.float32(10000.0) ** (np.arange(0, HD, 2, dtype=np.float32) / HD)).astype(np.float32)
    freqs = np.outer(np.arange(S, dtype=np.float32), inv_freq).astype(np.float32)
    emb = np.concatenate([freqs, freqs], axis=-1)
    put("cos", np.cos(emb.astype(np.float64)).T[p % HD])
    sign = np.where(p % HD < HD // 2, -1.0, 1.0)[:, None]
    put("sin", sign * np.sin(emb.astype(np.float64)).T[p % HD])
    k, q = np.arange(S)[None, :], (p % S)[:, None]
    put("causal", np.where(q < k, np.finfo(np.float32).min, np.float32(0)))
    put("pos", p[:, None] + P * np.arange(NJ)[None, :])
    put("step", np.arange(HB)[None, :])
    im = (p >= NMODE)[:, None]
    off = np.concatenate([np.where(im, 0.5, 0.25), np.where(im, 0.25, 0.0), np.where(im, 0.0, 0.25)], axis=1)
    put("off", off)
    put("off_rad", off * SIN_SCALE)
    put("half_pi", np.pi / 2)
    put("chan", (p % S)[:, None])
    put("iota8", np.arange(NE)[None, :])
    return t


class Step:

    def __init__(self, ctx, nc, name):
        self.sem = ctx.enter_context(nc.semaphore(name))

    def done(self, ins):
        ins.then_inc(self.sem, 1)

    def wait(self, eng, n):
        if n > 0:
            eng.wait_ge(self.sem, n)


class Loads:

    def __init__(self, ctx, nc, name, ring, parts=1):
        self.sems = [ctx.enter_context(nc.semaphore(f"{name}{i}")) for i in range(ring)]
        self.ring, self.parts = ring, parts

    def start(self, eng, use, dst, src):
        if dst.dtype == F32R:
            dst = dst.bitcast(F32)
        if src.dtype == F32R:
            src = src.bitcast(F32)
        eng.dma_start(dst, src).then_inc(self.sems[use % self.ring], 16)

    def wait(self, eng, use):
        eng.wait_ge(self.sems[use % self.ring], 16 * self.parts * (use // self.ring + 1))


def across(ap, n):
    return ap.unsqueeze(1).to_broadcast([ap.shape[0], n, ap.shape[1]])


def along(ap, n):
    return ap.unsqueeze(2).to_broadcast([ap.shape[0], ap.shape[1], n])


def build(nc, x_conv, x_nat, lens, cond, modes, d_skip,
          w_qk, w_v, w_o, w_cond, w_base, w_proj, w_b, consts, out):
    ctx = ExitStack()
    with ctx:
        def sb(name, shape, dt=F32, stack=ctx):
            return stack.enter_context(nc.sbuf_tensor(name, shape, dt))

        def step(name):
            return Step(ctx, nc, name)

        def loads(name, ring=1, parts=1):
            return Loads(ctx, nc, name, ring, parts)

        kpad = nc.dram_tensor("kpad", [S, KROW + 1], F32, kind="Internal")
        k_dram = [nc.dram_tensor(f"k_{n}", [NG, P, TOK], F32, kind="Internal").ap() for n in ("hi", "lo")]
        q_dram = [nc.dram_tensor(f"q_{n}", [NB, P, NQT, S], F32, kind="Internal").ap() for n in ("hi", "lo")]
        v_dram = [nc.dram_tensor(f"v_{n}", [TOK, NKV * HD], F32, kind="Internal").ap() for n in ("hi", "lo")]
        x1_dram = nc.dram_tensor("x1_scratch", [TOK, L], F32, kind="Internal").ap()

        ps = ctx.enter_context(nc.psum_tensor("ps", [P, 8, 512], F32))

        cst = sb("cst", [P, NCONST])

        def C(name):
            at, n = CONSTS[name]
            return cst[:, at:at + n]

        s12 = ExitStack()
        y = [sb(f"y_{n}", [P, NJ, NB, S], F32R, s12) for n in ("hi", "lo")]
        WR = 3
        wraw = sb("wraw", [P, WR, NJ * P], F32, s12)
        wsp = [sb(f"w12_{n}", [P, WR, NJ * P], F32R, s12) for n in ("hi", "lo")]

        s1 = ExitStack()
        TR = 3
        toep = sb("toep", [P, TR, L], F32, s1)
        XH, XR = 2, 4
        xc = sb("xc", [P, XR, XH, NJ * NB], F32, s1)
        ym = sb("ym", [P, 2, 2, NJ * NB], F32, s1)
        valid = sb("valid", [P, NJ, NB], F32, s1)
        len_i = sb("len_i", [P, NB], I32, s1)
        len_f = sb("len_f", [P, NB], F32, s1)
        prm = sb("prm", [P, 5, S], F32, s1)
        t64 = sb("t64", [P, 24, S], F32, s1)
        d_row = sb("d_row", [1, S], F32, s1)
        zeros = sb("zeros", [S, P - 1], F32, s1)
        GC = HGRP * HB
        ph = sb("ph", [P, 2, GC], F32, s1)
        mg = sb("mg", [P, 2, GC], F32, s1)
        rn = sb("rn", [P, 3, GC], F32, s1)
        ltab, rtab = ph[:, 0, :], ph[:, 1, :]
        ksb = sb("ksb", [HB, 2, GC], F32, s1)
        s1.close()

        s2 = ExitStack()
        RR = 2
        rot = sb("rot", [P, RR, 512], F32, s2)
        rc = sb("rc", [P, RR, 512], F32, s2)
        rf = sb("rf", [P, RR, 512], F32, s2)
        SR = 3
        stg = [sb(f"stg_{n}", [P, SR, 512], F32R, s2) for n in ("hi", "lo")]
        s2.close()
        s12.close()

        s3 = ExitStack()
        wo = [sb(f"wo_{n}", [P, NQT, L], F32R, s3) for n in ("hi", "lo")]
        WS3 = 4
        wstage3 = sb("wstage3", [P, WS3, L], F32, s3)
        ot = [sb(f"ot_{n}", [P, 2, NQT, 2, S], F32R, s3) for n in ("hi", "lo")]
        xr = sb("xr", [P, 3, L], F32, s3)
        k_bd = [sb(f"kbd_{n}", [P, 2, 2, NG, 4 * S], F32R, s3) for n in ("hi", "lo")]
        craw = sb("craw", [P, NPAIR, S], F32, s3)
        q_sb = [sb(f"qs_{n}", [P, 2, 2, NQT, S], F32R, s3) for n in ("hi", "lo")]
        v_bd = [sb(f"vbd_{n}", [P, 2, 2, NG, 2, P], F32R, s3) for n in ("hi", "lo")]
        sc = sb("sc", [P, 2, 1024], F32, s3)
        pt = [sb(f"pt_{n}", [P, 1024], F32R, s3) for n in ("hi", "lo")]
        mix = [sb(f"mix_{n}", [P, NPAIR, P], F32R, s3) for n in ("hi", "lo")]
        stat = sb("stat", [P, 2, 3, 16], F32, s3)
        cidx_i = sb("cidx_i", [P, NB], I32, s3)
        cidx = sb("cidx", [P, NPAIR], U32, s3)
        kc = sb("kc", [P, 2, 2, NG, P], F32R, s3)
        vc = sb("vc", [P, 2, 2, 2, NKV * HD], F32R, s3)
        s3.close()

        s4 = ExitStack()
        wb = [sb(f"wb_{n}", [P, NJ, L], F32R, s4) for n in ("hi", "lo")]
        wpj = [sb(f"wpj_{n}", [P, NJ, NPROJ], F32R, s4) for n in ("hi", "lo")]
        wpj_raw = sb("wpj_raw", [P, NJ, NPROJ], F32, s4)
        x1 = sb("x1", [P, 4, L], F32, s4)
        WS4 = 2
        wstage4 = sb("wstage4", [P, WS4, L], F32, s4)
        x1s = [sb(f"x1s_{n}", [P, 2, L], F32R, s4) for n in ("hi", "lo")]
        xf = [sb(f"xf_{n}", [P, 2, NJ, P], F32R, s4) for n in ("hi", "lo")]
        bexp = [sb(f"bexp_{n}", [NE * RANK, L], F32R, s4) for n in ("hi", "lo")]
        bexp_raw = sb("bexp_raw", [NE * RANK, L], F32, s4)
        gt = sb("gt", [P, 8, NE], F32, s4)
        gi = sb("gi", [P, NE], U32, s4)
        gs = sb("gs", [P, 8], F32, s4)
        hw = sb("hw", [P, NE * RANK], F32, s4)
        ht = [sb(f"ht_{n}", [NE * RANK, P], F32R, s4) for n in ("hi", "lo")]
        s4.close()

        ld_cst, ld_prm, ld_len, ld_d = loads("ld_cst"), loads("ld_prm", 1, 2), loads("ld_len"), loads("ld_d")
        ld_cond, ld_cmix = loads("ld_cond"), loads("ld_cmix", 1, NPAIR)
        st_zero, st_k = loads("st_zero"), loads("st_k", 2)
        ld_toep, ld_xc = loads("ld_toep", TR), loads("ld_xc", XR)
        ld_w = [ctx.enter_context(nc.semaphore(f"ld_w{i}")) for i in range(WR)]
        st_stg = loads("st_stg", SR, 2)
        ld_w3, ld_q, ld_k, ld_v, ld_x = (loads("ld_w3", WS3), loads("ld_q", 2, 2), loads("ld_k", 2, 2),
                                         loads("ld_v", 2, 4), loads("ld_x", 3))
        st_x1 = loads("st_x1", 3)
        ld_w4, ld_p4, ld_x1, st_out = loads("ld_w4", WS4), loads("ld_p4", 1, 2), loads("ld_x1", 4), loads("st_out", 4)
        a_set, v_set, v_rho, v_ang, v_cs = map(step, ("a_set", "v_set", "v_rho", "v_ang", "v_cs"))
        g_zero, v_cidx, v_len, v_valid = map(step, ("g_zero", "v_cidx", "v_len", "v_valid"))
        g_mag, a_mag, v_ph, v_round, a_sin, v_tab = map(step, ("g_mag", "a_mag", "v_ph", "v_round", "a_sin", "v_tab"))
        pe_k, v_ke, v_k = map(step, ("pe_k", "v_ke", "v_k"))
        pe_conv, v_mask, a_yhi, g_ylo = map(step, ("pe_conv", "v_mask", "a_yhi", "g_ylo"))
        a_mix, g_mix = map(step, ("a_mix", "g_mix"))
        a_whi, g_wlo, pe_unit = map(step, ("a_whi", "g_wlo", "pe_unit"))
        pe_v, a_vhi, v_vlo = map(step, ("pe_v", "a_vhi", "v_vlo"))
        pe_m, v_rot, v_rcos, g_rsin, g_rsum, a_rhi, v_rlo = map(
            step, ("pe_m", "v_rot", "v_rcos", "g_rsin", "g_rsum", "a_rhi", "v_rlo"))
        v_zero3, g_zero3, a_w3, v_w3 = map(step, ("v_zero3", "g_zero3", "a_w3", "v_w3"))
        a_kbd, a_vbd = step("a_kbd"), step("a_vbd")
        pe_s, v_sc, v_max, g_sub, a_exp, v_sum, v_rec, g_prob = map(
            step, ("pe_s", "v_sc", "v_max", "g_sub", "a_exp", "v_sum", "v_rec", "g_prob"))
        pe_t, a_pthi, v_ptlo, pe_o, a_othi, v_otlo, pe_y, v_x1 = map(
            step, ("pe_t", "a_pthi", "v_ptlo", "pe_o", "a_othi", "v_otlo", "pe_y", "v_x1"))
        a_p4, g_p4, a_w4, v_w4 = map(step, ("a_p4", "g_p4", "a_w4", "v_w4"))
        a_x1hi, g_x1lo, pe_mix, a_xfhi, v_xflo = map(step, ("a_x1hi", "g_x1lo", "pe_mix", "a_xfhi", "v_xflo"))
        pe_f, v_gate, a_gate, v_h, pe_ht, a_hthi, v_htlo, pe_out, v_out = map(
            step, ("pe_f", "v_gate", "a_gate", "v_h", "pe_ht", "a_hthi", "v_htlo", "pe_out", "v_out"))

        queues = {"sync": [], "gpsimd": [], "scalar": [], "vector": [], "tensor": []}

        def on(engine):
            return queues[engine].append

        def bank(n):
            return ps[:, n, :]

        PASSES = ((0, 0), (0, 1), (1, 0))

        names64 = ("dt", "ar", "rho", "rho32", "th", "k", "r", "vr", "v32", "e1", "tanh", "sh", "ch",
                   "cm1", "nr", "ni", "den", "t0", "t1", "t2", "gr", "gi", "cr", "ci")

        def M(name):
            return t64[:, names64.index(name), :]

        LOGDT, LOGA, AIM, CRE, CIM = (prm[:, i, :] for i in range(5))

        @on("sync")
        def _(sp):
            for half in (slice(0, NMODE), slice(NMODE, P)):
                ld_prm.start(sp, 0, prm[half, :, :], modes)
            ld_cst.start(sp, 0, cst[:], consts)
            ld_d.start(sp, 0, d_row[:], d_skip.rearrange("(a h) -> a h", a=1))
            ld_len.start(sp, 0, len_i[:], lens.partition_broadcast(P))
            g_zero.wait(sp, 1)
            st_zero.start(sp, 0, kpad.ap()[:, 0:P - 1], zeros[:])

        @on("scalar")
        def _(act):
            ld_prm.wait(act, 0)
            a_set.done(act.activation(M("dt"), LOGDT, ACT.Exp))
            a_set.done(act.activation(M("ar"), LOGA, ACT.Exp))
            v_rho.wait(act, 1)
            a_set.done(act.activation(M("e1"), M("rho"), ACT.Exp))
            a_set.done(act.activation(M("tanh"), M("rho"), ACT.Tanh, scale=0.5))

        def magnitudes(act, g):
            for i in range(2):
                g_mag.wait(act, 2 * g + i + 1)
                a_mag.done(act.activation(mg[:, i, :], mg[:, i, :], ACT.Exp))

        def sines(act, g):
            v_round.wait(act, 3 * (g + 1))
            for i in range(3):
                a_sin.done(act.activation(rn[:, i, :], rn[:, i, :], ACT.Sin, scale=-SIN_SCALE,
                                          bias=C("off_rad")[:, i:i + 1]))

        @on("scalar")
        def _(act):
            magnitudes(act, 0)
            v_ang.wait(act, 1)
            ld_cst.wait(act, 0)
            a_set.done(act.activation(M("sh"), M("r"), ACT.Sin, scale=0.5))
            a_set.done(act.activation(M("ch"), M("r"), ACT.Sin, scale=0.4999998, bias=C("half_pi")))
            sines(act, 0)

        def exponents(gp, g):
            v_tab.wait(gp, 2 * g)
            hs = slice(g * HGRP, (g + 1) * HGRP)
            for i, r in enumerate(("rho32", "rho")):
                g_mag.done(gp.tensor_tensor(mg[:, i, :].rearrange("p (h s) -> p h s", s=HB), along(M(r)[:, hs], HB),
                                            across(C("step"), HGRP), ALU.mult))

        @on("gpsimd")
        def _(gp):
            g_zero.done(gp.memset(zeros[:], 0.0))
            ld_cst.wait(gp, 0)
            v_rho.wait(gp, 1)
            exponents(gp, 0)

        def chain(v, ins):
            v_set.done(ins)
            chain.n += 1
            v_set.wait(v, chain.n)

        chain.n = 0

        @on("vector")
        def _(v):
            a_set.wait(v, 2)
            chain(v, v.tensor_scalar(M("ar"), M("ar"), -1.0, None, ALU.mult))
            chain(v, v.tensor_tensor(M("rho"), M("ar"), M("dt"), ALU.mult))
            v_rho.done(v.tensor_scalar(M("rho32"), M("rho"), float(HB), None, ALU.mult))
            chain(v, v.tensor_tensor(M("th"), AIM, M("dt"), ALU.mult))
            chain(v, v.tensor_scalar(M("k"), M("th"), 1.0 / TWO_PI, ROUND, ALU.mult, ALU.add))
            chain(v, v.tensor_scalar(M("k"), M("k"), ROUND, None, ALU.subtract))
            chain(v, v.scalar_tensor_tensor(M("t0"), M("k"), -PI_A, M("th"), ALU.mult, ALU.add))
            chain(v, v.scalar_tensor_tensor(M("t1"), M("k"), -PI_B, M("t0"), ALU.mult, ALU.add))
            chain(v, v.scalar_tensor_tensor(M("r"), M("k"), -PI_C, M("t1"), ALU.mult, ALU.add))
            chain(v, v.tensor_scalar(M("vr"), M("r"), 1.0 / TWO_PI, None, ALU.mult))
            chain(v, v.tensor_scalar(M("t0"), M("vr"), float(HB), ROUND, ALU.mult, ALU.add))
            chain(v, v.tensor_scalar(M("t1"), M("t0"), ROUND, None, ALU.subtract))
            v_ang.done(v.scalar_tensor_tensor(M("v32"), M("vr"), float(HB), M("t1"), ALU.mult, ALU.subtract))
            v_ang.wait(v, 1)

        def phases(v, g):
            hs = slice(g * HGRP, (g + 1) * HGRP)
            for i, r in enumerate(("v32", "vr")):
                v_ph.done(v.tensor_tensor(ph[:, i, :].rearrange("p (h s) -> p h s", s=HB), along(M(r)[:, hs], HB),
                                          across(C("step"), HGRP), ALU.mult))
            v_ph.wait(v, 5 * g + 2)
            for i, part in enumerate((0, 0, 1)):
                v_ph.done(v.tensor_scalar(rn[:, i, :], ph[:, part, :], C("off")[:, i:i + 1], ROUND, ALU.add, ALU.add))
            v_ph.wait(v, 5 * g + 5)
            for i, part in enumerate((0, 0, 1)):
                v_round.done(v.scalar_tensor_tensor(rn[:, i, :], rn[:, i, :], ROUND, ph[:, part, :],
                                                    ALU.subtract, ALU.subtract))

        @on("vector")
        def _(v):
            ld_cst.wait(v, 0)
            phases(v, 0)
            a_set.wait(v, 6)
            v.scalar_tensor_tensor(M("tanh"), M("e1"), 1.0, M("tanh"), ALU.add, ALU.mult)
            v.scalar_tensor_tensor(M("cm1"), M("sh"), -2.0, M("sh"), ALU.mult, ALU.mult)
            v.scalar_tensor_tensor(M("t1"), M("sh"), 2.0, M("ch"), ALU.mult, ALU.mult)
            v.tensor_tensor(M("k"), M("ar"), M("ar"), ALU.mult)
            chain(v, v.tensor_tensor(M("t2"), AIM, AIM, ALU.mult))
            v.scalar_tensor_tensor(M("t0"), M("cm1"), 1.0, M("tanh"), ALU.add, ALU.mult)
            v.tensor_tensor(M("ni"), M("t1"), M("e1"), ALU.mult)
            chain(v, v.tensor_tensor(M("k"), M("k"), M("t2"), ALU.add))
            v.tensor_tensor(M("nr"), M("t0"), M("cm1"), ALU.add)
            chain(v, v.reciprocal(M("den"), M("k")))
            v.tensor_tensor(M("t0"), M("nr"), M("ar"), ALU.mult)
            v.tensor_tensor(M("t1"), M("ni"), AIM, ALU.mult)
            v.tensor_tensor(M("t2"), M("ni"), M("ar"), ALU.mult)
            chain(v, v.tensor_tensor(M("k"), M("nr"), AIM, ALU.mult))
            v.tensor_tensor(M("gr"), M("t0"), M("t1"), ALU.add)
            chain(v, v.tensor_tensor(M("gi"), M("t2"), M("k"), ALU.subtract))
            v.tensor_tensor(M("gr"), M("gr"), M("den"), ALU.mult)
            chain(v, v.tensor_tensor(M("gi"), M("gi"), M("den"), ALU.mult))
            v.scalar_tensor_tensor(M("t0"), M("gr"), 2.0, CRE, ALU.mult, ALU.mult)
            v.scalar_tensor_tensor(M("t1"), M("gi"), 2.0, CIM, ALU.mult, ALU.mult)
            v.scalar_tensor_tensor(M("t2"), M("gi"), 2.0, CRE, ALU.mult, ALU.mult)
            chain(v, v.scalar_tensor_tensor(M("k"), M("gr"), 2.0, CIM, ALU.mult, ALU.mult))
            v.tensor_tensor(M("cr"), M("t0"), M("t1"), ALU.subtract)
            chain(v, v.tensor_tensor(M("ci"), M("t2"), M("k"), ALU.add))

        def tables(v, g):
            hs = slice(g * HGRP, (g + 1) * HGRP)
            a_sin.wait(v, 3 * (g + 1))
            for i, c in enumerate(("cr", "ci")):
                w = rn[:, i, :].rearrange("p (h s) -> p h s", s=HB)
                chain(v, v.tensor_tensor(w, w, along(M(c)[:, hs], HB), ALU.mult))
            chain(v, v.tensor_tensor(rn[:, 0, :], rn[:, 0, :], rn[:, 1, :], ALU.subtract))
            a_mag.wait(v, 2 * (g + 1))
            pe_k.wait(v, g)
            v_tab.done(v.tensor_tensor(ltab, rn[:, 0, :], mg[:, 0, :], ALU.mult))
            v_tab.done(v.tensor_tensor(rtab, rn[:, 2, :], mg[:, 1, :], ALU.mult))

        def kernels_pe(pe, g):
            v_tab.wait(pe, 2 * (g + 1))
            v_ke.wait(pe, g - 1)
            for h in range(HGRP):
                cols = slice(h * HB, (h + 1) * HB)
                mm = pe.matmul(ps[0:HB, 4 + g % 2, cols], ltab[:, cols], rtab[:, cols], start=True, stop=True)
            pe_k.done(mm)

        def kernels_out(v, g):
            pe_k.wait(v, g + 1)
            if g >= 2:
                st_k.wait(v, g - 2)
            v_ke.done(v.tensor_copy(ksb[:, g % 2, :], ps[0:HB, 4 + g % 2, 0:GC]))
            v_ke.wait(v, g + 1)
            k0 = ksb[0:1, g % 2, :].rearrange("p (h s) -> p h s", s=HB)[:, :, 0]
            v_k.done(v.tensor_tensor(k0, k0, d_row[:, g * HGRP:(g + 1) * HGRP], ALU.add))

        def store_kernels(sp, g):
            v_k.wait(sp, g + 1)
            st_k.start(sp, g, kpad.ap()[g * HGRP:(g + 1) * HGRP, P - 1:P - 1 + L].rearrange("h (a b) -> a h b", b=HB),
                       ksb[:, g % 2, :].rearrange("a (h b) -> a h b", b=HB))

        def load_x_conv(sp, t):
            if t >= XR:
                pe_conv.wait(sp, (t - XR + 1) * XH)
            ld_xc.start(sp, t, xc[:, t % XR, :, :], x_conv[:, t * XH:(t + 1) * XH, :])

        @on("sync")
        def _(sp):
            for t in range(XR):
                load_x_conv(sp, t)
            sp.dma_start(wraw[:, 0:2, :].rearrange("p a n -> p (a n)"), w_v).then_inc(ld_w[0], 16)
            sp.dma_start(wraw[:, 2, :], w_qk[0]).then_inc(ld_w[2], 16)
            store_kernels(sp, 0)
            st_zero.wait(sp, 0)
            for h in range(S):
                g = h // HGRP
                if h % HGRP == 0:
                    st_k.wait(sp, g)
                if h % HGRP == 6 and g + 1 < NHG:
                    store_kernels(sp, g + 1)
                if h >= TR:
                    pe_conv.wait(sp, h - TR + 1)
                ld_toep.start(sp, h, toep[:, h % TR, :], bass.AP(kpad, h * (KROW + 1), [[1, P], [1, L]]))
                done = h - TR + 1
                if done > 0 and done % XH == 0 and done // XH + XR - 1 < S // XH:
                    load_x_conv(sp, done // XH + XR - 1)

        def convolve(pe, h):
            n, i = h // 2, h % 2
            if h % XH == 0:
                ld_xc.wait(pe, h // XH)
            if i == 0:
                v_mask.wait(pe, n - 3)
            ld_toep.wait(pe, h)
            for d in range(NJ):
                mm = pe.matmul(ps[:, n % 4, i * 256 + d * NB:(i + 1) * 256], toep[:, h % TR, d * P:(d + 1) * P],
                               xc[:, (h // XH) % XR, h % XH, 0:(NJ - d) * NB], start=(d == 0), stop=(d == NJ - 1))
            pe_conv.done(mm)

        @on("tensor")
        def _(pe):
            kernels_pe(pe, 0)
            for h in range(S):
                convolve(pe, h)
                if h % HGRP == 3 and h // HGRP + 1 < NHG:
                    kernels_pe(pe, h // HGRP + 1)

        @on("vector")
        def _(v):
            ld_len.wait(v, 0)
            v_len.done(v.tensor_copy(len_f[:], len_i[:]))
            v_len.wait(v, 1)
            v_valid.done(v.tensor_tensor(valid[:], across(len_f[:], NJ), along(C("pos"), NB), ALU.is_gt))
            tables(v, 0)
            ld_d.wait(v, 0)
            kernels_out(v, 0)
            v_valid.wait(v, 1)
            phases(v, 1)
            for n in range(S // 2):
                g, k = n // GP, n % GP
                if k == 0 and g + 1 < NHG:
                    tables(v, g + 1)
                pe_conv.wait(v, 2 * n + 2)
                a_yhi.wait(v, n - 1)
                g_ylo.wait(v, n - 1)
                v_mask.done(v.tensor_tensor(ym[:, n % 2, :, :], bank(n % 4).rearrange("p (i c) -> p i c", i=2),
                                            across(valid[:].rearrange("p j b -> p (j b)"), 2), ALU.mult))
                if k == 1 and g + 1 < NHG:
                    kernels_out(v, g + 1)
                if k == 2 and g + 2 < NHG:
                    phases(v, g + 2)

        def y_pair(part, n, i):
            return y[part][:, :, :, 2 * n + i]

        def ym_pair(n, i):
            return ym[:, n % 2, i, :].rearrange("p (j b) -> p j b", b=NB)

        @on("scalar")
        def _(act):
            weight_hi(act, -1)
            weight_hi(act, 0)
            magnitudes(act, 1)
            sines(act, 1)
            for n in range(S // 2):
                g = n // GP
                if n % GP == 3 and g + 2 < NHG:
                    magnitudes(act, g + 2)
                    sines(act, g + 2)
                v_mask.wait(act, n + 1)
                act.activation(y_pair(0, n, 0), ym_pair(n, 0), ACT.Copy)
                a_yhi.done(act.activation(y_pair(0, n, 1), ym_pair(n, 1), ACT.Copy))

        @on("gpsimd")
        def _(gp):
            weight_lo(gp, -1)
            weight_lo(gp, 0)
            exponents(gp, 1)
            for n in range(S // 2):
                g = n // GP
                if n % GP == 2 and g + 2 < NHG:
                    exponents(gp, g + 2)
                a_yhi.wait(gp, n + 1)
                gp.tensor_tensor(y_pair(1, n, 0), ym_pair(n, 0), y_pair(0, n, 0).bitcast(F32), ALU.subtract)
                g_ylo.done(gp.tensor_tensor(y_pair(1, n, 1), ym_pair(n, 1), y_pair(0, n, 1).bitcast(F32), ALU.subtract))

        NU = NG + NQT

        def w_slot(m):
            return slice(0, 2) if m < 0 else slice((m + 2) % WR, (m + 2) % WR + 1)

        def w_loaded(eng, m):
            s = w_slot(m).start
            eng.wait_ge(ld_w[s], 16 * (1 if m < 0 else (m - 1) // WR + 2 if s == 0 else m // WR + 1))

        def w_users(m):
            return 0 if m <= 0 else 1 if m < WR else m - WR + 2

        def load_weights(sp, m):
            a_whi.wait(sp, w_users(m))
            g_wlo.wait(sp, w_users(m))
            s = w_slot(m).start
            sp.dma_start(wraw[:, s, :], w_qk[m]).then_inc(ld_w[s], 16)

        def weight_hi(act, m):
            w_loaded(act, m)
            pe_unit.wait(act, w_users(m))
            a_whi.done(act.activation(wsp[0][:, w_slot(m), :], wraw[:, w_slot(m), :], ACT.Copy))

        def weight_lo(gp, m):
            a_whi.wait(gp, m + 2)
            g_wlo.done(gp.tensor_tensor(wsp[1][:, w_slot(m), :], wraw[:, w_slot(m), :],
                                        wsp[0][:, w_slot(m), :].bitcast(F32), ALU.subtract))

        NVB = TOK // P // 2

        @on("sync")
        def _(sp):
            load_weights(sp, 1)
            load_weights(sp, 2)
            for n in range(NVB):
                a_vhi.wait(sp, n + 1)
                v_vlo.wait(sp, n + 1)
                for part in range(2):
                    dst = v_dram[part][2 * n * P:(2 * n + 2) * P, :].rearrange("(t p) d -> p t d", p=P)
                    st_stg.start(sp, n, dst, stg[part][:, n % SR, :].rearrange("p (t d) -> p t d", t=2))
            for m in range(NU):
                if m + WR < NU:
                    load_weights(sp, m + WR)
                if m == NG + 1:
                    for n in range(NVB + 4 * NG, NVB + 4 * NG + SR):
                        st_stg.wait(sp, n)
                    load_kv(sp, 0)
                    load_kv(sp, 1)
                for g in range(4):
                    n = NVB + 4 * m + g
                    if m == NU - 1 and g == 3:
                        pe_unit.wait(sp, NU + 1)
                        for t in range(WS3):
                            load_w3(sp, t)
                    a_rhi.wait(sp, 4 * m + g + 1)
                    v_rlo.wait(sp, 4 * m + g + 1)
                    for part in range(2):
                        src = stg[part][:, n % SR, :]
                        if m < NG:
                            st_stg.start(sp, n, k_dram[part][m, :, g * 512:(g + 1) * 512], src)
                        else:
                            st_stg.start(sp, n, q_dram[part][8 * g:8 * g + 8, :, m - NG, :].rearrange("b p s -> p b s"),
                                         src.rearrange("p (b s) -> p b s", s=S))
                    if m == NU - 1 and g == 0:
                        for last in range(n - SR + 1, n + 1):
                            st_stg.wait(sp, last)
                        a_whi.wait(sp, NU + 1)
                        g_wlo.wait(sp, NU + 1)
                        pe_unit.wait(sp, NU - 1)
                        load_q(sp, 0)
                        load_q(sp, 1)
            for n in range(NVB + 4 * NU - SR, NVB + 4 * NU):
                st_stg.wait(sp, n)

        @on("tensor")
        def _(pe):
            yt = [p.rearrange("p j b s -> p j (b s)") for p in (y[0][:], y[1][:])]
            wv = [w[:, 0:2, :].rearrange("p a n -> p (a n)").rearrange("p (j d) -> p j d", j=NJ) for w in wsp]
            v_mask.wait(pe, S // 2)
            v_ke.wait(pe, NHG)
            a_yhi.wait(pe, S // 2)
            g_ylo.wait(pe, S // 2)
            a_whi.wait(pe, 1)
            g_wlo.wait(pe, 1)
            for n in range(NVB):
                for t in range(2):
                    tok = slice((2 * n + t) * P, (2 * n + t + 1) * P)
                    for j in range(NJ):
                        for a, b in PASSES:
                            mm = pe.matmul(ps[:, n, t * 256:(t + 1) * 256], yt[a][:, j, tok], wv[b][:, j, :],
                                           start=(j == 0 and a + b == 0), stop=(j == NJ - 1 and a == 1))
                pe_v.done(mm) if n < NVB - 1 else pe_unit.done(mm)
            for m in range(NU):
                a_whi.wait(pe, m + 2)
                g_wlo.wait(pe, m + 2)
                w = [x[:, w_slot(m).start, :].rearrange("p (j d) -> p j d", j=NJ) for x in wsp]
                for g in range(4):
                    if m < 2:
                        v_vlo.wait(pe, 4 * m + g + 1)
                    else:
                        v_rcos.wait(pe, 4 * (m - 2) + g + 1)
                    for j in range(NJ):
                        for a, b in PASSES:
                            mm = pe.matmul(ps[:, 4 * (m % 2) + g, :], w[a][:, j, :], yt[b][:, j, g * 512:(g + 1) * 512],
                                           start=(j == 0 and a + b == 0), stop=(j == NJ - 1 and a == 1))
                    pe_m.done(mm) if g < 3 else pe_unit.done(mm)

        def v_ready(eng, n):
            if n < NVB - 1:
                pe_v.wait(eng, n + 1)
            else:
                pe_unit.wait(eng, 1)

        def m_ready(eng, m, g):
            if g < 3:
                pe_m.wait(eng, 3 * m + g + 1)
            else:
                pe_unit.wait(eng, m + 2)

        def staging_free(eng, n):
            if n >= SR:
                st_stg.wait(eng, n - SR)

        @on("scalar")
        def _(act):
            g_ylo.wait(act, S // 2)
            for n in range(NVB):
                v_ready(act, n)
                staging_free(act, n)
                a_vhi.done(act.activation(stg[0][:, n % SR, :], bank(n), ACT.Copy))
            for m in range(NU):
                if m < NU - 1:
                    weight_hi(act, m + 1)
                for g in range(4):
                    n = 4 * m + g
                    g_rsum.wait(act, n + 1)
                    staging_free(act, NVB + n)
                    a_rhi.done(act.activation(stg[0][:, (NVB + n) % SR, :], rf[:, n % RR, :], ACT.Copy))

        @on("vector")
        def _(v):
            for n in range(NVB):
                a_vhi.wait(v, n + 1)
                v_vlo.done(v.tensor_tensor(stg[1][:, n % SR, :], bank(n), stg[0][:, n % SR, :].bitcast(F32),
                                           ALU.subtract))
            swap = [(i + HD // 2) % HD for i in range(HD)]

            def rope_lo(n):
                s = (NVB + n) % SR
                a_rhi.wait(v, n + 1)
                v_rlo.done(v.tensor_tensor(stg[1][:, s, :], rf[:, n % RR, :], stg[0][:, s, :].bitcast(F32), ALU.subtract))

            for n in range(4 * NU):
                m, g = n // 4, n % 4
                m_ready(v, m, g)
                g_rsum.wait(v, n + 1 - RR)
                acc = bank(4 * (m % 2) + g)
                v_rot.done(v.stream_shuffle(rot[:, n % RR, :], acc, swap))
                v_rcos.done(v.tensor_tensor(rc[:, n % RR, :].rearrange("p (b s) -> p b s", s=S),
                                            acc.rearrange("p (b s) -> p b s", s=S), across(C("cos"), 8), ALU.mult))
                if n >= 1:
                    rope_lo(n - 1)
            for slot in range(2):
                if slot == 1:
                    rope_lo(4 * NU - 1)
                for part in range(2):
                    v_zero3.done(v.memset(k_bd[part][:, slot, :, :, :].bitcast(F32), 0.0))

        @on("gpsimd")
        def _(gp):
            for m in range(NU):
                if m < NU - 1:
                    weight_lo(gp, m + 1)
                for g in range(4):
                    n = 4 * m + g
                    v_rot.wait(gp, n + 1)
                    r = rot[:, n % RR, :].rearrange("p (b s) -> p b s", s=S)
                    g_rsin.done(gp.tensor_tensor(r, r, across(C("sin"), 8), ALU.mult))
                    g_rsin.wait(gp, n + 1)
                    v_rcos.wait(gp, n + 1)
                    v_rlo.wait(gp, n + 1 - RR)
                    g_rsum.done(gp.tensor_tensor(rf[:, n % RR, :], rot[:, n % RR, :], rc[:, n % RR, :], ALU.add))

        NUNIT = 2 * NPAIR
        HALF_SLOTS = range(-2, NUNIT + 2)
        INV_SQRT = 1.0 / float(np.sqrt(HD))
        WO_TILES = {-1: (0, 1), 0: (2, 3), 1: (4, 5, 6, 7)}

        def load_kv(sp, i):
            a_kbd.wait(sp, 8 * (i - 1))
            a_vbd.wait(sp, 4 * (i - 1))
            for part in range(2):
                ld_k.start(sp, i, kc[:, i % 2, part, :, :],
                           k_dram[part][:, :, i * P:(i + 1) * P].rearrange("t p k -> p t k"))
            for part in range(2):
                for x in range(2):
                    ld_v.start(sp, i, vc[x * S:(x + 1) * S, i % 2, part, :, :],
                               v_dram[part][i * P:(i + 1) * P, :].rearrange("(b k) c -> k b c", b=2))

        def load_q(sp, i):
            pe_s.wait(sp, 2 * (i - 2) + 2)
            for part in range(2):
                ld_q.start(sp, i, q_sb[part][:, i % 2, :, :, :], q_dram[part][2 * i:2 * i + 2].rearrange("b p t s -> p b t s"))

        def load_w3(sp, t):
            a_w3.wait(sp, t - WS3 + 1)
            v_w3.wait(sp, t - WS3 + 1)
            ld_w3.start(sp, t, wstage3[:, t % WS3, :], w_o[:, t, :])

        def place_k(act, i):
            v_zero3.wait(act, 2 * min(i + 1, 2))
            ld_k.wait(act, i)
            if i >= 2:
                pe_s.wait(act, 2 * (i - 2) + 2)
            for part in range(2):
                for g in range(4):
                    rows = slice(g * HD, (g + 1) * HD)
                    a_kbd.done(act.activation(k_bd[part][rows, i % 2, :, :, g * S:(g + 1) * S].rearrange("p b t k -> p t b k"),
                                              kc[rows, i % 2, part, :, :].rearrange("p t (b k) -> p t b k", b=2), ACT.Copy))

        def place_v(act, i):
            ld_v.wait(act, i)
            if i >= 2:
                pe_o.wait(act, 2 * (i - 2) + 2)
            for part in range(2):
                for x in range(2):
                    rows = slice(x * S, (x + 1) * S)
                    slot = v_bd[part][rows, i % 2, :, :, :, :].rearrange("p b t m c -> p (b t) (m c)")
                    dst = bass.AP(slot.tensor, slot.offset + x * HD, [list(slot.ap[0]), [2 * P, 2 * NG], [P + 64, 2], [1, HD]])
                    src = vc[rows, i % 2, part, :, :].rearrange("p b (t m c) -> p (b t) m c", t=NG, m=2)
                    a_vbd.done(act.activation(dst, src[:, :, :, x * HD:(x + 1) * HD], ACT.Copy))

        def store_x1(sp, i):
            v_x1.wait(sp, 2 * i + 2)
            st_x1.start(sp, i, x1_dram[i * P:(i + 1) * P, :], xr[:, i % 3, :])

        def load_residual(sp, i):
            if i >= 3:
                st_x1.wait(sp, i - 3)
            ld_x.start(sp, i, xr[:, i % 3, :], x_nat[i * P:(i + 1) * P, :])

        @on("sync")
        def _(sp):
            for t in range(WS3, NQT):
                load_w3(sp, t)
            ld_cond.start(sp, 0, cidx_i[:], cond.partition_broadcast(P))
            load_residual(sp, 0)
            load_residual(sp, 1)
            load_kv(sp, 2)
            for i in range(NPAIR):
                if i + 2 < NPAIR:
                    load_q(sp, i + 2)
                if i + 3 < NPAIR:
                    load_kv(sp, i + 3)
                if i >= 1:
                    store_x1(sp, i - 1)
                    if i + 1 < NPAIR:
                        load_residual(sp, i + 1)
            store_x1(sp, NPAIR - 1)
            for i in range(NPAIR - 3, NPAIR):
                st_x1.wait(sp, i)

        def scores(pe, u):
            i, b = u // 2, u % 2
            ld_q.wait(pe, i)
            a_kbd.wait(pe, 8 * (i + 1))
            v_sc.wait(pe, u)
            for G in range(NG):
                for rp in range(2):
                    for a, c in PASSES:
                        mm = pe.matmul(ps[:, G, rp * 256:(rp + 1) * 256],
                                       q_sb[a][:, i % 2, b, G * REP + 2 * rp:G * REP + 2 * rp + 2, :],
                                       k_bd[c][:, i % 2, b, G, :], start=(a + c == 0), stop=(a == 1))
            pe_s.done(mm)

        def turn_probs(pe, u):
            g_prob.wait(pe, u + 1)
            v_ptlo.wait(pe, u)
            for G in range(NG):
                for rp in range(2):
                    for pair in range(2):
                        at = G * 512 + rp * 256 + pair * P
                        mm = pe.transpose(ps[:, 2 + G, pair * 256 + rp * P:pair * 256 + (rp + 1) * P],
                                          sc[:, u % 2, at:at + P], C("ident"))
            pe_t.done(mm)

        def values(pe, u):
            i, b = u // 2, u % 2
            a_vbd.wait(pe, 4 * (i + 1))
            a_pthi.wait(pe, u + 1)
            v_ptlo.wait(pe, u + 1)
            v_otlo.wait(pe, u - 1)
            for G in range(NG):
                for pair in range(2):
                    for a, c in PASSES:
                        at = G * 512 + pair * 256
                        mm = pe.matmul(ps[:, 4 + u % 2, G * 256:(G + 1) * 256], v_bd[c][:, i % 2, b, G, pair, :],
                                       pt[a][:, at:at + 256], start=(pair == 0 and a + c == 0),
                                       stop=(pair == 1 and a == 1))
            pe_o.done(mm)

        def project(pe, i, quarter):
            n, tiles = quarter // 2, range(quarter % 2 * 4, quarter % 2 * 4 + 4)
            if quarter == 0:
                a_othi.wait(pe, 2 * i + 2)
                v_otlo.wait(pe, 2 * i + 2)
            if quarter % 2 == 0:
                v_x1.wait(pe, 2 * (i - 1) + n + 1)
            for t in tiles:
                a_w3.wait(pe, t + 1)
                v_w3.wait(pe, t + 1)
                for a, c in PASSES:
                    mm = pe.matmul(ps[:, 6 + n, :], ot[a][:, i % 2, t, :, :], wo[c][:, t, n * 512:(n + 1) * 512],
                                   start=(t == 0 and a + c == 0), stop=(t == NQT - 1 and a == 1))
            pe_y.done(mm)

        @on("tensor")
        def _(pe):
            v_rcos.wait(pe, 4 * NU)
            for w in HALF_SLOTS:
                i, k = w // 2 - 1, w % 2
                if 0 <= w < NUNIT:
                    turn_probs(pe, w)
                if i >= 0:
                    project(pe, i, 2 * k)
                if 0 <= w < NUNIT:
                    values(pe, w)
                if w + 2 < NUNIT:
                    scores(pe, w + 2)
                if i >= 0:
                    project(pe, i, 2 * k + 1)

        def sc_groups(u):
            return sc[:, u % 2, :].rearrange("p (g k) -> p g k", k=S)

        @on("vector")
        def _(v):
            def wo_lo(t):
                a_w3.wait(v, t + 1)
                v_w3.done(v.tensor_tensor(wo[1][:, t, :], wstage3[:, t % WS3, :], wo[0][:, t, :].bitcast(F32),
                                          ALU.subtract))

            def scale_and_max(u):
                pe_s.wait(v, u + 1)
                pe_t.wait(v, u - 1)
                v_sc.done(v.scalar_tensor_tensor(sc_groups(u), ps[:, 0:2, :].rearrange("p a (g k) -> p (a g) k", k=S),
                                                 INV_SQRT, across(C("causal"), 16), ALU.mult, ALU.add))
                v_sc.wait(v, u + 1)
                v_max.done(v.tensor_reduce(stat[:, u % 2, 0, :], sc_groups(u), AX_X, ALU.max))

            for w in HALF_SLOTS:
                if w == -1:
                    scale_and_max(w + 2)
                for t in WO_TILES.get(w, ()):
                    wo_lo(t)
                if w == 1:
                    ld_cond.wait(v, 0)
                    for b in range(2):
                        r = slice(b * S, (b + 1) * S)
                        v_cidx.done(v.tensor_scalar(cidx[r, :], cidx_i[r, b::2], float(S), C("chan")[r, :],
                                                    ALU.mult, ALU.add))
                if 0 <= w < NUNIT:
                    a_pthi.wait(v, w + 1)
                    v_ptlo.done(v.tensor_tensor(pt[1][:], ps[:, 2:4, :].rearrange("p a c -> p (a c)"),
                                                pt[0][:].bitcast(F32), ALU.subtract))
                if w >= 3:
                    i, n = (w - 1) // 2 - 1, (w - 1) % 2
                    pe_y.wait(v, 4 * i + 2 * n + 2)
                    ld_x.wait(v, i)
                    x = xr[:, i % 3, n * 512:(n + 1) * 512]
                    v_x1.done(v.tensor_tensor(x, bank(6 + n), x, ALU.add))
                if 0 <= w + 1 < NUNIT:
                    u = w + 1
                    a_exp.wait(v, u + 1)
                    v_sum.done(v.tensor_reduce(stat[:, u % 2, 1, :], sc_groups(u), AX_X, ALU.add))
                    v_sum.wait(v, u + 1)
                    v_rec.done(v.reciprocal(stat[:, u % 2, 2, :], stat[:, u % 2, 1, :]))
                if 0 <= w < NUNIT:
                    a_othi.wait(v, w + 1)
                    v_otlo.done(v.tensor_tensor(ot[1][:, (w // 2) % 2, :, w % 2, :],
                                                bank(4 + w % 2).rearrange("p (t q) -> p t q", q=S),
                                                ot[0][:, (w // 2) % 2, :, w % 2, :].bitcast(F32), ALU.subtract))
                if w != -1 and w + 2 < NUNIT:
                    scale_and_max(w + 2)
            i = NPAIR - 1
            pe_y.wait(v, 4 * i + 4)
            x = xr[:, i % 3, 512:]
            v_x1.done(v.tensor_tensor(x, bank(7), x, ALU.add))

        @on("gpsimd")
        def _(gp):
            pe_unit.wait(gp, NU + 1)
            for part in range(2):
                g_zero3.done(gp.memset(v_bd[part][:].bitcast(F32), 0.0))
            for w in range(-1, NUNIT - 1):
                u = w + 1
                v_max.wait(gp, u + 1)
                g_sub.done(gp.tensor_tensor(sc_groups(u), sc_groups(u), along(stat[:, u % 2, 0, :], S), ALU.subtract))
                if u in (6, 7):
                    g_zero3.done(gp.memset(mix[u - 6][:].bitcast(F32), 0.0))
                if 8 <= u < 8 + NPAIR:
                    v_cidx.wait(gp, 2)
                    i = u - 8
                    gp.indirect_dma_start(craw[:, i, :], None, w_cond.rearrange("n c d -> (n c) d"),
                                          bass.IndirectOffsetOnAxis(ap=cidx[:, i:i + 1], axis=0))\
                      .then_inc(ld_cmix.sems[0], 16)
                if u == 12 + NPAIR:
                    a_mix.wait(gp, 2)
                    g_sub.wait(gp, u + 1)
                    for b in range(2):
                        r = slice(b * S, (b + 1) * S)
                        g_mix.done(gp.tensor_tensor(mix[1][r, :, b * S:(b + 1) * S], craw[r, :, :],
                                                    mix[0][r, :, b * S:(b + 1) * S].bitcast(F32), ALU.subtract))
                        g_mix.wait(gp, b + 1)
                v_rec.wait(gp, u + 1)
                g_prob.done(gp.tensor_tensor(sc_groups(u), sc_groups(u), along(stat[:, u % 2, 2, :], S), ALU.mult))

        @on("scalar")
        def _(act):
            place_k(act, 0)
            g_zero3.wait(act, 2)
            place_v(act, 0)
            place_k(act, 1)

            def wo_hi(t):
                ld_w3.wait(act, t)
                a_w3.done(act.activation(wo[0][:, t, :], wstage3[:, t % WS3, :], ACT.Copy))

            for w in HALF_SLOTS:
                if w >= 1 and w % 2 == 1 and (w + 3) // 2 < NPAIR:
                    place_k(act, (w + 3) // 2)
                if w >= 0 and w % 2 == 0 and (w + 2) // 2 < NPAIR:
                    place_v(act, (w + 2) // 2)
                for t in WO_TILES.get(w, ()) if w >= 0 else ():
                    wo_hi(t)
                if 0 <= w < NUNIT:
                    pe_t.wait(act, w + 1)
                    pe_o.wait(act, w)
                    a_pthi.done(act.activation(pt[0][:], ps[:, 2:4, :].rearrange("p a c -> p (a c)"), ACT.Copy))
                if 0 <= w + 1 < NUNIT:
                    u = w + 1
                    g_sub.wait(act, u + 1)
                    a_exp.done(act.activation(sc[:, u % 2, :], sc[:, u % 2, :], ACT.Exp))
                for t in WO_TILES.get(w, ()) if w < 0 else ():
                    wo_hi(t)
                if w == 8 + NPAIR:
                    ld_cmix.wait(act, 0)
                    g_zero3.wait(act, 4)
                    for b in range(2):
                        r = slice(b * S, (b + 1) * S)
                        a_mix.done(act.activation(mix[0][r, :, b * S:(b + 1) * S], craw[r, :, :], ACT.Copy))
                if 0 <= w < NUNIT:
                    i = w // 2
                    pe_o.wait(act, w + 1)
                    pe_y.wait(act, 4 * (i - 1))
                    a_othi.done(act.activation(ot[0][:, i % 2, :, w % 2, :],
                                               bank(4 + w % 2).rearrange("p (t q) -> p t q", q=S), ACT.Copy))

        def load_x1(sp, i):
            if i >= 4:
                st_out.wait(sp, i - 4)
            ld_x1.start(sp, i, x1[:, i % 4, :], x1_dram[i * P:(i + 1) * P, :])

        @on("sync")
        def _(sp):
            v_x1.wait(sp, 2 * NPAIR)
            load_x1(sp, 0)
            ld_p4.start(sp, 0, wpj_raw[:], w_proj)
            ld_p4.start(sp, 0, bexp_raw[:], w_b)
            for t in range(NJ):
                if t >= WS4:
                    a_w4.wait(sp, t - WS4 + 1)
                    v_w4.wait(sp, t - WS4 + 1)
                ld_w4.start(sp, t, wstage4[:, t % WS4, :], w_base[:, t, :])
                if t == WS4 - 1:
                    load_x1(sp, 1)
            for i in range(NPAIR + 1):
                if i + 2 < NPAIR:
                    load_x1(sp, i + 2)
                if i >= 1:
                    v_out.wait(sp, 2 * i)
                    st_out.start(sp, i - 1, out[(i - 1) * P:i * P, :], x1[:, (i - 1) % 4, :])
            for i in range(NPAIR - 4, NPAIR):
                st_out.wait(sp, i)

        def mix_channels(pe, i):
            a_x1hi.wait(pe, i + 1)
            g_x1lo.wait(pe, i + 1)
            a_mix.wait(pe, 2)
            g_mix.wait(pe, 2)
            for half in range(2):
                v_xflo.wait(pe, 2 * (i - 1) + half + 1)
                for t in range(4):
                    for a, c in PASSES:
                        at = (half * 4 + t) * P
                        mm = pe.matmul(ps[:, half, t * P:(t + 1) * P], x1s[a][:, i % 2, at:at + P], mix[c][:, i, :],
                                       start=(a + c == 0), stop=(a == 1))
                pe_mix.done(mm)

        def base(pe, i, half):
            a_xfhi.wait(pe, 2 * i + half + 1)
            v_xflo.wait(pe, 2 * i + half + 1)
            if half == 0:
                v_out.wait(pe, 2 * (i - 1))
                v_h.wait(pe, i - 1)
                v_htlo.wait(pe, i - 1)
            for t in range(half * 4, half * 4 + 4):
                a_w4.wait(pe, t + 1)
                v_w4.wait(pe, t + 1)
                for a, c in PASSES:
                    first, last = t == 0 and a + c == 0, t == NJ - 1 and a == 1
                    for n in range(2):
                        pe.matmul(ps[:, 2 + 2 * (i % 2) + n, :], xf[a][:, i % 2, t, :], wb[c][:, t, n * 512:(n + 1) * 512],
                                  start=first, stop=False)
                    mm = pe.matmul(ps[:, 6 + i % 2, 0:NPROJ], xf[a][:, i % 2, t, :], wpj[c][:, t, :], start=first, stop=last)
            if half == 1:
                pe_f.done(mm)

        def turned_h(i):
            return ps[0:NE * RANK, 6 + i % 2, P:2 * P]

        def turn_h(pe, i):
            v_h.wait(pe, i + 1)
            v_htlo.wait(pe, i)
            pe_ht.done(pe.transpose(turned_h(i), hw[:], C("ident")))

        def experts(pe, i):
            a_hthi.wait(pe, i + 1)
            v_htlo.wait(pe, i + 1)
            for n in range(2):
                for a, c in PASSES:
                    mm = pe.matmul(ps[:, 2 + 2 * (i % 2) + n, :], ht[a][:], bexp[c][:, n * 512:(n + 1) * 512],
                                   start=False, stop=(a == 1))
                pe_out.done(mm)

        @on("tensor")
        def _(pe):
            v_x1.wait(pe, 2 * NPAIR)
            mix_channels(pe, 0)
            a_p4.wait(pe, 2)
            g_p4.wait(pe, 2)
            for i in range(NPAIR + 1):
                if i < NPAIR:
                    base(pe, i, 0)
                if i >= 1:
                    turn_h(pe, i - 1)
                if i + 1 < NPAIR:
                    mix_channels(pe, i + 1)
                if i >= 1:
                    experts(pe, i - 1)
                if i < NPAIR:
                    base(pe, i, 1)

        def x1_hi(act, i):
            ld_x1.wait(act, i)
            pe_mix.wait(act, 2 * (i - 1))
            a_x1hi.done(act.activation(x1s[0][:, i % 2, :], x1[:, i % 4, :], ACT.Copy))

        def xf_hi(act, i):
            pe_f.wait(act, i - 1)
            for half in range(2):
                pe_mix.wait(act, 2 * i + half + 1)
                a_xfhi.done(act.activation(xf[0][:, i % 2, half * 4:half * 4 + 4, :],
                                           bank(half).rearrange("p (t q) -> p t q", q=P), ACT.Copy))

        @on("scalar")
        def _(act):
            x1_hi(act, 0)
            ld_p4.wait(act, 0)
            a_p4.done(act.activation(wpj[0][:], wpj_raw[:], ACT.Copy))
            a_p4.done(act.activation(bexp[0][:], bexp_raw[:], ACT.Copy))
            for t in range(NJ):
                ld_w4.wait(act, t)
                a_w4.done(act.activation(wb[0][:, t, :], wstage4[:, t % WS4, :], ACT.Copy))
                if t == 1:
                    xf_hi(act, 0)
            x1_hi(act, 1)
            for i in range(NPAIR + 1):
                if i >= 1:
                    v_gate.wait(act, GATE_STEPS * (i - 1) + 2)
                    a_gate.done(act.activation(gt[:, 0, :], ps[:, 6 + (i - 1) % 2, 0:NE], ACT.Exp, bias=gs[:, 1:2],
                                               accum_out=gs[:, 2:3]))
                    pe_ht.wait(act, i)
                    pe_out.wait(act, 2 * (i - 1))
                    a_hthi.done(act.activation(ht[0][:], turned_h(i - 1), ACT.Copy))
                if i + 1 < NPAIR:
                    xf_hi(act, i + 1)
                if i + 2 < NPAIR:
                    x1_hi(act, i + 2)

        @on("gpsimd")
        def _(gp):
            def x1_lo(i):
                a_x1hi.wait(gp, i + 1)
                g_x1lo.done(gp.tensor_tensor(x1s[1][:, i % 2, :], x1[:, i % 4, :], x1s[0][:, i % 2, :].bitcast(F32),
                                             ALU.subtract))

            x1_lo(0)
            for n, (lo, raw, hi) in enumerate(((wpj[1], wpj_raw, wpj[0]), (bexp[1], bexp_raw, bexp[0]))):
                a_p4.wait(gp, n + 1)
                g_p4.done(gp.tensor_tensor(lo[:], raw[:], hi[:].bitcast(F32), ALU.subtract))
            for i in range(1, NPAIR):
                x1_lo(i)

        GATE_STEPS = 11

        def gate(v, i):
            n0 = GATE_STEPS * i

            def link(k, ins):
                v_gate.done(ins)
                v_gate.wait(v, n0 + k)

            logits = ps[:, 6 + i % 2, 0:NE]
            pe_f.wait(v, i + 1)
            link(1, v.tensor_reduce(gs[:, 0:1], logits, AX_X, ALU.max))
            link(2, v.tensor_scalar(gs[:, 1:2], gs[:, 0:1], -1.0, None, ALU.mult))
            a_gate.wait(v, i + 1)
            link(3, v.reciprocal(gs[:, 3:4], gs[:, 2:3]))
            link(4, v.tensor_scalar(gt[:, 1, :], gt[:, 0, :], gs[:, 3:4], None, ALU.mult))
            link(5, v.max(gt[:, 2, :], gt[:, 1, :]))
            link(6, v.max_index(gi[:], gt[:, 2, :], gt[:, 1, :]))
            link(7, v.tensor_copy(gt[:, 3, :], gi[:]))
            link(8, v.tensor_tensor(gs[:, 4:5], gt[:, 2, 0:1], gt[:, 2, 1:2], ALU.add))
            v.reciprocal(gs[:, 5:6], gs[:, 4:5]).then_inc(v_gate.sem, 1)
            for k in range(2):
                ins = v.tensor_scalar(gt[:, 4 + k, :], C("iota8"), gt[:, 3, k:k + 1], gt[:, 2, k:k + 1],
                                      ALU.is_equal, ALU.mult)
            v_gate.done(ins)
            v_gate.wait(v, n0 + 10)
            link(11, v.tensor_tensor(gt[:, 6, :], gt[:, 4, :], gt[:, 5, :], ALU.add))
            v_wts.done(v.tensor_scalar(gt[:, 7, :], gt[:, 6, :], gs[:, 5:6], SCALING, ALU.mult, ALU.mult))
            v_wts.wait(v, i + 1)
            pe_ht.wait(v, i)
            v_h.done(v.tensor_tensor(hw[:].rearrange("p (e r) -> p e r", r=RANK),
                                     ps[:, 6 + i % 2, NE:NPROJ].rearrange("p (e r) -> p e r", r=RANK),
                                     along(gt[:, 7, :], RANK), ALU.mult))

        v_wts = step("v_wts")

        def xf_lo(v, i):
            for half in range(2):
                a_xfhi.wait(v, 2 * i + half + 1)
                dst, hi = (xf[part][:, i % 2, half * 4:half * 4 + 4, :] for part in (1, 0))
                v_xflo.done(v.tensor_tensor(dst, bank(half).rearrange("p (t q) -> p t q", q=P), hi.bitcast(F32),
                                            ALU.subtract))

        @on("vector")
        def _(v):
            for t in range(NJ):
                a_w4.wait(v, t + 1)
                v_w4.done(v.tensor_tensor(wb[1][:, t, :], wstage4[:, t % WS4, :], wb[0][:, t, :].bitcast(F32),
                                          ALU.subtract))
                if t == 1:
                    xf_lo(v, 0)
            for i in range(NPAIR + 1):
                if i >= 1:
                    gate(v, i - 1)
                    a_hthi.wait(v, i)
                    v_htlo.done(v.tensor_tensor(ht[1][:], turned_h(i - 1), ht[0][:].bitcast(F32), ALU.subtract))
                if i + 1 < NPAIR:
                    xf_lo(v, i + 1)
                if i >= 1:
                    for n in range(2):
                        pe_out.wait(v, 2 * (i - 1) + n + 1)
                        x = x1[:, (i - 1) % 4, n * 512:(n + 1) * 512]
                        v_out.done(v.tensor_tensor(x, bank(2 + 2 * ((i - 1) % 2) + n), x, ALU.add))

        block = ctx.enter_context(nc.Block())
        for name, register in (("sync", block.sync), ("gpsimd", block.gpsimd), ("scalar", block.scalar),
                               ("vector", block.vector), ("tensor", block.tensor)):
            @register
            def _(eng, queue=queues[name]):
                for part in queue:
                    part(eng)


def _layouts(i):
    def head_rows(w, heads):
        return w.reshape(-1, HD, L)[heads].reshape(-1, L)

    def feature_major(w):
        return w.reshape(-1, NJ, P).transpose(2, 1, 0)

    x = i["x"]
    q_heads = np.array([(4 * G + g) * REP + r for G in range(NG) for r in range(REP) for g in range(4)])
    wqk = np.concatenate([i["L0_attn_Wk"], head_rows(i["L0_attn_Wq"], q_heads)])
    wo = i["L0_attn_Wo"].reshape(L, -1, HD)[:, q_heads].reshape(L, NQT, P)
    proj = np.concatenate([i["L0_ffn_gate_W"], i["L0_ffn_A"].reshape(NE * RANK, L)])
    return [
        x.reshape(NB, S, NJ, P)[..., ::-1].transpose(3, 1, 2, 0).reshape(P, S, NJ * NB),
        x.reshape(TOK, L),
        i["itok_B_8_3872"], i["itok_B_0_15"],
        np.stack([np.broadcast_to(i["L0_cond_log_dt"][:, None], (S, NMODE)), i["L0_cond_log_A_real"],
                  i["L0_cond_A_imag"], i["L0_cond_C"][..., 0], i["L0_cond_C"][..., 1]]).transpose(2, 0, 1),
        i["L0_cond_D"],
        wqk.reshape(NG + NQT, P, NJ, P).transpose(0, 3, 2, 1).reshape(NG + NQT, P, NJ * P),
        feature_major(i["L0_attn_Wv"]).reshape(P, -1),
        wo.transpose(2, 1, 0),
        i["L0_cond2_weights"],
        feature_major(i["L0_ffn_W_base"]),
        feature_major(proj),
        i["L0_ffn_B"].transpose(0, 2, 1).reshape(NE * RANK, L),
        constants(),
    ]


def kernel(**inputs):
    import concourse.bacc as bacc
    from concourse.bass_utils import run_bass_kernel_spmd

    nc = bacc.Bacc("TRN2", target_bir_lowering=False, num_devices=1)
    arrays, args = {}, []
    for n, a in enumerate(_layouts({k: np.asarray(v) for k, v in inputs.items()})):
        a = np.ascontiguousarray(a)
        arrays[f"in_{n}_dram"] = a
        args.append(nc.dram_tensor(f"in_{n}_dram", a.shape, mybir.dt.from_np(a.dtype), kind="ExternalInput").ap())
    out = nc.dram_tensor("out_dram", (TOK, L), F32, kind="ExternalOutput").ap()
    build(nc, *args, out)
    r = run_bass_kernel_spmd(nc, [arrays], core_ids=[0])
    return r.results[0]["out_dram"].reshape(NB, S, L)
```

```python
from contextlib import ExitStack

import concourse.bass as bass
import numpy as np
from concourse import mybir

F32 = mybir.dt.float32
F32R = mybir.dt.float32r
I32 = mybir.dt.int32
U32 = mybir.dt.uint32
ALU = mybir.AluOpType
ACT = mybir.ActivationFunctionType
AX_X = mybir.AxisListType.X

P = 128
NB, S, L = 32, 64, 1024
TOK = NB * S
NJ = L // P
NMODE = 64
HD, NKV, REP = 32, 8, 4
NG = NKV // 4
NQT = NG * REP
NPAIR = NB // 2
NE, RANK = 8, 8
NPROJ = NE + NE * RANK
NBASE = NPROJ + L
JOINT = [(0, 256), (256, 676), (676, NBASE)]
NCOND = 16
SCALING = 2.0
HB = 32
HGRP = 8
NHG = S // HGRP
GP = HGRP // 2
KROW = P - 1 + L
ROUND = 12582912.0
SIN_SCALE = 6.283184
TWO_PI = 2.0 * np.pi


def _short(v, bits):
    m, e = np.frexp(v)
    return float(np.ldexp(np.round(m * 2.0 ** bits), int(e) - bits))


PI_A = 6.28125
PI_B = _short(TWO_PI - PI_A, 11)
PI_C = float(TWO_PI - PI_A - PI_B)

CONSTS = {}


def _layout(*fields):
    at = 0
    for name, n in fields:
        CONSTS[name] = (at, n)
        at += n
    return at


NCONST = _layout(("ident", P), ("cos", S), ("sin", S), ("causal", S), ("pos", NJ), ("step", HB),
                 ("off", 3), ("off_rad", 3), ("half_pi", 1), ("chan", 1), ("iota8", NE))


def constants():
    t = np.zeros((P, NCONST), np.float32)

    def put(name, v):
        at, n = CONSTS[name]
        t[:, at:at + n] = v

    p = np.arange(P)
    put("ident", np.eye(P))
    inv_freq = (1.0 / np.float32(10000.0) ** (np.arange(0, HD, 2, dtype=np.float32) / HD)).astype(np.float32)
    freqs = np.outer(np.arange(S, dtype=np.float32), inv_freq).astype(np.float32)
    emb = np.concatenate([freqs, freqs], axis=-1)
    put("cos", np.cos(emb.astype(np.float64)).T[p % HD])
    sign = np.where(p % HD < HD // 2, -1.0, 1.0)[:, None]
    put("sin", sign * np.sin(emb.astype(np.float64)).T[p % HD])
    k, q = np.arange(S)[None, :], (p % S)[:, None]
    put("causal", np.where(q < k, np.finfo(np.float32).min, np.float32(0)))
    put("pos", p[:, None] + P * np.arange(NJ)[None, :])
    put("step", np.arange(HB)[None, :])
    im = (p >= NMODE)[:, None]
    off = np.concatenate([np.where(im, 0.5, 0.25), np.where(im, 0.25, 0.0), np.where(im, 0.0, 0.25)], axis=1)
    put("off", off)
    put("off_rad", off * SIN_SCALE)
    put("half_pi", np.pi / 2)
    put("chan", (p % S)[:, None])
    put("iota8", np.arange(NE)[None, :])
    return t


class Step:

    def __init__(self, ctx, nc, name):
        self.sem = ctx.enter_context(nc.semaphore(name))

    def done(self, ins):
        ins.then_inc(self.sem, 1)

    def wait(self, eng, n):
        if n > 0:
            eng.wait_ge(self.sem, n)


class Loads:

    def __init__(self, ctx, nc, name, ring, parts=1):
        self.sems = [ctx.enter_context(nc.semaphore(f"{name}{i}")) for i in range(ring)]
        self.ring, self.parts = ring, parts

    def start(self, eng, use, dst, src):
        if dst.dtype == F32R:
            dst = dst.bitcast(F32)
        if src.dtype == F32R:
            src = src.bitcast(F32)
        eng.dma_start(dst, src).then_inc(self.sems[use % self.ring], 16)

    def wait(self, eng, use):
        eng.wait_ge(self.sems[use % self.ring], 16 * self.parts * (use // self.ring + 1))


def across(ap, n):
    return ap.unsqueeze(1).to_broadcast([ap.shape[0], n, ap.shape[1]])


def along(ap, n):
    return ap.unsqueeze(2).to_broadcast([ap.shape[0], ap.shape[1], n])


def build(nc, x_conv, x_nat, lens, cond, modes, d_skip,
          w_qk, w_v, w_o, w_cond, w_ffn, w_b, consts, out):
    ctx = ExitStack()
    with ctx:
        def sb(name, shape, dt=F32, stack=ctx):
            return stack.enter_context(nc.sbuf_tensor(name, shape, dt))

        def step(name):
            return Step(ctx, nc, name)

        def loads(name, ring=1, parts=1):
            return Loads(ctx, nc, name, ring, parts)

        kpad = nc.dram_tensor("kpad", [S, KROW + 1], F32, kind="Internal")
        k_dram = [nc.dram_tensor(f"k_{n}", [NG, P, TOK], F32, kind="Internal").ap() for n in ("hi", "lo")]
        q_dram = [nc.dram_tensor(f"q_{n}", [NB, P, NQT, S], F32, kind="Internal").ap() for n in ("hi", "lo")]
        v_dram = [nc.dram_tensor(f"v_{n}", [TOK, NKV * HD], F32, kind="Internal").ap() for n in ("hi", "lo")]
        x1_dram = nc.dram_tensor("x1_scratch", [TOK, L], F32, kind="Internal").ap()

        ps = ctx.enter_context(nc.psum_tensor("ps", [P, 8, 512], F32))

        cst = sb("cst", [P, NCONST])

        def C(name):
            at, n = CONSTS[name]
            return cst[:, at:at + n]

        s12 = ExitStack()
        y = [sb(f"y_{n}", [P, NJ, NB, S], F32R, s12) for n in ("hi", "lo")]
        WR = 3
        wraw = sb("wraw", [P, WR, NJ * P], F32, s12)
        wsp = [sb(f"w12_{n}", [P, WR, NJ * P], F32R, s12) for n in ("hi", "lo")]

        s1 = ExitStack()
        TR = 3
        toep = sb("toep", [P, TR, L], F32, s1)
        XH, XR = 2, 4
        xc = sb("xc", [P, XR, XH, NJ * NB], F32, s1)
        ym = sb("ym", [P, 2, 2, NJ * NB], F32, s1)
        valid = sb("valid", [P, NJ, NB], F32, s1)
        len_i = sb("len_i", [P, NB], I32, s1)
        len_f = sb("len_f", [P, NB], F32, s1)
        prm = sb("prm", [P, 5, S], F32, s1)
        t64 = sb("t64", [P, 24, S], F32, s1)
        d_row = sb("d_row", [1, S], F32, s1)
        zeros = sb("zeros", [S, P - 1], F32, s1)
        GC = HGRP * HB
        ph = sb("ph", [P, 2, GC], F32, s1)
        mg = sb("mg", [P, 2, GC], F32, s1)
        rn = sb("rn", [P, 3, GC], F32, s1)
        ltab, rtab = ph[:, 0, :], ph[:, 1, :]
        ksb = sb("ksb", [HB, 2, GC], F32, s1)
        s1.close()

        s2 = ExitStack()
        RR = 2
        rot = sb("rot", [P, RR, 512], F32, s2)
        rc = sb("rc", [P, RR, 512], F32, s2)
        rf = sb("rf", [P, RR, 512], F32, s2)
        SR = 3
        stg = [sb(f"stg_{n}", [P, SR, 512], F32R, s2) for n in ("hi", "lo")]
        s2.close()
        s12.close()

        s3 = ExitStack()
        wo = [sb(f"wo_{n}", [P, NQT, L], F32R, s3) for n in ("hi", "lo")]
        WS3 = 4
        wstage3 = sb("wstage3", [P, WS3, L], F32, s3)
        ot = [sb(f"ot_{n}", [P, 2, NQT, 2, S], F32R, s3) for n in ("hi", "lo")]
        xr = sb("xr", [P, 3, L], F32, s3)
        def k_slot(n):
            return sb(f"kbd_{n}", [P, 2, 2, NG, 4 * S], F32R, s3)

        def q_slot(n):
            return sb(f"q_{n}", [P, 2, 2, NQT, S], F32R, s3)

        def v_slot(n):
            return sb(f"vbd_{n}", [P, 2, 2, NG, 2, P], F32R, s3)

        k_1, q_1 = k_slot(1), q_slot(1)
        craw = sb("craw", [P, NPAIR, S], F32, s3)
        q_0, k_0 = q_slot(0), k_slot(0)
        sc = sb("sc", [P, 2, 1024], F32, s3)
        v_0, v_1 = v_slot(0), v_slot(1)
        q_sb, k_bd, v_bd = (q_0, q_1), (k_0, k_1), (v_0, v_1)
        pt = [sb(f"pt_{n}", [P, 1024], F32R, s3) for n in ("hi", "lo")]
        mix = sb("mix", [P, NPAIR, P], F32, s3)
        sb("rest_of_stg", [P, (2 * SR * 512) - NPAIR * P], F32, s3)
        stat = sb("stat", [P, 2, 3, 16], F32, s3)
        cidx_i = sb("cidx_i", [P, NB], I32, s3)
        cidx = sb("cidx", [P, NPAIR], U32, s3)
        kc = sb("kc", [P, 2, 2, NG, P], F32R, s3)
        vc = sb("vc", [P, 2, 2, 2, NKV * HD], F32R, s3)
        s3.close()

        s4 = ExitStack()
        x1_late = [sb(f"x1_{n}", [P, L], F32, s4) for n in (2, 3)]
        xf_late = sb("xf_1", [P, 2, NJ, P], F32R, s4)
        WB_EARLY = 6
        wb_late = [sb(f"wb_{t}", [P, 2, NBASE], F32R, s4) for t in range(WB_EARLY, NJ)]
        bexp = [sb(f"bexp_{n}", [NE * RANK, L], F32R, s4) for n in ("hi", "lo")]
        bexp_raw = sb("bexp_raw", [NE * RANK, L], F32, s4)
        gt = sb("gt", [P, 8, NE], F32, s4)
        gi = sb("gi", [P, NE], U32, s4)
        gs = sb("gs", [P, 8], F32, s4)
        hw = sb("hw", [P, NE * RANK], F32, s4)
        ht = [sb(f"ht_{n}", [NE * RANK, P], F32R, s4) for n in ("hi", "lo")]
        late = 2 * L + 2 * NJ * P + 2 * (NJ - WB_EARLY) * NBASE + 3 * L + 10 * NE + NE * RANK + 2 * P
        sb("rest_of_wo", [P, 2 * NQT * L - late], F32, s4)
        WS4 = 3
        wstage4 = sb("wstage4", [P, WS4, NBASE], F32, s4)
        sb("ot_and_xr", [P, (WS3 * L + 4 * NQT * 2 * S + 3 * L) - WS4 * NBASE], F32, s4)
        x1 = [sb(f"x1_{n}", [P, L], F32, s4) for n in (0, 1)] + x1_late
        xf = [sb("xf_0", [P, 2, NJ, P], F32R, s4), xf_late]
        wb = [sb(f"wb_{t}", [P, 2, NBASE], F32R, s4) for t in range(WB_EARLY)] + wb_late
        s4.close()

        ld_cst, ld_prm, ld_len, ld_d = loads("ld_cst"), loads("ld_prm", 1, 2), loads("ld_len"), loads("ld_d")
        ld_cond, ld_cmix = loads("ld_cond"), loads("ld_cmix", 1, NPAIR)
        st_zero, st_k = loads("st_zero"), loads("st_k", 2)
        ld_toep, ld_xc = loads("ld_toep", TR), loads("ld_xc", XR)
        ld_w = [ctx.enter_context(nc.semaphore(f"ld_w{i}")) for i in range(WR)]
        st_stg = loads("st_stg", SR, 2)
        ld_w3, ld_q, ld_k, ld_v, ld_x = (loads("ld_w3", WS3), loads("ld_q", 2, 2), loads("ld_k", 2, 2),
                                         loads("ld_v", 2, 4), loads("ld_x", 3))
        st_x1 = loads("st_x1", 3)
        ld_w4, ld_p4, ld_x1, st_out = loads("ld_w4", WS4), loads("ld_p4"), loads("ld_x1", 4), loads("st_out", 4)
        a_set, v_set, v_rho, v_ang, v_cs = map(step, ("a_set", "v_set", "v_rho", "v_ang", "v_cs"))
        g_zero, v_cidx, v_len, v_valid = map(step, ("g_zero", "v_cidx", "v_len", "v_valid"))
        g_mag, a_mag, v_ph, v_round, a_sin, v_tab = map(step, ("g_mag", "a_mag", "v_ph", "v_round", "a_sin", "v_tab"))
        pe_k, v_ke, v_k = map(step, ("pe_k", "v_ke", "v_k"))
        pe_conv, v_mask, a_yhi, g_ylo = map(step, ("pe_conv", "v_mask", "a_yhi", "g_ylo"))
        a_mix = step("a_mix")
        a_whi, g_wlo, pe_unit = map(step, ("a_whi", "g_wlo", "pe_unit"))
        pe_v, a_vhi, v_vlo = map(step, ("pe_v", "a_vhi", "v_vlo"))
        pe_m, v_rot, v_rcos, g_rsin, g_rsum, a_rhi, v_rlo = map(
            step, ("pe_m", "v_rot", "v_rcos", "g_rsin", "g_rsum", "a_rhi", "v_rlo"))
        v_zero3, g_zero3, a_w3, v_w3, g_w3 = map(step, ("v_zero3", "g_zero3", "a_w3", "v_w3", "g_w3"))
        a_kbd, a_vbd = step("a_kbd"), step("a_vbd")
        pe_s, v_sc, v_max, g_sub, a_exp, v_sum, v_rec, g_prob = map(
            step, ("pe_s", "v_sc", "v_max", "g_sub", "a_exp", "v_sum", "v_rec", "g_prob"))
        pe_t, a_pthi, v_ptlo, pe_o, a_othi, v_otlo, pe_y, v_x1 = map(
            step, ("pe_t", "a_pthi", "v_ptlo", "pe_o", "a_othi", "v_otlo", "pe_y", "v_x1"))
        a_p4, g_p4, a_w4, v_w4 = map(step, ("a_p4", "g_p4", "a_w4", "v_w4"))
        pe_mix, a_xfhi, v_xflo = map(step, ("pe_mix", "a_xfhi", "v_xflo"))
        pe_f, v_gate, a_gate, v_h, pe_ht, a_hthi, v_htlo, pe_out, v_out = map(
            step, ("pe_f", "v_gate", "a_gate", "v_h", "pe_ht", "a_hthi", "v_htlo", "pe_out", "v_out"))

        queues = {"sync": [], "gpsimd": [], "scalar": [], "vector": [], "tensor": []}

        def on(engine):
            return queues[engine].append

        def bank(n):
            return ps[:, n, :]

        PASSES = ((0, 0), (0, 1), (1, 0))

        names64 = ("dt", "ar", "rho", "rho32", "th", "k", "r", "vr", "v32", "e1", "tanh", "sh", "ch",
                   "cm1", "nr", "ni", "den", "t0", "t1", "t2", "gr", "gi", "cr", "ci")

        def M(name):
            return t64[:, names64.index(name), :]

        LOGDT, LOGA, AIM, CRE, CIM = (prm[:, i, :] for i in range(5))

        @on("sync")
        def _(sp):
            for half in (slice(0, NMODE), slice(NMODE, P)):
                ld_prm.start(sp, 0, prm[half, :, :], modes)
            ld_cst.start(sp, 0, cst[:], consts)
            ld_d.start(sp, 0, d_row[:], d_skip.rearrange("(a h) -> a h", a=1))
            ld_len.start(sp, 0, len_i[:], lens.partition_broadcast(P))
            g_zero.wait(sp, 1)
            st_zero.start(sp, 0, kpad.ap()[:, 0:P - 1], zeros[:])

        @on("scalar")
        def _(act):
            ld_prm.wait(act, 0)
            a_set.done(act.activation(M("dt"), LOGDT, ACT.Exp))
            a_set.done(act.activation(M("ar"), LOGA, ACT.Exp))
            v_rho.wait(act, 1)
            a_set.done(act.activation(M("e1"), M("rho"), ACT.Exp))
            a_set.done(act.activation(M("tanh"), M("rho"), ACT.Tanh, scale=0.5))

        def magnitudes(act, g):
            for i in range(2):
                g_mag.wait(act, 2 * g + i + 1)
                a_mag.done(act.activation(mg[:, i, :], mg[:, i, :], ACT.Exp))

        def sines(act, g):
            v_round.wait(act, 3 * (g + 1))
            for i in range(3):
                a_sin.done(act.activation(rn[:, i, :], rn[:, i, :], ACT.Sin, scale=-SIN_SCALE,
                                          bias=C("off_rad")[:, i:i + 1]))

        @on("scalar")
        def _(act):
            magnitudes(act, 0)
            v_ang.wait(act, 1)
            ld_cst.wait(act, 0)
            a_set.done(act.activation(M("sh"), M("r"), ACT.Sin, scale=0.5))
            a_set.done(act.activation(M("ch"), M("r"), ACT.Sin, scale=0.4999998, bias=C("half_pi")))
            sines(act, 0)

        def exponents(gp, g):
            v_tab.wait(gp, 2 * g)
            hs = slice(g * HGRP, (g + 1) * HGRP)
            for i, r in enumerate(("rho32", "rho")):
                g_mag.done(gp.tensor_tensor(mg[:, i, :].rearrange("p (h s) -> p h s", s=HB), along(M(r)[:, hs], HB),
                                            across(C("step"), HGRP), ALU.mult))

        @on("gpsimd")
        def _(gp):
            g_zero.done(gp.memset(zeros[:], 0.0))
            ld_cst.wait(gp, 0)
            v_rho.wait(gp, 1)
            exponents(gp, 0)

        def chain(v, ins):
            v_set.done(ins)
            chain.n += 1
            v_set.wait(v, chain.n)

        chain.n = 0

        @on("vector")
        def _(v):
            a_set.wait(v, 2)
            chain(v, v.tensor_scalar(M("ar"), M("ar"), -1.0, None, ALU.mult))
            chain(v, v.tensor_tensor(M("rho"), M("ar"), M("dt"), ALU.mult))
            v_rho.done(v.tensor_scalar(M("rho32"), M("rho"), float(HB), None, ALU.mult))
            chain(v, v.tensor_tensor(M("th"), AIM, M("dt"), ALU.mult))
            chain(v, v.tensor_scalar(M("k"), M("th"), 1.0 / TWO_PI, ROUND, ALU.mult, ALU.add))
            chain(v, v.tensor_scalar(M("k"), M("k"), ROUND, None, ALU.subtract))
            chain(v, v.scalar_tensor_tensor(M("t0"), M("k"), -PI_A, M("th"), ALU.mult, ALU.add))
            chain(v, v.scalar_tensor_tensor(M("t1"), M("k"), -PI_B, M("t0"), ALU.mult, ALU.add))
            chain(v, v.scalar_tensor_tensor(M("r"), M("k"), -PI_C, M("t1"), ALU.mult, ALU.add))
            chain(v, v.tensor_scalar(M("vr"), M("r"), 1.0 / TWO_PI, None, ALU.mult))
            chain(v, v.tensor_scalar(M("t0"), M("vr"), float(HB), ROUND, ALU.mult, ALU.add))
            chain(v, v.tensor_scalar(M("t1"), M("t0"), ROUND, None, ALU.subtract))
            v_ang.done(v.scalar_tensor_tensor(M("v32"), M("vr"), float(HB), M("t1"), ALU.mult, ALU.subtract))
            v_ang.wait(v, 1)

        def phases(v, g):
            hs = slice(g * HGRP, (g + 1) * HGRP)
            for i, r in enumerate(("v32", "vr")):
                v_ph.done(v.tensor_tensor(ph[:, i, :].rearrange("p (h s) -> p h s", s=HB), along(M(r)[:, hs], HB),
                                          across(C("step"), HGRP), ALU.mult))
            v_ph.wait(v, 5 * g + 2)
            for i, part in enumerate((0, 0, 1)):
                v_ph.done(v.tensor_scalar(rn[:, i, :], ph[:, part, :], C("off")[:, i:i + 1], ROUND, ALU.add, ALU.add))
            v_ph.wait(v, 5 * g + 5)
            for i, part in enumerate((0, 0, 1)):
                v_round.done(v.scalar_tensor_tensor(rn[:, i, :], rn[:, i, :], ROUND, ph[:, part, :],
                                                    ALU.subtract, ALU.subtract))

        @on("vector")
        def _(v):
            ld_cst.wait(v, 0)
            phases(v, 0)
            a_set.wait(v, 6)
            v.scalar_tensor_tensor(M("tanh"), M("e1"), 1.0, M("tanh"), ALU.add, ALU.mult)
            v.scalar_tensor_tensor(M("cm1"), M("sh"), -2.0, M("sh"), ALU.mult, ALU.mult)
            v.scalar_tensor_tensor(M("t1"), M("sh"), 2.0, M("ch"), ALU.mult, ALU.mult)
            v.tensor_tensor(M("k"), M("ar"), M("ar"), ALU.mult)
            chain(v, v.tensor_tensor(M("t2"), AIM, AIM, ALU.mult))
            v.scalar_tensor_tensor(M("t0"), M("cm1"), 1.0, M("tanh"), ALU.add, ALU.mult)
            v.tensor_tensor(M("ni"), M("t1"), M("e1"), ALU.mult)
            chain(v, v.tensor_tensor(M("k"), M("k"), M("t2"), ALU.add))
            v.tensor_tensor(M("nr"), M("t0"), M("cm1"), ALU.add)
            chain(v, v.reciprocal(M("den"), M("k")))
            v.tensor_tensor(M("t0"), M("nr"), M("ar"), ALU.mult)
            v.tensor_tensor(M("t1"), M("ni"), AIM, ALU.mult)
            v.tensor_tensor(M("t2"), M("ni"), M("ar"), ALU.mult)
            chain(v, v.tensor_tensor(M("k"), M("nr"), AIM, ALU.mult))
            v.tensor_tensor(M("gr"), M("t0"), M("t1"), ALU.add)
            chain(v, v.tensor_tensor(M("gi"), M("t2"), M("k"), ALU.subtract))
            v.tensor_tensor(M("gr"), M("gr"), M("den"), ALU.mult)
            chain(v, v.tensor_tensor(M("gi"), M("gi"), M("den"), ALU.mult))
            v.scalar_tensor_tensor(M("t0"), M("gr"), 2.0, CRE, ALU.mult, ALU.mult)
            v.scalar_tensor_tensor(M("t1"), M("gi"), 2.0, CIM, ALU.mult, ALU.mult)
            v.scalar_tensor_tensor(M("t2"), M("gi"), 2.0, CRE, ALU.mult, ALU.mult)
            chain(v, v.scalar_tensor_tensor(M("k"), M("gr"), 2.0, CIM, ALU.mult, ALU.mult))
            v.tensor_tensor(M("cr"), M("t0"), M("t1"), ALU.subtract)
            chain(v, v.tensor_tensor(M("ci"), M("t2"), M("k"), ALU.add))

        def tables(v, g):
            hs = slice(g * HGRP, (g + 1) * HGRP)
            a_sin.wait(v, 3 * (g + 1))
            for i, c in enumerate(("cr", "ci")):
                w = rn[:, i, :].rearrange("p (h s) -> p h s", s=HB)
                chain(v, v.tensor_tensor(w, w, along(M(c)[:, hs], HB), ALU.mult))
            chain(v, v.tensor_tensor(rn[:, 0, :], rn[:, 0, :], rn[:, 1, :], ALU.subtract))
            a_mag.wait(v, 2 * (g + 1))
            pe_k.wait(v, g)
            v_tab.done(v.tensor_tensor(ltab, rn[:, 0, :], mg[:, 0, :], ALU.mult))
            v_tab.done(v.tensor_tensor(rtab, rn[:, 2, :], mg[:, 1, :], ALU.mult))

        def kernels_pe(pe, g):
            v_tab.wait(pe, 2 * (g + 1))
            v_ke.wait(pe, g - 1)
            for h in range(HGRP):
                cols = slice(h * HB, (h + 1) * HB)
                mm = pe.matmul(ps[0:HB, 4 + g % 2, cols], ltab[:, cols], rtab[:, cols], start=True, stop=True)
            pe_k.done(mm)

        def kernels_out(v, g):
            pe_k.wait(v, g + 1)
            if g >= 2:
                st_k.wait(v, g - 2)
            v_ke.done(v.tensor_copy(ksb[:, g % 2, :], ps[0:HB, 4 + g % 2, 0:GC]))
            v_ke.wait(v, g + 1)
            k0 = ksb[0:1, g % 2, :].rearrange("p (h s) -> p h s", s=HB)[:, :, 0]
            v_k.done(v.tensor_tensor(k0, k0, d_row[:, g * HGRP:(g + 1) * HGRP], ALU.add))

        def store_kernels(sp, g):
            v_k.wait(sp, g + 1)
            st_k.start(sp, g, kpad.ap()[g * HGRP:(g + 1) * HGRP, P - 1:P - 1 + L].rearrange("h (a b) -> a h b", b=HB),
                       ksb[:, g % 2, :].rearrange("a (h b) -> a h b", b=HB))

        def load_x_conv(sp, t):
            if t >= XR:
                pe_conv.wait(sp, (t - XR + 1) * XH)
            ld_xc.start(sp, t, xc[:, t % XR, :, :], x_conv[:, t * XH:(t + 1) * XH, :])

        @on("sync")
        def _(sp):
            for t in range(XR):
                load_x_conv(sp, t)
            sp.dma_start(wraw[:, 0:2, :].rearrange("p a n -> p (a n)"), w_v).then_inc(ld_w[0], 16)
            sp.dma_start(wraw[:, 2, :], w_qk[0]).then_inc(ld_w[2], 16)
            store_kernels(sp, 0)
            st_zero.wait(sp, 0)
            for h in range(S):
                g = h // HGRP
                if h % HGRP == 0:
                    st_k.wait(sp, g)
                if h % HGRP == 6 and g + 1 < NHG:
                    store_kernels(sp, g + 1)
                if h >= TR:
                    pe_conv.wait(sp, h - TR + 1)
                ld_toep.start(sp, h, toep[:, h % TR, :], bass.AP(kpad, h * (KROW + 1), [[1, P], [1, L]]))
                done = h - TR + 1
                if done > 0 and done % XH == 0 and done // XH + XR - 1 < S // XH:
                    load_x_conv(sp, done // XH + XR - 1)

        def convolve(pe, h):
            n, i = h // 2, h % 2
            if h % XH == 0:
                ld_xc.wait(pe, h // XH)
            if i == 0:
                v_mask.wait(pe, n - 3)
            ld_toep.wait(pe, h)
            for d in range(NJ):
                mm = pe.matmul(ps[:, n % 4, i * 256 + d * NB:(i + 1) * 256], toep[:, h % TR, d * P:(d + 1) * P],
                               xc[:, (h // XH) % XR, h % XH, 0:(NJ - d) * NB], start=(d == 0), stop=(d == NJ - 1))
            pe_conv.done(mm)

        @on("tensor")
        def _(pe):
            kernels_pe(pe, 0)
            for h in range(S):
                convolve(pe, h)
                if h % HGRP == 2 and h // HGRP + 1 < NHG:
                    kernels_pe(pe, h // HGRP + 1)

        @on("vector")
        def _(v):
            tables(v, 0)
            ld_d.wait(v, 0)
            kernels_out(v, 0)
            phases(v, 1)
            ld_len.wait(v, 0)
            v_len.done(v.tensor_copy(len_f[:], len_i[:]))
            v_len.wait(v, 1)
            v_valid.done(v.tensor_tensor(valid[:], across(len_f[:], NJ), along(C("pos"), NB), ALU.is_gt))
            v_valid.wait(v, 1)
            for n in range(S // 2):
                g, k = n // GP, n % GP
                if k == 0 and g + 1 < NHG:
                    tables(v, g + 1)
                if k == 1 and g + 1 < NHG:
                    kernels_out(v, g + 1)
                pe_conv.wait(v, 2 * n + 2)
                a_yhi.wait(v, n - 1)
                g_ylo.wait(v, n - 1)
                v_mask.done(v.tensor_tensor(ym[:, n % 2, :, :], bank(n % 4).rearrange("p (i c) -> p i c", i=2),
                                            across(valid[:].rearrange("p j b -> p (j b)"), 2), ALU.mult))
                if k == 2 and g + 2 < NHG:
                    phases(v, g + 2)

        def y_pair(part, n, i):
            return y[part][:, :, :, 2 * n + i]

        def ym_pair(n, i):
            return ym[:, n % 2, i, :].rearrange("p (j b) -> p j b", b=NB)

        @on("scalar")
        def _(act):
            weight_hi(act, -1)
            weight_hi(act, 0)
            magnitudes(act, 1)
            sines(act, 1)
            for n in range(S // 2):
                g = n // GP
                if n % GP == 3 and g + 2 < NHG:
                    magnitudes(act, g + 2)
                    sines(act, g + 2)
                v_mask.wait(act, n + 1)
                act.activation(y_pair(0, n, 0), ym_pair(n, 0), ACT.Copy)
                a_yhi.done(act.activation(y_pair(0, n, 1), ym_pair(n, 1), ACT.Copy))

        @on("gpsimd")
        def _(gp):
            weight_lo(gp, -1)
            weight_lo(gp, 0)
            exponents(gp, 1)
            for n in range(S // 2):
                g = n // GP
                if n % GP == 2 and g + 2 < NHG:
                    exponents(gp, g + 2)
                a_yhi.wait(gp, n + 1)
                gp.tensor_tensor(y_pair(1, n, 0), ym_pair(n, 0), y_pair(0, n, 0).bitcast(F32), ALU.subtract)
                g_ylo.done(gp.tensor_tensor(y_pair(1, n, 1), ym_pair(n, 1), y_pair(0, n, 1).bitcast(F32), ALU.subtract))

        NU = NG + NQT

        def w_slot(m):
            return slice(0, 2) if m < 0 else slice((m + 2) % WR, (m + 2) % WR + 1)

        def w_loaded(eng, m):
            s = w_slot(m).start
            eng.wait_ge(ld_w[s], 16 * (1 if m < 0 else (m - 1) // WR + 2 if s == 0 else m // WR + 1))

        def w_users(m):
            return 0 if m <= 0 else 1 if m < WR else m - WR + 2

        def load_weights(sp, m):
            a_whi.wait(sp, w_users(m))
            g_wlo.wait(sp, w_users(m))
            s = w_slot(m).start
            sp.dma_start(wraw[:, s, :], w_qk[m]).then_inc(ld_w[s], 16)

        def weight_hi(act, m):
            w_loaded(act, m)
            pe_unit.wait(act, w_users(m))
            a_whi.done(act.activation(wsp[0][:, w_slot(m), :], wraw[:, w_slot(m), :], ACT.Copy))

        def weight_lo(gp, m):
            a_whi.wait(gp, m + 2)
            g_wlo.done(gp.tensor_tensor(wsp[1][:, w_slot(m), :], wraw[:, w_slot(m), :],
                                        wsp[0][:, w_slot(m), :].bitcast(F32), ALU.subtract))

        NVB = TOK // P // 2

        @on("sync")
        def _(sp):
            load_weights(sp, 1)
            load_weights(sp, 2)
            for n in range(NVB):
                a_vhi.wait(sp, n + 1)
                v_vlo.wait(sp, n + 1)
                for part in range(2):
                    dst = v_dram[part][2 * n * P:(2 * n + 2) * P, :].rearrange("(t p) d -> p t d", p=P)
                    st_stg.start(sp, n, dst, stg[part][:, n % SR, :].rearrange("p (t d) -> p t d", t=2))
            for m in range(NU):
                if m + WR < NU:
                    load_weights(sp, m + WR)
                if m == NG + 1:
                    for n in range(NVB + 4 * NG, NVB + 4 * NG + SR):
                        st_stg.wait(sp, n)
                    load_kv(sp, 0)
                    load_kv(sp, 1)
                for g in range(4):
                    n = NVB + 4 * m + g
                    if m == NU - 1 and g == 3:
                        pe_unit.wait(sp, NU + 1)
                        load_q(sp, 1)
                        for t in range(WS3):
                            load_w3(sp, t)
                    a_rhi.wait(sp, 4 * m + g + 1)
                    v_rlo.wait(sp, 4 * m + g + 1)
                    for part in range(2):
                        src = stg[part][:, n % SR, :]
                        if m < NG:
                            st_stg.start(sp, n, k_dram[part][m, :, g * 512:(g + 1) * 512], src)
                        else:
                            st_stg.start(sp, n, q_dram[part][8 * g:8 * g + 8, :, m - NG, :].rearrange("b p s -> p b s"),
                                         src.rearrange("p (b s) -> p b s", s=S))
                    if m == NU - 1 and g == 0:
                        for last in range(n - SR + 1, n + 1):
                            st_stg.wait(sp, last)
                        a_whi.wait(sp, NU + 1)
                        g_wlo.wait(sp, NU + 1)
                        pe_unit.wait(sp, NU - 1)
                        load_q(sp, 0)
                        load_kv(sp, 2)
            load_q(sp, 2)
            ld_cond.start(sp, 0, cidx_i[:], cond.partition_broadcast(P))
            load_residual(sp, 0)
            load_residual(sp, 1)
            for t in range(WS3, NQT):
                load_w3(sp, t)
            for n in range(NVB + 4 * NU - SR, NVB + 4 * NU):
                st_stg.wait(sp, n)

        @on("tensor")
        def _(pe):
            yt = [p.rearrange("p j b s -> p j (b s)") for p in (y[0][:], y[1][:])]
            wv = [w[:, 0:2, :].rearrange("p a n -> p (a n)").rearrange("p (j d) -> p j d", j=NJ) for w in wsp]
            v_mask.wait(pe, S // 2)
            v_ke.wait(pe, NHG)
            a_yhi.wait(pe, S // 2)
            g_ylo.wait(pe, S // 2)
            a_whi.wait(pe, 1)
            g_wlo.wait(pe, 1)
            for n in range(NVB):
                for t in range(2):
                    tok = slice((2 * n + t) * P, (2 * n + t + 1) * P)
                    for j in range(NJ):
                        for a, b in PASSES:
                            mm = pe.matmul(ps[:, n, t * 256:(t + 1) * 256], yt[a][:, j, tok], wv[b][:, j, :],
                                           start=(j == 0 and a + b == 0), stop=(j == NJ - 1 and a == 1))
                pe_v.done(mm) if n < NVB - 1 else pe_unit.done(mm)
            for m in range(NU):
                a_whi.wait(pe, m + 2)
                g_wlo.wait(pe, m + 2)
                w = [x[:, w_slot(m).start, :].rearrange("p (j d) -> p j d", j=NJ) for x in wsp]
                for g in range(4):
                    if m < 2:
                        v_vlo.wait(pe, 4 * m + g + 1)
                    else:
                        v_rcos.wait(pe, 4 * (m - 2) + g + 1)
                    for j in range(NJ):
                        if (m, g, j) == (NU - 1, 3, NJ - 1):
                            scores(pe, 0)
                        for a, b in PASSES:
                            mm = pe.matmul(ps[:, 4 * (m % 2) + g, :], w[a][:, j, :], yt[b][:, j, g * 512:(g + 1) * 512],
                                           start=(j == 0 and a + b == 0), stop=(j == NJ - 1 and a == 1))
                    pe_m.done(mm) if g < 3 else pe_unit.done(mm)

        def v_ready(eng, n):
            if n < NVB - 1:
                pe_v.wait(eng, n + 1)
            else:
                pe_unit.wait(eng, 1)

        def m_ready(eng, m, g):
            if g < 3:
                pe_m.wait(eng, 3 * m + g + 1)
            else:
                pe_unit.wait(eng, m + 2)

        def staging_free(eng, n):
            if n >= SR:
                st_stg.wait(eng, n - SR)

        @on("scalar")
        def _(act):
            g_ylo.wait(act, S // 2)
            for n in range(NVB):
                v_ready(act, n)
                staging_free(act, n)
                a_vhi.done(act.activation(stg[0][:, n % SR, :], bank(n), ACT.Copy))
            for m in range(NU):
                if m < NU - 1:
                    weight_hi(act, m + 1)
                for g in range(4):
                    n = 4 * m + g
                    g_rsum.wait(act, n + 1)
                    staging_free(act, NVB + n)
                    a_rhi.done(act.activation(stg[0][:, (NVB + n) % SR, :], rf[:, n % RR, :], ACT.Copy))
                    if n == 4 * NU - 4:
                        place_k(act, 0)
                    if n == 4 * NU - 3:
                        place_v(act, 0)
                    if n == 4 * NU - 2:
                        exponentials(act, 0)

        @on("vector")
        def _(v):
            for n in range(NVB):
                a_vhi.wait(v, n + 1)
                v_vlo.done(v.tensor_tensor(stg[1][:, n % SR, :], bank(n), stg[0][:, n % SR, :].bitcast(F32),
                                           ALU.subtract))
            swap = [(i + HD // 2) % HD for i in range(HD)]

            def rope_lo(n):
                s = (NVB + n) % SR
                a_rhi.wait(v, n + 1)
                v_rlo.done(v.tensor_tensor(stg[1][:, s, :], rf[:, n % RR, :], stg[0][:, s, :].bitcast(F32), ALU.subtract))

            for n in range(4 * NU):
                m, g = n // 4, n % 4
                m_ready(v, m, g)
                g_rsum.wait(v, n + 1 - RR)
                acc = bank(4 * (m % 2) + g)
                v_rot.done(v.stream_shuffle(rot[:, n % RR, :], acc, swap))
                v_rcos.done(v.tensor_tensor(rc[:, n % RR, :].rearrange("p (b s) -> p b s", s=S),
                                            acc.rearrange("p (b s) -> p b s", s=S), across(C("cos"), 8), ALU.mult))
                if 1 <= n <= 4 * NU - 4:
                    rope_lo(n - 1)
                if 4 * NU - 4 <= n < 4 * NU - 1:
                    rope_lo(n)
                if n == 4 * NU - 4:
                    a_whi.wait(v, NU + 1)
                    g_wlo.wait(v, NU + 1)
                    pe_unit.wait(v, NU - 1)
                    v_zero3.done(v.memset(k_bd[0][:].bitcast(F32), 0.0))
                if n == 4 * NU - 2:
                    scale_and_max(v, 0)
            sums(v, 0)
            scale_and_max(v, 1)
            rope_lo(4 * NU - 1)

        @on("gpsimd")
        def _(gp):
            for m in range(NU):
                if m < NU - 1:
                    weight_lo(gp, m + 1)
                for g in range(4):
                    n = 4 * m + g
                    v_rot.wait(gp, n + 1)
                    r = rot[:, n % RR, :].rearrange("p (b s) -> p b s", s=S)
                    g_rsin.done(gp.tensor_tensor(r, r, across(C("sin"), 8), ALU.mult))
                    g_rsin.wait(gp, n + 1)
                    v_rcos.wait(gp, n + 1)
                    v_rlo.wait(gp, n + 1 - RR)
                    g_rsum.done(gp.tensor_tensor(rf[:, n % RR, :], rot[:, n % RR, :], rc[:, n % RR, :], ALU.add))
                    if n == 4 * NU - 4:
                        pe_unit.wait(gp, NU)
                        zero_3(gp, v_bd[0])
                    if n == 4 * NU - 2:
                        subtract_max(gp, 0)
            normalise(gp, 0)
            subtract_max(gp, 1)
            pe_unit.wait(gp, NU + 1)
            zero_3(gp, k_bd[1])
            g_rsum.wait(gp, 4 * NU)
            zero_3(gp, v_bd[1])

        NUNIT = 2 * NPAIR
        HALF_SLOTS = range(NUNIT + 2)
        INV_SQRT = 1.0 / float(np.sqrt(HD))
        W4_TILES = {NUNIT: (0, 1, 2), NUNIT + 1: (3, 4, 5)}
        WO_TILES = {0: (0, 1, 2, 3), 1: (4, 5, 6, 7)}

        def wo_split(eng, t):
            a_w3.wait(eng, t + 1)
            v_w3.wait(eng, t // 2 + 1)
            g_w3.wait(eng, (t + 1) // 2)

        def wo_lo(eng, t):
            a_w3.wait(eng, t + 1)
            ins = eng.tensor_tensor(wo[1][:, t, :], wstage3[:, t % WS3, :], wo[0][:, t, :].bitcast(F32), ALU.subtract)
            (g_w3 if t % 2 else v_w3).done(ins)


        def load_kv(sp, i):
            a_kbd.wait(sp, 8 * (i - 1))
            a_vbd.wait(sp, 4 * (i - 1))
            for part in range(2):
                ld_k.start(sp, i, kc[:, i % 2, part, :, :],
                           k_dram[part][:, :, i * P:(i + 1) * P].rearrange("t p k -> p t k"))
            for part in range(2):
                for x in range(2):
                    ld_v.start(sp, i, vc[x * S:(x + 1) * S, i % 2, part, :, :],
                               v_dram[part][i * P:(i + 1) * P, :].rearrange("(b k) c -> k b c", b=2))

        def load_q(sp, i):
            pe_s.wait(sp, 2 * (i - 2) + 2)
            for part in range(2):
                ld_q.start(sp, i, q_sb[i % 2][:, part, :, :, :], q_dram[part][2 * i:2 * i + 2].rearrange("b p t s -> p b t s"))

        def load_w3(sp, t):
            if t >= WS3:
                wo_split(sp, t - WS3)
            ld_w3.start(sp, t, wstage3[:, t % WS3, :], w_o[:, t, :])

        def zero_3(gp, tensor):
            g_zero3.done(gp.memset(tensor[:].bitcast(F32), 0.0))

        def place_k(act, i):
            v_zero3.wait(act, 1) if i == 0 else g_zero3.wait(act, 2)
            ld_k.wait(act, i)
            if i >= 2:
                pe_s.wait(act, 2 * (i - 2) + 2)
            for part in range(2):
                for g in range(4):
                    rows = slice(g * HD, (g + 1) * HD)
                    a_kbd.done(act.activation(k_bd[i % 2][rows, part, :, :, g * S:(g + 1) * S].rearrange("p b t k -> p t b k"),
                                              kc[rows, i % 2, part, :, :].rearrange("p t (b k) -> p t b k", b=2), ACT.Copy))

        def place_v(act, i):
            g_zero3.wait(act, 1 if i == 0 else 3)
            ld_v.wait(act, i)
            if i >= 2:
                pe_o.wait(act, 2 * (i - 2) + 2)
            for part in range(2):
                for x in range(2):
                    rows = slice(x * S, (x + 1) * S)
                    slot = v_bd[i % 2][rows, part, :, :, :, :].rearrange("p b t m c -> p (b t) (m c)")
                    dst = bass.AP(slot.tensor, slot.offset + x * HD, [list(slot.ap[0]), [2 * P, 2 * NG], [P + 64, 2], [1, HD]])
                    src = vc[rows, i % 2, part, :, :].rearrange("p b (t m c) -> p (b t) m c", t=NG, m=2)
                    a_vbd.done(act.activation(dst, src[:, :, :, x * HD:(x + 1) * HD], ACT.Copy))

        def store_x1(sp, i):
            v_x1.wait(sp, 2 * i + 2)
            st_x1.start(sp, i, x1_dram[i * P:(i + 1) * P, :], xr[:, i % 3, :])

        def load_residual(sp, i):
            if i >= 3:
                st_x1.wait(sp, i - 3)
            ld_x.start(sp, i, xr[:, i % 3, :], x_nat[i * P:(i + 1) * P, :])

        @on("sync")
        def _(sp):
            for i in range(NPAIR):
                if 1 <= i < NPAIR - 2:
                    load_q(sp, i + 2)
                if i + 3 < NPAIR:
                    load_kv(sp, i + 3)
                if i >= 1:
                    if i == NPAIR - 1:
                        for t in range(WS4):
                            load_w4(sp, t)
                        pe_s.wait(sp, NUNIT)
                        load_x1(sp, 0)
                        load_x1(sp, 1)
                    store_x1(sp, i - 1)
                    if i + 1 < NPAIR:
                        load_residual(sp, i + 1)
            for t in range(WS4, WB_EARLY):
                load_w4(sp, t)
            store_x1(sp, NPAIR - 1)

        def scores(pe, u):
            i, b = u // 2, u % 2
            ld_q.wait(pe, i)
            a_kbd.wait(pe, 8 * (i + 1))
            v_sc.wait(pe, u)
            v_rcos.wait(pe, 4 * (NU - 1))
            for G in range(NG):
                for rp in range(2):
                    for a, c in PASSES:
                        mm = pe.matmul(ps[:, G, rp * 256:(rp + 1) * 256],
                                       q_sb[i % 2][:, a, b, G * REP + 2 * rp:G * REP + 2 * rp + 2, :],
                                       k_bd[i % 2][:, c, b, G, :], start=(a + c == 0), stop=(a == 1))
            pe_s.done(mm)

        def turn_probs(pe, u):
            g_prob.wait(pe, u + 1)
            v_ptlo.wait(pe, u)
            for G in range(NG):
                for rp in range(2):
                    for pair in range(2):
                        at = G * 512 + rp * 256 + pair * P
                        mm = pe.transpose(ps[:, 2 + G, pair * 256 + rp * P:pair * 256 + (rp + 1) * P],
                                          sc[:, u % 2, at:at + P], C("ident"))
            pe_t.done(mm)

        def values(pe, u):
            i, b = u // 2, u % 2
            a_vbd.wait(pe, 4 * (i + 1))
            a_pthi.wait(pe, u + 1)
            v_ptlo.wait(pe, u + 1)
            v_otlo.wait(pe, u - 1)
            for G in range(NG):
                for pair in range(2):
                    for a, c in PASSES:
                        at = G * 512 + pair * 256
                        mm = pe.matmul(ps[:, 4 + u % 2, G * 256:(G + 1) * 256], v_bd[i % 2][:, c, b, G, pair, :],
                                       pt[a][:, at:at + 256], start=(pair == 0 and a + c == 0),
                                       stop=(pair == 1 and a == 1))
            pe_o.done(mm)

        def project(pe, i, quarter):
            n, tiles = quarter // 2, range(quarter % 2 * 4, quarter % 2 * 4 + 4)
            if quarter == 0:
                a_othi.wait(pe, 2 * i + 2)
                v_otlo.wait(pe, 2 * i + 2)
            if quarter % 2 == 0:
                v_x1.wait(pe, 2 * (i - 1) + n + 1)
            for t in tiles:
                wo_split(pe, t)
                for a, c in PASSES:
                    mm = pe.matmul(ps[:, 6 + n, :], ot[a][:, i % 2, t, :, :], wo[c][:, t, n * 512:(n + 1) * 512],
                                   start=(t == 0 and a + c == 0), stop=(t == NQT - 1 and a == 1))
            pe_y.done(mm)

        @on("tensor")
        def _(pe):
            scores(pe, 1)
            v_rcos.wait(pe, 4 * NU)
            for w in HALF_SLOTS:
                i, k = w // 2 - 1, w % 2
                if 0 <= w < NUNIT:
                    turn_probs(pe, w)
                if w == NUNIT + 1:
                    mix_channels(pe, 0)
                if i >= 0:
                    project(pe, i, 2 * k)
                for part in (values, scores) if w < 2 else (scores, values):
                    u = w if part is values else w + 2
                    if u < NUNIT:
                        part(pe, u)
                if i >= 0:
                    project(pe, i, 2 * k + 1)

        def sc_groups(u):
            return sc[:, u % 2, :].rearrange("p (g k) -> p g k", k=S)

        def scale_and_max(v, u):
            pe_s.wait(v, u + 1)
            pe_t.wait(v, u - 1)
            v_sc.done(v.scalar_tensor_tensor(sc_groups(u), ps[:, 0:2, :].rearrange("p a (g k) -> p (a g) k", k=S),
                                             INV_SQRT, across(C("causal"), 16), ALU.mult, ALU.add))
            v_sc.wait(v, u + 1)
            v_max.done(v.tensor_reduce(stat[:, u % 2, 0, :], sc_groups(u), AX_X, ALU.max))

        def subtract_max(gp, u):
            v_max.wait(gp, u + 1)
            g_sub.done(gp.tensor_tensor(sc_groups(u), sc_groups(u), along(stat[:, u % 2, 0, :], S), ALU.subtract))

        def exponentials(act, u):
            g_sub.wait(act, u + 1)
            a_exp.done(act.activation(sc[:, u % 2, :], sc[:, u % 2, :], ACT.Exp))

        def sums(v, u):
            a_exp.wait(v, u + 1)
            v_sum.done(v.tensor_reduce(stat[:, u % 2, 1, :], sc_groups(u), AX_X, ALU.add))
            v_sum.wait(v, u + 1)
            v_rec.done(v.reciprocal(stat[:, u % 2, 2, :], stat[:, u % 2, 1, :]))

        def normalise(gp, u):
            v_rec.wait(gp, u + 1)
            g_prob.done(gp.tensor_tensor(sc_groups(u), sc_groups(u), along(stat[:, u % 2, 2, :], S), ALU.mult))

        @on("vector")
        def _(v):
            for w in HALF_SLOTS:
                if w == 1:
                    ld_cond.wait(v, 0)
                    for b in range(2):
                        r = slice(b * S, (b + 1) * S)
                        v_cidx.done(v.tensor_scalar(cidx[r, :], cidx_i[r, b::2], float(S), C("chan")[r, :],
                                                    ALU.mult, ALU.add))
                if 0 <= w < NUNIT:
                    a_pthi.wait(v, w + 1)
                    v_ptlo.done(v.tensor_tensor(pt[1][:], ps[:, 2:4, :].rearrange("p a c -> p (a c)"),
                                                pt[0][:].bitcast(F32), ALU.subtract))
                if w >= 3:
                    i, n = (w - 1) // 2 - 1, (w - 1) % 2
                    pe_y.wait(v, 4 * i + 2 * n + 2)
                    ld_x.wait(v, i)
                    x = xr[:, i % 3, n * 512:(n + 1) * 512]
                    v_x1.done(v.tensor_tensor(x, bank(6 + n), x, ALU.add))
                for t in W4_TILES.get(w, ()):
                    w4_lo(v, t)
                if w == NUNIT + 1:
                    xf_lo(v, 0)
                if w + 1 < NUNIT:
                    sums(v, w + 1)
                if w < NUNIT:
                    a_othi.wait(v, w + 1)
                    v_otlo.done(v.tensor_tensor(ot[1][:, (w // 2) % 2, :, w % 2, :],
                                                bank(4 + w % 2).rearrange("p (t q) -> p t q", q=S),
                                                ot[0][:, (w // 2) % 2, :, w % 2, :].bitcast(F32), ALU.subtract))
                if w + 2 < NUNIT:
                    scale_and_max(v, w + 2)
                for t in WO_TILES.get(w, ())[::2]:
                    wo_lo(v, t)
            i = NPAIR - 1
            pe_y.wait(v, 4 * i + 4)
            x = xr[:, i % 3, 512:]
            v_x1.done(v.tensor_tensor(x, bank(7), x, ALU.add))

        @on("gpsimd")
        def _(gp):
            for u in range(1, NUNIT):
                if u > 1:
                    subtract_max(gp, u)
                if u - 2 in WO_TILES:
                    wo_lo(gp, WO_TILES[u - 2][3])
                if u == 6:
                    zero_3(gp, mix)
                if 8 <= u < 8 + NPAIR:
                    v_cidx.wait(gp, 2)
                    i = u - 8
                    gp.indirect_dma_start(craw[:, i, :], None, w_cond.rearrange("n c d -> (n c) d"),
                                          bass.IndirectOffsetOnAxis(ap=cidx[:, i:i + 1], axis=0))\
                      .then_inc(ld_cmix.sems[0], 16)
                normalise(gp, u)
                if u - 1 in WO_TILES:
                    wo_lo(gp, WO_TILES[u - 1][1])

        @on("scalar")
        def _(act):
            for w in HALF_SLOTS:
                if w == 0:
                    v_rlo.wait(act, 4 * NU)
                if 0 <= w < NUNIT:
                    pe_t.wait(act, w + 1)
                    pe_o.wait(act, w)
                    a_pthi.done(act.activation(pt[0][:], ps[:, 2:4, :].rearrange("p a c -> p (a c)"), ACT.Copy))
                if w + 1 < NUNIT:
                    exponentials(act, w + 1)
                if w == 0:
                    place_k(act, 1)
                for t in W4_TILES.get(w, ()):
                    w4_hi(act, t)
                if w == NUNIT:
                    xf_hi(act, 0)
                if w == 8 + NPAIR:
                    ld_cmix.wait(act, 0)
                    g_zero3.wait(act, 4)
                    for b in range(2):
                        r = slice(b * S, (b + 1) * S)
                        a_mix.done(act.activation(mix[r, :, b * S:(b + 1) * S], craw[r, :, :], ACT.Copy))
                if 0 <= w < NUNIT:
                    i = w // 2
                    pe_o.wait(act, w + 1)
                    pe_y.wait(act, 4 * (i - 1))
                    a_othi.done(act.activation(ot[0][:, i % 2, :, w % 2, :],
                                               bank(4 + w % 2).rearrange("p (t q) -> p t q", q=S), ACT.Copy))
                for t in WO_TILES.get(w, ()):
                    ld_w3.wait(act, t)
                    a_w3.done(act.activation(wo[0][:, t, :], wstage3[:, t % WS3, :], ACT.Copy))
                if w % 2 == 0 and (w + 2) // 2 < NPAIR:
                    place_v(act, (w + 2) // 2)
                if w % 2 == 1 and (w + 3) // 2 < NPAIR:
                    place_k(act, (w + 3) // 2)

        def load_x1(sp, i):
            if i >= 4:
                st_out.wait(sp, i - 4)
            if i >= NPAIR - 3:
                st_x1.wait(sp, i)
            ld_x1.start(sp, i, x1[i % 4][:], x1_dram[i * P:(i + 1) * P, :])

        def load_w4(sp, t):
            if t < WS4:
                wo_split(sp, NQT - 1)
            a_w4.wait(sp, t - WS4 + 1)
            v_w4.wait(sp, t - WS4 + 1)
            ld_w4.start(sp, t, wstage4[:, t % WS4, :], w_ffn[:, t, :])

        @on("sync")
        def _(sp):
            for t in range(WB_EARLY, WB_EARLY + 1):
                load_w4(sp, t)
            pe_y.wait(sp, 4 * NPAIR)
            ld_p4.start(sp, 0, bexp_raw[:], w_b)
            for t in range(WB_EARLY + 1, NJ):
                load_w4(sp, t)
            for i in range(NPAIR + 1):
                if i + 2 < NPAIR:
                    load_x1(sp, i + 2)
                if i >= 1:
                    v_out.wait(sp, 3 * i)
                    st_out.start(sp, i - 1, out[(i - 1) * P:i * P, :], x1[(i - 1) % 4][:])
            for i in range(NPAIR - 4, NPAIR):
                st_out.wait(sp, i)

        def mix_channels(pe, i):
            ld_x1.wait(pe, i)
            a_mix.wait(pe, 2)
            v_sc.wait(pe, NUNIT)
            for half in range(2):
                v_xflo.wait(pe, 2 * (i - 1) + half + 1)
                if half == 1:
                    a_hthi.wait(pe, i - 1)
                    v_htlo.wait(pe, i - 1)
                for t in range(4):
                    at = (half * 4 + t) * P
                    mm = pe.matmul(ps[:, half, t * P:(t + 1) * P], x1[i % 4][:, at:at + P], mix[:, i, :],
                                   start=True, stop=True)
                pe_mix.done(mm)

        def joint_bank(i, piece):
            return ps[:, 2 + 3 * (i % 2) + piece, :]

        def own_experts(i):
            lo, hi = JOINT[0]
            return joint_bank(i, 0)[:, hi:hi + hi - NPROJ]

        def joint(pe, i, half):
            a_xfhi.wait(pe, 2 * i + half + 1)
            v_xflo.wait(pe, 2 * i + half + 1)
            if half == 0:
                v_out.wait(pe, 3 * (i - 1))
                if i == 1:
                    v_x1.wait(pe, 2 * NPAIR)
            for t in range(half * 4, half * 4 + 4):
                a_w4.wait(pe, t + 1)
                v_w4.wait(pe, t + 1)
                for a, c in PASSES:
                    for piece, (lo, hi) in enumerate(JOINT):
                        mm = pe.matmul(joint_bank(i, piece)[:, 0:hi - lo], xf[i % 2][:, a, t, :], wb[t][:, c, lo:hi],
                                       start=(t == 0 and a + c == 0), stop=(piece == 0 and t == NJ - 1 and a == 1))
            if half == 1:
                pe_f.done(mm)

        turned_h = ps[0:NE * RANK, 1, 0:P]

        def turn_h(pe, i):
            v_h.wait(pe, i + 1)
            v_xflo.wait(pe, min(2 * (i + 2), 2 * NPAIR))
            v_htlo.wait(pe, i)
            pe_ht.done(pe.transpose(turned_h, hw[:], C("ident")))

        def experts(pe, i):
            a_hthi.wait(pe, i + 1)
            v_htlo.wait(pe, i + 1)
            for piece, (lo, hi) in enumerate(JOINT):
                col = slice(max(lo - NPROJ, 0), hi - NPROJ)
                dst = joint_bank(i, piece)[:, 0:hi - lo] if piece else own_experts(i)
                for a, c in PASSES:
                    mm = pe.matmul(dst, ht[a][:], bexp[c][:, col], start=(piece == 0 and a + c == 0), stop=(a == 1))
                pe_out.done(mm)

        @on("tensor")
        def _(pe):
            for i in range(NPAIR + 1):
                if i < NPAIR:
                    joint(pe, i, 0)
                if i >= 1:
                    turn_h(pe, i - 1)
                if i + 1 < NPAIR:
                    mix_channels(pe, i + 1)
                if i >= 1:
                    a_p4.wait(pe, 1)
                    g_p4.wait(pe, 1)
                    experts(pe, i - 1)
                if i < NPAIR:
                    joint(pe, i, 1)

        def xf_hi(act, i):
            pe_f.wait(act, i - 1)
            for half in range(2):
                pe_mix.wait(act, 2 * i + half + 1)
                a_xfhi.done(act.activation(xf[i % 2][:, 0, half * 4:half * 4 + 4, :],
                                           bank(half).rearrange("p (t q) -> p t q", q=P), ACT.Copy))

        def w4_hi(act, t):
            ld_w4.wait(act, t)
            a_w4.done(act.activation(wb[t][:, 0, :], wstage4[:, t % WS4, :], ACT.Copy))

        def w4_lo(v, t):
            a_w4.wait(v, t + 1)
            v_w4.done(v.tensor_tensor(wb[t][:, 1, :], wstage4[:, t % WS4, :], wb[t][:, 0, :].bitcast(F32),
                                      ALU.subtract))

        @on("scalar")
        def _(act):
            pe_y.wait(act, 4 * NPAIR)
            for t in range(WB_EARLY, NJ):
                w4_hi(act, t)
            ld_p4.wait(act, 0)
            a_p4.done(act.activation(bexp[0][:], bexp_raw[:], ACT.Copy))
            for i in range(NPAIR + 1):
                if i >= 1:
                    v_gate.wait(act, GATE_STEPS * (i - 1) + 2)
                    a_gate.done(act.activation(gt[:, 0, :], joint_bank(i - 1, 0)[:, 0:NE], ACT.Exp, bias=gs[:, 1:2],
                                               accum_out=gs[:, 2:3]))
                    pe_ht.wait(act, i)
                    pe_out.wait(act, 3 * (i - 1))
                    a_hthi.done(act.activation(ht[0][:], turned_h, ACT.Copy))
                if i + 1 < NPAIR:
                    xf_hi(act, i + 1)

        @on("gpsimd")
        def _(gp):
            a_p4.wait(gp, 1)
            g_p4.done(gp.tensor_tensor(bexp[1][:], bexp_raw[:], bexp[0][:].bitcast(F32), ALU.subtract))

        GATE_STEPS = 11

        def gate(v, i):
            n0 = GATE_STEPS * i

            def link(k, ins):
                v_gate.done(ins)
                v_gate.wait(v, n0 + k)

            logits = joint_bank(i, 0)[:, 0:NE]
            pe_f.wait(v, i + 1)
            x = x1[i % 4][:, 0:JOINT[0][1] - NPROJ]
            v_base.done(v.tensor_tensor(x, joint_bank(i, 0)[:, NPROJ:JOINT[0][1]], x, ALU.add))
            link(1, v.tensor_reduce(gs[:, 0:1], logits, AX_X, ALU.max))
            link(2, v.tensor_scalar(gs[:, 1:2], gs[:, 0:1], -1.0, None, ALU.mult))
            a_gate.wait(v, i + 1)
            link(3, v.reciprocal(gs[:, 3:4], gs[:, 2:3]))
            link(4, v.tensor_scalar(gt[:, 1, :], gt[:, 0, :], gs[:, 3:4], None, ALU.mult))
            link(5, v.max(gt[:, 2, :], gt[:, 1, :]))
            link(6, v.max_index(gi[:], gt[:, 2, :], gt[:, 1, :]))
            link(7, v.tensor_copy(gt[:, 3, :], gi[:]))
            link(8, v.tensor_tensor(gs[:, 4:5], gt[:, 2, 0:1], gt[:, 2, 1:2], ALU.add))
            v.reciprocal(gs[:, 5:6], gs[:, 4:5]).then_inc(v_gate.sem, 1)
            for k in range(2):
                ins = v.tensor_scalar(gt[:, 4 + k, :], C("iota8"), gt[:, 3, k:k + 1], gt[:, 2, k:k + 1],
                                      ALU.is_equal, ALU.mult)
            v_gate.done(ins)
            v_gate.wait(v, n0 + 10)
            link(11, v.tensor_tensor(gt[:, 6, :], gt[:, 4, :], gt[:, 5, :], ALU.add))
            v_wts.done(v.tensor_scalar(gt[:, 7, :], gt[:, 6, :], gs[:, 5:6], SCALING, ALU.mult, ALU.mult))
            v_wts.wait(v, i + 1)
            pe_ht.wait(v, i)
            v_h.done(v.tensor_tensor(hw[:].rearrange("p (e r) -> p e r", r=RANK),
                                     joint_bank(i, 0)[:, NE:NPROJ].rearrange("p (e r) -> p e r", r=RANK),
                                     along(gt[:, 7, :], RANK), ALU.mult))

        v_wts, v_base = step("v_wts"), step("v_base")

        def xf_lo(v, i):
            for half in range(2):
                a_xfhi.wait(v, 2 * i + half + 1)
                dst, hi = (xf[i % 2][:, part, half * 4:half * 4 + 4, :] for part in (1, 0))
                v_xflo.done(v.tensor_tensor(dst, bank(half).rearrange("p (t q) -> p t q", q=P), hi.bitcast(F32),
                                            ALU.subtract))

        @on("vector")
        def _(v):
            for t in range(WB_EARLY, NJ):
                w4_lo(v, t)
            for i in range(NPAIR + 1):
                if i >= 1:
                    gate(v, i - 1)
                    a_hthi.wait(v, i)
                    v_htlo.done(v.tensor_tensor(ht[1][:], turned_h, ht[0][:].bitcast(F32), ALU.subtract))
                if i + 1 < NPAIR:
                    xf_lo(v, i + 1)
                if i >= 1:
                    v_base.wait(v, i)
                    for piece, (lo, hi) in enumerate(JOINT):
                        pe_out.wait(v, 3 * (i - 1) + piece + 1)
                        x = x1[(i - 1) % 4][:, max(lo - NPROJ, 0):hi - NPROJ]
                        total = joint_bank(i - 1, piece)[:, 0:hi - lo] if piece else own_experts(i - 1)
                        v_out.done(v.tensor_tensor(x, total, x, ALU.add))

        block = ctx.enter_context(nc.Block())
        for name, register in (("sync", block.sync), ("gpsimd", block.gpsimd), ("scalar", block.scalar),
                               ("vector", block.vector), ("tensor", block.tensor)):
            @register
            def _(eng, queue=queues[name]):
                for part in queue:
                    part(eng)


def _layouts(i):
    def head_rows(w, heads):
        return w.reshape(-1, HD, L)[heads].reshape(-1, L)

    def feature_major(w):
        return w.reshape(-1, NJ, P).transpose(2, 1, 0)

    x = i["x"]
    q_heads = np.array([(4 * G + g) * REP + r for G in range(NG) for r in range(REP) for g in range(4)])
    wqk = np.concatenate([i["L0_attn_Wk"], head_rows(i["L0_attn_Wq"], q_heads)])
    wo = i["L0_attn_Wo"].reshape(L, -1, HD)[:, q_heads].reshape(L, NQT, P)
    ffn = np.concatenate([i["L0_ffn_gate_W"], i["L0_ffn_A"].reshape(NE * RANK, L), i["L0_ffn_W_base"]])
    return [
        x.reshape(NB, S, NJ, P)[..., ::-1].transpose(3, 1, 2, 0).reshape(P, S, NJ * NB),
        x.reshape(TOK, L),
        i["itok_B_8_3872"], i["itok_B_0_15"],
        np.stack([np.broadcast_to(i["L0_cond_log_dt"][:, None], (S, NMODE)), i["L0_cond_log_A_real"],
                  i["L0_cond_A_imag"], i["L0_cond_C"][..., 0], i["L0_cond_C"][..., 1]]).transpose(2, 0, 1),
        i["L0_cond_D"],
        wqk.reshape(NG + NQT, P, NJ, P).transpose(0, 3, 2, 1).reshape(NG + NQT, P, NJ * P),
        feature_major(i["L0_attn_Wv"]).reshape(P, -1),
        wo.transpose(2, 1, 0),
        i["L0_cond2_weights"],
        feature_major(ffn),
        i["L0_ffn_B"].transpose(0, 2, 1).reshape(NE * RANK, L),
        constants(),
    ]


def kernel(**inputs):
    import concourse.bacc as bacc
    from concourse.bass_utils import run_bass_kernel_spmd

    nc = bacc.Bacc("TRN2", target_bir_lowering=False, num_devices=1)
    arrays, args = {}, []
    for n, a in enumerate(_layouts({k: np.asarray(v) for k, v in inputs.items()})):
        a = np.ascontiguousarray(a)
        arrays[f"in_{n}_dram"] = a
        args.append(nc.dram_tensor(f"in_{n}_dram", a.shape, mybir.dt.from_np(a.dtype), kind="ExternalInput").ap())
    out = nc.dram_tensor("out_dram", (TOK, L), F32, kind="ExternalOutput").ap()
    build(nc, *args, out)
    r = run_bass_kernel_spmd(nc, [arrays], core_ids=[0])
    return r.results[0]["out_dram"].reshape(NB, S, L)
```
